# Optimizing a Trainium2 kernel written in Bass

```python
import numpy as np
import jax
import jax.numpy as jnp

def _softmax(x, axis=-1):
    return jax.nn.softmax(x, axis=axis)

def _gelu(x):
    return jax.nn.gelu(x, approximate=True)

def _silu(x):
    return jax.nn.silu(x)

def _sigmoid(x):
    return jax.nn.sigmoid(x)

def _layernorm(x, axis=-1, eps=1e-05):
    m = jnp.mean(x, axis=axis, keepdims=True)
    v = jnp.var(x, axis=axis, keepdims=True)
    return (x - m) / jnp.sqrt(v + eps)

def _scatter_add(tgt, idx, src, axis=0):
    return tgt.at[idx].add(src)

def _segment_sum(src, seg, n):
    return jax.ops.segment_sum(src, seg, n)
kernel_name = 'mk_xattn_ffn_d1_seqx_r4_dc9e82'

def setup_inputs(seed: int=0):
    np.random.seed(seed)
    _w = jnp.asarray

    def _rec_inputs():
        import jax
        import jax.numpy as jnp
        _rk = jax.random.key(seed)
        x = -0.0002928 + 1 * jax.random.normal(jax.random.fold_in(_rk, 1), (16, 128, 512), jnp.float32)
        _lenS = 128 - jax.random.randint(jax.random.fold_in(_rk, 7), (16,), 0, max(1, 128 // 4) + 1, jnp.int32)
        _lenS2 = 128 - jax.random.randint(jax.random.fold_in(_rk, 8), (16,), 0, max(1, 128 // 4) + 1, jnp.int32)
        _ctx_2048P = jax.random.normal(jax.random.fold_in(_rk, 11), (16, 16, 512), jnp.float32)
        _ctx_2048c = jax.random.dirichlet(jax.random.fold_in(_rk, 511), 0.3 * jnp.ones((16,), jnp.float32), (16, 128))
        _ctx_2048t = jnp.einsum('bsk,bkd->bsd', _ctx_2048c, _ctx_2048P)
        _ctx_2048t = _ctx_2048t * jax.lax.rsqrt(jnp.mean(jnp.square(_ctx_2048t)) + 1e-12) * 0.953939
        ctx_2048 = 4.13588e-05 + 0.999923 * (_ctx_2048t + 0.3 * jax.random.normal(jax.random.fold_in(_rk, 611), (16, 128, 512), jnp.float32))
        _validS = jnp.arange(128)[None, :] < _lenS[:, None]
        _validS2 = jnp.arange(128)[None, :] < _lenS2[:, None]
        _causal = jnp.tril(jnp.ones((128, 128), dtype=bool))
        mask_1xSxS2_ff0 = jnp.where(jnp.ones((1, 128, 128), dtype=bool), 0.0, -1000000000.0).astype(jnp.float32)
        return (x, ctx_2048, mask_1xSxS2_ff0)
    x, ctx_2048, mask_1xSxS2_ff0 = _rec_inputs()

    def _L0_xattn_setup():
        import jax, jax.numpy as jnp
        import numpy as np
        H = 512
        NH = 16
        NKV = 4
        HD = 128
        GROUPS = NH // NKV
        EPS = 1e-06
        B, S, SE = (1, 512, 1024)

        def _rmsnorm(x, w, eps=EPS):
            xf = x.astype(jnp.float32)
            var = jnp.mean(xf * xf, axis=-1, keepdims=True)
            return (xf * jax.lax.rsqrt(var + eps)).astype(x.dtype) * w
        key = jax.random.key(seed)
        ks = jax.random.split(key, 12)
        sc = 0.02
        return {'hidden_states': jax.random.normal(ks[0], (B, S, H), jnp.float32), 'encoder_hidden_states': jax.random.normal(ks[1], (B, SE, H), jnp.float32), 'attention_mask': jnp.zeros((B, S, SE), jnp.float32), 'Wq': jax.random.normal(ks[2], (H, NH * HD), jnp.float32) * sc, 'bq': jax.random.normal(ks[3], (NH * HD,), jnp.float32) * sc, 'Wk': jax.random.normal(ks[4], (H, NKV * HD), jnp.float32) * sc, 'bk': jax.random.normal(ks[5], (NKV * HD,), jnp.float32) * sc, 'Wv': jax.random.normal(ks[6], (H, NKV * HD), jnp.float32) * sc, 'bv': jax.random.normal(ks[7], (NKV * HD,), jnp.float32) * sc, 'Wo': jax.random.normal(ks[8], (NH * HD, H), jnp.float32) * sc, 'qn_w': jnp.ones((HD,), jnp.float32), 'kn_w': jnp.ones((HD,), jnp.float32)}
    _L0_xattn_all = _L0_xattn_setup()
    _L0_xattn_in = {k: v for k, v in _L0_xattn_all.items() if k in ('Wq', 'bq', 'Wk', 'bk', 'Wv', 'bv', 'Wo', 'qn_w', 'kn_w')}
    del _L0_xattn_all

    def _L0_ffn_setup():
        import jax, jax.numpy as jnp
        import numpy as np
        CAPACITY = 0.125
        HEAD_DIM = 128
        N_HEADS = 16
        N_KV_HEADS = 8
        ROPE_THETA = 10000.0
        EPS = 1e-06

        def _rms_norm(x, w):
            return x * jax.lax.rsqrt(jnp.mean(x * x, axis=-1, keepdims=True) + EPS) * w

        def _rotate_half(t):
            h = t.shape[-1] // 2
            return jnp.concatenate([-t[..., h:], t[..., :h]], axis=-1)
        key = jax.random.key(seed)
        ks = jax.random.split(key, 12)
        B, T, D = (4, 1024, 512)
        I = 2048
        s = 0.02
        return {'hidden_states': jax.random.normal(ks[0], (B, T, D), jnp.float32), 'w_router': jax.random.normal(ks[1], (D,), jnp.float32) * s, 'wq': jax.random.normal(ks[2], (D, N_HEADS * HEAD_DIM), jnp.float32) * s, 'bq': jnp.zeros((N_HEADS * HEAD_DIM,), jnp.float32), 'wk': jax.random.normal(ks[3], (D, N_KV_HEADS * HEAD_DIM), jnp.float32) * s, 'bk': jnp.zeros((N_KV_HEADS * HEAD_DIM,), jnp.float32), 'wv': jax.random.normal(ks[4], (D, N_KV_HEADS * HEAD_DIM), jnp.float32) * s, 'bv': jnp.zeros((N_KV_HEADS * HEAD_DIM,), jnp.float32), 'wo': jax.random.normal(ks[5], (N_HEADS * HEAD_DIM, D), jnp.float32) * s, 'w_gate': jax.random.normal(ks[6], (D, I), jnp.float32) * s, 'w_up': jax.random.normal(ks[7], (D, I), jnp.float32) * s, 'w_down': jax.random.normal(ks[8], (I, D), jnp.float32) * s, 'ln1_w': jnp.ones((D,), jnp.float32), 'ln2_w': jnp.ones((D,), jnp.float32)}
    _L0_ffn_all = _L0_ffn_setup()
    _L0_ffn_in = {k: v for k, v in _L0_ffn_all.items() if k in ('w_router', 'wq', 'bq', 'wk', 'bk', 'wv', 'bv', 'wo', 'w_gate', 'w_up', 'w_down', 'ln1_w', 'ln2_w')}
    del _L0_ffn_all
    return {'x': x, 'ctx_2048': ctx_2048, 'mask_1xSxS2_ff0': mask_1xSxS2_ff0, 'L0_xattn_Wq': _L0_xattn_in['Wq'], 'L0_xattn_bq': _L0_xattn_in['bq'], 'L0_xattn_Wk': _L0_xattn_in['Wk'], 'L0_xattn_bk': _L0_xattn_in['bk'], 'L0_xattn_Wv': _L0_xattn_in['Wv'], 'L0_xattn_bv': _L0_xattn_in['bv'], 'L0_xattn_Wo': _L0_xattn_in['Wo'], 'L0_xattn_qn_w': _L0_xattn_in['qn_w'], 'L0_xattn_kn_w': _L0_xattn_in['kn_w'], 'L0_ffn_w_router': _L0_ffn_in['w_router'], 'L0_ffn_wq': _L0_ffn_in['wq'], 'L0_ffn_bq': _L0_ffn_in['bq'], 'L0_ffn_wk': _L0_ffn_in['wk'], 'L0_ffn_bk': _L0_ffn_in['bk'], 'L0_ffn_wv': _L0_ffn_in['wv'], 'L0_ffn_bv': _L0_ffn_in['bv'], 'L0_ffn_wo': _L0_ffn_in['wo'], 'L0_ffn_w_gate': _L0_ffn_in['w_gate'], 'L0_ffn_w_up': _L0_ffn_in['w_up'], 'L0_ffn_w_down': _L0_ffn_in['w_down'], 'L0_ffn_ln1_w': _L0_ffn_in['ln1_w'], 'L0_ffn_ln2_w': _L0_ffn_in['ln2_w']}

def reference(x, ctx_2048, mask_1xSxS2_ff0, L0_xattn_Wq, L0_xattn_bq, L0_xattn_Wk, L0_xattn_bk, L0_xattn_Wv, L0_xattn_bv, L0_xattn_Wo, L0_xattn_qn_w, L0_xattn_kn_w, L0_ffn_w_router, L0_ffn_wq, L0_ffn_bq, L0_ffn_wk, L0_ffn_bk, L0_ffn_wv, L0_ffn_bv, L0_ffn_wo, L0_ffn_w_gate, L0_ffn_w_up, L0_ffn_w_down, L0_ffn_ln1_w, L0_ffn_ln2_w):
    import jax
    import jax.numpy as jnp

    def _L0_xattn_ref(hidden_states, encoder_hidden_states, attention_mask, Wq, bq, Wk, bk, Wv, bv, Wo, qn_w, kn_w):
        import jax, jax.numpy as jnp
        import numpy as np
        H = 512
        NH = 16
        NKV = 4
        HD = 128
        GROUPS = NH // NKV
        EPS = 1e-06
        B, S, SE = (1, 512, 1024)

        def _rmsnorm(x, w, eps=EPS):
            xf = x.astype(jnp.float32)
            var = jnp.mean(xf * xf, axis=-1, keepdims=True)
            return (xf * jax.lax.rsqrt(var + eps)).astype(x.dtype) * w
        b, s, _ = hidden_states.shape
        se = encoder_hidden_states.shape[1]
        q = (hidden_states @ Wq + bq).reshape(b, s, NH, HD).transpose(0, 2, 1, 3)
        k = (encoder_hidden_states @ Wk + bk).reshape(b, se, NKV, HD).transpose(0, 2, 1, 3)
        v = (encoder_hidden_states @ Wv + bv).reshape(b, se, NKV, HD).transpose(0, 2, 1, 3)
        k = jnp.repeat(k, GROUPS, axis=1)
        v = jnp.repeat(v, GROUPS, axis=1)
        q = _rmsnorm(q, qn_w)
        k = _rmsnorm(k, kn_w)
        scale = 1.0 / np.sqrt(HD).astype(np.float32)
        scores = jnp.einsum('bhsd,bhed->bhse', q, k) * scale
        scores = scores + attention_mask[:, None, :, :]
        probs = jax.nn.softmax(scores.astype(jnp.float32), axis=-1).astype(q.dtype)
        out = jnp.einsum('bhse,bhed->bhsd', probs, v)
        out = out.transpose(0, 2, 1, 3).reshape(b, s, NH * HD)
        return out @ Wo

    def _L0_ffn_ref(hidden_states, w_router, wq, bq, wk, bk, wv, bv, wo, w_gate, w_up, w_down, ln1_w, ln2_w):
        import jax, jax.numpy as jnp
        import numpy as np
        CAPACITY = 0.125
        HEAD_DIM = 128
        N_HEADS = 16
        N_KV_HEADS = 8
        ROPE_THETA = 10000.0
        EPS = 1e-06

        def _rms_norm(x, w):
            return x * jax.lax.rsqrt(jnp.mean(x * x, axis=-1, keepdims=True) + EPS) * w

        def _rotate_half(t):
            h = t.shape[-1] // 2
            return jnp.concatenate([-t[..., h:], t[..., :h]], axis=-1)
        B, T, D = hidden_states.shape
        k = max(1, int(T * CAPACITY))
        scores = jnp.einsum('btd,d->bt', hidden_states, w_router)
        _, idx = jax.lax.top_k(scores, k)
        idx = jnp.sort(idx, axis=-1)
        b = jnp.arange(B)[:, None]
        sel = hidden_states[b, idx]
        sel_scores = scores[b, idx]
        S = B * k
        x = sel.reshape(S, D)
        pos = idx.reshape(S)
        inv_freq = 1.0 / ROPE_THETA ** (jnp.arange(0, HEAD_DIM, 2, dtype=jnp.float32) / HEAD_DIM)
        ang = pos.astype(jnp.float32)[:, None] * inv_freq
        cos = jnp.concatenate([jnp.cos(ang), jnp.cos(ang)], axis=-1)[:, None, :]
        sin = jnp.concatenate([jnp.sin(ang), jnp.sin(ang)], axis=-1)[:, None, :]
        h = _rms_norm(x, ln1_w)
        q = (h @ wq + bq).reshape(S, N_HEADS, HEAD_DIM)
        kk = (h @ wk + bk).reshape(S, N_KV_HEADS, HEAD_DIM)
        v = (h @ wv + bv).reshape(S, N_KV_HEADS, HEAD_DIM)
        q = q * cos + _rotate_half(q) * sin
        kk = kk * cos + _rotate_half(kk) * sin
        rep = N_HEADS // N_KV_HEADS
        kk = jnp.repeat(kk, rep, axis=1)
        v = jnp.repeat(v, rep, axis=1)
        att = jnp.einsum('shd,thd->hst', q, kk) / np.sqrt(HEAD_DIM)
        causal = jnp.tril(jnp.ones((S, S), bool))
        att = jnp.where(causal[None], att, jnp.finfo(att.dtype).min)
        att = jax.nn.softmax(att, axis=-1)
        attn_out = jnp.einsum('hst,thd->shd', att, v).reshape(S, N_HEADS * HEAD_DIM) @ wo
        x1 = x + attn_out
        h2 = _rms_norm(x1, ln2_w)
        mlp = jax.nn.silu(h2 @ w_gate) * (h2 @ w_up) @ w_down
        processed = x1 + mlp
        gate = jax.nn.sigmoid(sel_scores).reshape(S, 1)
        gated = gate * processed + (1.0 - gate) * x
        output = hidden_states.at[b, idx].set(gated.reshape(B, k, D))
        return output
    x = x + _L0_xattn_ref(_layernorm(x, axis=-1), ctx_2048, mask_1xSxS2_ff0, L0_xattn_Wq, L0_xattn_bq, L0_xattn_Wk, L0_xattn_bk, L0_xattn_Wv, L0_xattn_bv, L0_xattn_Wo, L0_xattn_qn_w, L0_xattn_kn_w)
    x = x + _L0_ffn_ref(_layernorm(x, axis=-1), L0_ffn_w_router, L0_ffn_wq, L0_ffn_bq, L0_ffn_wk, L0_ffn_bk, L0_ffn_wv, L0_ffn_bv, L0_ffn_wo, L0_ffn_w_gate, L0_ffn_w_up, L0_ffn_w_down, L0_ffn_ln1_w, L0_ffn_ln2_w)
    return x

_drawn_inputs = setup_inputs


def setup_inputs(seed=0):
    import zlib

    import numpy as np

    out = dict(_drawn_inputs(seed))
    spreads = {'L0_xattn_qn_w': (1.0, 0.6),
     'L0_xattn_kn_w': (1.0, 0.6),
     'L0_ffn_bq': (0.0, 0.8),
     'L0_ffn_bk': (0.0, 0.8),
     'L0_ffn_bv': (0.0, 0.682),
     'L0_ffn_ln1_w': (1.0, 0.6),
     'L0_ffn_ln2_w': (1.0, 0.6)}
    factors = {'L0_xattn_bq': 8.0,
     'L0_xattn_bk': 8.0,
     'L0_xattn_bv': 3.156,
     'L0_ffn_w_router': 2.91,
     'L0_ffn_wq': 8.0,
     'L0_ffn_wk': 8.0,
     'L0_ffn_wv': 5.17,
     'L0_ffn_wo': 3.623,
     'L0_ffn_w_gate': 4.545,
     'L0_ffn_w_up': 4.424,
     'L0_ffn_w_down': 4.467}
    for name, (base, spread) in spreads.items():
        noise = np.random.default_rng([zlib.crc32(name.encode()), seed]).standard_normal(out[name].shape)
        drawn = base * np.exp(spread * noise) if base else spread * noise
        out[name] = jnp.asarray(drawn.astype(out[name].dtype))
    for name, factor in factors.items():
        out[name] = (out[name] * factor).astype(out[name].dtype)
    return out
```

```python
import concourse.bass as bass
from concourse import mybir
from contextlib import ExitStack


def xattn_then_routed_ffn(
    nc: bass.Bass,
    x: bass.AP,
    context: bass.AP,
    attn_mask: bass.AP,
    Wq: bass.AP,
    bq: bass.AP,
    Wk: bass.AP,
    bk: bass.AP,
    Wv: bass.AP,
    bv: bass.AP,
    Wo: bass.AP,
    qn_w: bass.AP,
    kn_w: bass.AP,
    w_router: bass.AP,
    ffn_wq: bass.AP,
    ffn_bq: bass.AP,
    ffn_wk: bass.AP,
    ffn_bk: bass.AP,
    ffn_wv: bass.AP,
    ffn_bv: bass.AP,
    ffn_wo: bass.AP,
    w_gate: bass.AP,
    w_up: bass.AP,
    w_down: bass.AP,
    ln1_w: bass.AP,
    ln2_w: bass.AP,
    rope_table: bass.AP,
    slot_base: bass.AP,
    out: bass.AP,
):
    fp32 = mybir.dt.float32
    f32r = mybir.dt.float32r
    bf16 = mybir.dt.bfloat16
    u32 = mybir.dt.uint32
    ALU = mybir.AluOpType
    ACT = mybir.ActivationFunctionType
    AX = mybir.AxisListType

    P = 128
    NB, S, D = x.shape
    DC = D // P
    HD = qn_w.shape[0]
    NH = Wq.shape[1] // HD
    NKV = Wk.shape[1] // HD
    QUAD = NH // NKV
    NQUAD = NKV
    STEPS = NB * NQUAD
    W = QUAD * HD
    PICK = S // 8
    NSEL = NB * PICK
    NJ = NSEL // P
    BPJ = NB // NJ
    SCALE = float(HD) ** -0.5
    EPS_LN, EPS_RMS = 1e-5, 1e-6
    MASKED = -3.0e38
    FH = ffn_wq.shape[1] // HD
    FKV = ffn_wk.shape[1] // HD
    FQ = FH // QUAD
    FK = FKV // QUAD
    FI = w_gate.shape[1] // W
    NRAW, NSLOT = 2, 4

    x_rows = x.rearrange("b s d -> (b s) d")
    ctx_rows = context.rearrange("b s d -> (b s) d")
    out_rows = out.rearrange("b s d -> (b s) d")
    k_store = nc.dram_tensor("k_store", [NB * P, NKV * S], fp32, kind="Internal").ap()
    v_store = nc.dram_tensor("v_store", [NB * P, NKV * HD], fp32, kind="Internal").ap()
    h_store = nc.dram_tensor("h_store", [NB * S, D], fp32, kind="Internal").ap()

    def chunked(w):
        return w.rearrange("(c p) n -> p c n", p=P)

    def columns(w, n):
        return chunked(w)[:, :, n * W:(n + 1) * W]

    def rows(w, g):
        return chunked(w[g * 4 * P:(g + 1) * 4 * P, :])

    PIECES = [columns(ffn_wk, n) for n in range(FK)] + [columns(ffn_wv, n) for n in range(FK)]
    PIECES += [columns(ffn_wq, 0), columns(ffn_wq, 1)]
    for n in range(FQ - 2):
        PIECES += [rows(ffn_wo, n), columns(ffn_wq, n + 2)]
    PIECES += [rows(ffn_wo, FQ - 2), rows(ffn_wo, FQ - 1)]
    PIECES += [columns(w_gate, 0), columns(w_up, 0)]
    for m in range(FI - 1):
        PIECES += [columns(w_gate, m + 1), columns(w_up, m + 1), rows(w_down, m)]
    PIECES += [rows(w_down, FI - 1)]
    NP = len(PIECES)
    P_WK, P_WV, P_WQ0 = 0, FK, 2 * FK

    def p_wq(n):
        return P_WQ0 + n if n < 2 else P_WQ0 + 2 * n - 1

    def p_wo(n):
        return P_WQ0 + 2 * n + 2 if n < FQ - 1 else P_WQ0 + 2 * FQ - 1

    P_MLP = P_WQ0 + 2 * FQ

    def p_gate(m):
        return P_MLP if m == 0 else P_MLP + 3 * m - 1

    def p_up(m):
        return p_gate(m) + 1

    def p_down(m):
        return P_MLP + 3 * m + 4 if m < FI - 1 else NP - 1

    ctx = ExitStack()
    with ctx:
        def sem(name):
            return ctx.enter_context(nc.semaphore(name))

        def sb_in(stack, name, shape, dt=fp32):
            return stack.enter_context(nc.sbuf_tensor(name, shape, dt))

        def split_in(stack, name, shape):
            return (sb_in(stack, name + "_hi", shape, f32r), sb_in(stack, name + "_lo", shape, f32r))

        ident = sb_in(ctx, "ident", [P, P])
        earlier = sb_in(ctx, "earlier", [P, P])
        later = sb_in(ctx, "later", [P, P])
        causal = sb_in(ctx, "causal", [P, 2 * P])
        slots = sb_in(ctx, "slots", [P, PICK])
        token = sb_in(ctx, "token", [P, 1])
        half = sb_in(ctx, "half", [P, QUAD])
        eps_head = sb_in(ctx, "eps_head", [P, QUAD])
        eps_ln = sb_in(ctx, "eps_ln", [P, 1])
        qw = sb_in(ctx, "qw", [P, 1])
        kw = sb_in(ctx, "kw", [P, 1])
        base_row = sb_in(ctx, "base_row", [P, NJ])
        picked = sb_in(ctx, "picked", [P, NB])
        raw = [sb_in(ctx, f"raw{i}", [P, 4, W]) for i in range(NRAW)]

        wq_place = ExitStack()
        wq_hi, wq_lo = split_in(wq_place, "wq", [P, DC, NH * HD])
        wo_place = ExitStack()
        wo_hi, wo_lo = split_in(wo_place, "wo", [P, NH, D])

        with ExitStack() as st:
            cx = [sb_in(st, f"cx{i}", [P, D]) for i in range(2)]
            cT_hi, cT_lo = zip(*[split_in(st, f"cT{i}", [P, DC, P]) for i in range(2)])
            wq_raw = sb_in(st, "wq_raw", [P, DC, HD])
            wo_raw = sb_in(st, "wo_raw", [P, D])
            wk_hi, wk_lo = split_in(st, "wk", [P, DC, W])
            wv_hi, wv_lo = split_in(st, "wv", [P, DC, W])
            k_row = sb_in(st, "k_row", [P, NKV, HD])
            k_out = sb_in(st, "k_out", [P, NKV * S])
            v_out = sb_in(st, "v_out", [P, NKV * HD])
            bk_row = sb_in(st, "bk_row", [P, NKV * HD])
            bv_row = sb_in(st, "bv_row", [P, NKV * HD])
            k_sq = sb_in(st, "k_sq", [P, NKV, HD], bf16)
            k_ss = sb_in(st, "k_ss", [P, NKV])
            k_rs = sb_in(st, "k_rs", [P, NKV])

        with ExitStack() as st:
            xr = sb_in(st, "xr", [P, D])
            xn = sb_in(st, "xn", [P, D])
            xT_hi, xT_lo = split_in(st, "xT", [P, DC, P])
            k_raw = sb_in(st, "k_raw", [P, NKV * S])
            v_raw = sb_in(st, "v_raw", [P, NKV * HD])
            q_row = sb_in(st, "q_row", [P, QUAD, HD])
            q_nrm = sb_in(st, "q_nrm", [P, QUAD, HD])
            kT_hi, kT_lo = split_in(st, "kT", [P, NKV * S])
            v_hi, v_lo = split_in(st, "v", [P, NKV * HD])
            qT_hi, qT_lo = split_in(st, "qT", [P, W])
            s_row = sb_in(st, "s_row", [P, QUAD, S])
            p_row = sb_in(st, "p_row", [P, QUAD, S])
            pT_hi, pT_lo = split_in(st, "pT", [P, W])
            oT_hi, oT_lo = split_in(st, "oT", [P, W])
            x_res = sb_in(st, "x_res", [P, D])
            x1 = sb_in(st, "x1", [P, D])
            h_row = sb_in(st, "h_row", [P, D])
            mask = sb_in(st, "mask", [P, S])
            bq_row = sb_in(st, "bq_row", [P, NH * HD])
            wr_row = sb_in(st, "wr_row", [P, D])
            dot_junk = sb_in(st, "dot_junk", [P, D], bf16)
            sq_junk = sb_in(st, "sq_junk", [P, QUAD, HD], bf16)
            rank_junk = sb_in(st, "rank_junk", [P, 2, S], bf16)
            score_wide = sb_in(st, "score_wide", [P, S])
            q_ss = sb_in(st, "q_ss", [P, QUAD])
            q_rs = sb_in(st, "q_rs", [P, QUAD])
            neg_max = sb_in(st, "neg_max", [P, QUAD])
            p_sum = sb_in(st, "p_sum", [P, QUAD])
            p_inv = sb_in(st, "p_inv", [P, QUAD])
            bn = sb_in(st, "bn", [P, 6])
            mv = sb_in(st, "mv", [P, 2])
            rstd = sb_in(st, "rstd", [P, 1])
            bn1 = sb_in(st, "bn1", [P, 6])
            mv1 = sb_in(st, "mv1", [P, 2])
            rstd1 = sb_in(st, "rstd1", [P, 1])
            score = sb_in(st, "score", [P, 1])
            above = sb_in(st, "above", [P, 1])
            tied = sb_in(st, "tied", [P, 1])
        wo_place.close()
        wq_place.close()

        with ExitStack() as st:
            wp_hi = [sb_in(st, f"wp_hi{i}", [P, 4, W], f32r) for i in range(NSLOT)]
            wp_lo = [sb_in(st, f"wp_lo{i}", [P, 4, W], f32r) for i in range(NSLOT)]
            hT_hi, hT_lo = split_in(st, "hT", [P, NJ, DC, P])
            fkT_hi, fkT_lo = split_in(st, "fkT", [P, FKV, NSEL])
            fv_hi, fv_lo = split_in(st, "fv", [P, NJ, FKV * HD])
            fqT_hi, fqT_lo = split_in(st, "fqT", [P, NJ, QUAD, P])
            foT_hi, foT_lo = split_in(st, "foT", [P, QUAD, NSEL])
            fp0_hi, fp0_lo = split_in(st, "fp0", [P, QUAD, NSEL])
            fp1_hi, fp1_lo = split_in(st, "fp1", [P, QUAD, P])
            fs = [sb_in(st, f"fs{i}", [P, W]) for i in range(3)]
            h_sel = [sb_in(st, f"h_sel{j}", [P, D]) for j in range(NJ)]
            base = [sb_in(st, f"base{j}", [P, D]) for j in range(NJ)]
            rope = [sb_in(st, f"rope{j}", [P, 4 * (HD // 2)]) for j in range(NJ)]
            hn_row = [sb_in(st, f"hn_row{j}", [P, D]) for j in range(NJ)]
            proj = [sb_in(st, f"proj{i}", [P, W]) for i in range(2)]
            turned = [sb_in(st, f"turned{j}", [P, W]) for j in range(NJ)]
            by_cos = sb_in(st, "by_cos", [P, W])
            by_sin = sb_in(st, "by_sin", [P, W])
            attn_row = [sb_in(st, f"attn_row{j}", [P, D]) for j in range(NJ)]
            x2_row = [sb_in(st, f"x2_row{j}", [P, D]) for j in range(NJ)]
            bias_row = [sb_in(st, f"bias_row{i}", [P, W]) for i in range(2)]
            ln1_row = sb_in(st, "ln1_row", [P, D])
            ln2_row = sb_in(st, "ln2_row", [P, D])
            wr2_row = sb_in(st, "wr2_row", [P, D])
            onehot = sb_in(st, "onehot", [P, NB, PICK])
            row_idx = [sb_in(st, f"row_idx{j}", [P, 1], u32) for j in range(NJ)]
            pos_idx = [sb_in(st, f"pos_idx{j}", [P, 1], u32) for j in range(NJ)]
            f_ss = sb_in(st, "f_ss", [P, 2 * NJ])
            f_ms = sb_in(st, "f_ms", [P, 2 * NJ])
            f_rs = sb_in(st, "f_rs", [P, 2 * NJ])
            f_max = sb_in(st, "f_max", [P, 8])
            f_sum = sb_in(st, "f_sum", [P, 8])
            f_inv = sb_in(st, "f_inv", [P, 8])
            g_dot = sb_in(st, "g_dot", [P, NJ])
            g_exp = sb_in(st, "g_exp", [P, NJ])
            g_one = sb_in(st, "g_one", [P, NJ])
            gate = sb_in(st, "gate", [P, NJ])
        act_row = turned
        tanh_row = proj
        final = hn_row

        banks = {n: ctx.enter_context(nc.psum_tensor(n, [P, W], fp32))
                 for n in ("b_q", "b_qT", "b_s", "b_pT", "b_o", "b_y", "b_xT", "b_rank")}
        b_q, b_qT, b_s, b_pT, b_o, b_y, b_xT, b_rank = banks.values()
        b_c, b_k, b_v, b_kT = b_xT, b_q, b_s, b_qT
        f_proj = [b_q, b_y]
        f_T, f_T2, f_S, f_O = b_qT, b_pT, b_s, b_o
        f_W = [b_xT, b_rank]

        const_made = sem("const_made")
        const_loaded = sem("const_loaded")
        kw_scaled = sem("kw_scaled")
        wk_loaded = [sem(f"wk_loaded{i}") for i in range(2)]
        wv_loaded = [sem("wv_loaded")]
        kv_w_hi = sem("kv_w_hi")
        kv_w_lo = sem("kv_w_lo")
        kv_bias_loaded = sem("kv_bias_loaded")
        cx_loaded = [sem(f"cx_loaded{i}") for i in range(2)]
        c_turned = sem("c_turned")
        c_hi = sem("c_hi")
        c_lo = sem("c_lo")
        k_projected = sem("k_projected")
        v_projected = sem("v_projected")
        k_biased = sem("k_biased")
        v_biased = sem("v_biased")
        k_squared = sem("k_squared")
        k_summed = sem("k_summed")
        k_rooted = sem("k_rooted")
        k_normed = sem("k_normed")
        k_turned = sem("k_turned")
        k_weighted = sem("k_weighted")
        k_stored = sem("k_stored")
        v_stored = sem("v_stored")
        wq_loaded = sem("wq_loaded")
        wo_loaded = sem("wo_loaded")
        w_hi = sem("w_hi")
        w_lo = sem("w_lo")
        rows_loaded = sem("rows_loaded")
        bq_loaded = sem("bq_loaded")
        x_loaded = sem("x_loaded")
        x_stats = sem("x_stats")
        x_mean = sem("x_mean")
        x_eps = sem("x_eps")
        x_rstd = sem("x_rstd")
        x_normed = sem("x_normed")
        x_turned = sem("x_turned")
        xT_hi_done = sem("xT_hi_done")
        xT_lo_done = sem("xT_lo_done")
        k_loaded = sem("k_loaded")
        v_loaded = sem("v_loaded")
        kT_hi_done = sem("kT_hi_done")
        kT_lo_done = sem("kT_lo_done")
        v_hi_done = sem("v_hi_done")
        v_lo_done = sem("v_lo_done")
        q_projected = sem("q_projected")
        q_biased = sem("q_biased")
        q_squared = sem("q_squared")
        q_summed = sem("q_summed")
        q_rooted = sem("q_rooted")
        q_normed = sem("q_normed")
        q_turned = sem("q_turned")
        qT_hi_done = sem("qT_hi_done")
        qT_lo_done = sem("qT_lo_done")
        scored = sem("scored")
        s_masked = sem("s_masked")
        s_maxed = sem("s_maxed")
        p_exped = sem("p_exped")
        p_inverted = sem("p_inverted")
        p_normed = sem("p_normed")
        p_turned = sem("p_turned")
        pT_hi_done = sem("pT_hi_done")
        pT_lo_done = sem("pT_lo_done")
        mixed = sem("mixed")
        oT_hi_done = sem("oT_hi_done")
        oT_lo_done = sem("oT_lo_done")
        y_added = sem("y_added")
        res_loaded = sem("res_loaded")
        x1_made = sem("x1_made")
        x1_stats = sem("x1_stats")
        x1_mean = sem("x1_mean")
        x1_eps = sem("x1_eps")
        x1_rstd = sem("x1_rstd")
        h_made = sem("h_made")
        h_stored = sem("h_stored")
        base_made = sem("base_made")
        base_stored = sem("base_stored")
        scored_row = sem("scored_row")
        score_spread = sem("score_spread")
        score_turned = sem("score_turned")
        counted_above = sem("counted_above")
        counted_tied = sem("counted_tied")
        picks_made = sem("picks_made")
        raw_loaded = [sem(f"raw_loaded{i}") for i in range(NRAW)]
        piece_hi = sem("piece_hi")
        piece_lo_dve = sem("piece_lo_dve")
        piece_lo_pool = sem("piece_lo_pool")
        place_found = sem("place_found")
        onehot_raw = sem("onehot_raw")
        onehot_made = sem("onehot_made")
        rows_found = sem("rows_found")
        idx_made = sem("idx_made")
        gathered_h = [sem(f"gathered_h{j}") for j in range(NJ)]
        gathered_rope = [sem(f"gathered_rope{j}") for j in range(NJ)]
        gathered_base = [sem(f"gathered_base{j}") for j in range(NJ)]
        f_rows_loaded = sem("f_rows_loaded")
        bias_loaded = [sem(f"bias_loaded{i}") for i in range(2)]
        f_squared = sem("f_squared")
        f_meaned = sem("f_meaned")
        f_rooted = sem("f_rooted")
        hn_made = sem("hn_made")
        h_turned = sem("h_turned")
        hT_hi_done = sem("hT_hi_done")
        hT_lo_done = sem("hT_lo_done")
        f_projected = sem("f_projected")
        f_biased = sem("f_biased")
        cos_done = sem("cos_done")
        sin_done = sem("sin_done")
        f_roped = sem("f_roped")
        fv_hi_done = sem("fv_hi_done")
        fv_lo_done = sem("fv_lo_done")
        fk_turned = sem("fk_turned")
        fk_hi_done = sem("fk_hi_done")
        fk_lo_done = sem("fk_lo_done")
        fq_turned = sem("fq_turned")
        fq_hi_done = sem("fq_hi_done")
        fq_lo_done = sem("fq_lo_done")
        f_scored = sem("f_scored")
        f_masked = sem("f_masked")
        f_maxed = sem("f_maxed")
        f_exped = sem("f_exped")
        f_inverted = sem("f_inverted")
        f_normed = sem("f_normed")
        fp_turned = sem("fp_turned")
        fp_hi_done = sem("fp_hi_done")
        fp_lo_done = sem("fp_lo_done")
        f_mixed = sem("f_mixed")
        fo_hi_done = sem("fo_hi_done")
        fo_lo_done = sem("fo_lo_done")
        attn_done = sem("attn_done")
        attn_copied = sem("attn_copied")
        x2_made = sem("x2_made")
        gated = sem("gated")
        upped = sem("upped")
        tanh_done = sem("tanh_done")
        silu_done = sem("silu_done")
        act_done = sem("act_done")
        act_turned = sem("act_turned")
        aT_hi_done = sem("aT_hi_done")
        aT_lo_done = sem("aT_lo_done")
        mlp_done = sem("mlp_done")
        g_dotted = sem("g_dotted")
        g_exped = sem("g_exped")
        g_plus = sem("g_plus")
        g_made = sem("g_made")
        delta_made = sem("delta_made")
        final_made = sem("final_made")
        out_stored = [sem(f"out_stored{j}") for j in range(NJ)]

        block = ctx.enter_context(nc.Block())

        def wait(eng, s, n):
            if not isinstance(n, int) or n > 0:
                eng.wait_ge(s, n)

        used_up = {}
        for n in range(FK):
            used_up[P_WK + n] = (f_projected, NJ * (n + 1))
            used_up[P_WV + n] = (f_projected, NJ * (FK + n + 1))
        for n in range(FQ):
            used_up[p_wq(n)] = (f_projected, NJ * (2 * FK + n + 1))
            used_up[p_wo(n)] = (attn_done, NJ * (n + 1))
        for m in range(FI):
            used_up[p_gate(m)] = (gated, NJ * (m + 1))
            used_up[p_up(m)] = (upped, NJ * (m + 1))
            used_up[p_down(m)] = (mlp_done, NJ * (m + 1))

        def keys_over(eng):
            eng.wait_ge(k_stored, 16 * NB)
            eng.wait_ge(v_stored, 16 * NB)
            eng.wait_ge(w_lo, 2 * NB)
            eng.wait_ge(w_hi, 2 * NB)

        def layer1_over(eng):
            eng.wait_ge(h_stored, 16 * NB)
            eng.wait_ge(base_stored, 16 * NB)
            eng.wait_ge(picks_made, NB)

        def layer1_batches(one_batch):
            def run(eng):
                one_batch(0, True, False)
                with eng.Fori(1, NB - 1) as b:
                    one_batch(b, False, False)
                one_batch(NB - 1, False, True)
            return run

        @block.sync
        def _(sp):
            def spread(dst, vec):
                return sp.dma_start(dst, vec.partition_broadcast(P))

            sp.dma_start(cx[0][:], ctx_rows[0:S, :]).then_inc(cx_loaded[0], 16)
            for i in range(2):
                half_chunks = slice(i * DC // 2, (i + 1) * DC // 2)
                sp.dma_start(raw[0][:, half_chunks, :], chunked(Wk)[:, half_chunks, :]).then_inc(wk_loaded[i], 16)
            sp.dma_start(cx[1][:], ctx_rows[S:2 * S, :]).then_inc(cx_loaded[1], 16)
            sp.dma_start(raw[1][:], chunked(Wv)).then_inc(wv_loaded[0], 16)
            spread(bk_row[:], bk).then_inc(kv_bias_loaded, 16)
            spread(bv_row[:], bv).then_inc(kv_bias_loaded, 16)
            sp.dma_start(qw[:], qn_w.rearrange("(p a) -> p a", a=1)).then_inc(const_loaded, 16)
            sp.dma_start(kw[:], kn_w.rearrange("(p a) -> p a", a=1)).then_inc(const_loaded, 16)
            sp.dma_start(base_row[:], slot_base).then_inc(const_loaded, 16)

            def store_v(b):
                sp.wait_ge(v_biased, b + 1)
                sp.dma_start(v_store[bass.ds(b * P, P), :], v_out[:]).then_inc(v_stored, 16)

            def store_k(b):
                sp.wait_ge(k_weighted, b + 1)
                sp.dma_start(k_store[bass.ds(b * P, P), :], k_out[:]).then_inc(k_stored, 16)

            def kv_batch(b, par, first, last, last_two):
                wait(sp, w_lo, 2 * b)
                sp.dma_start(wq_raw[:], chunked(Wq)[:, :, bass.ds(b * HD, HD)]).then_inc(wq_loaded, 16)
                sp.dma_start(wo_raw[:], Wo[bass.ds(b * P, P), :]).then_inc(wo_loaded, 16)
                if not first:
                    store_v(b - 1)
                if not last_two:
                    sp.wait_ge(c_turned, b + 1)
                    sp.dma_start(cx[par][:], ctx_rows[bass.ds((b + 2) * S, S), :]
                                 ).then_inc(cx_loaded[par], 16)
                if not first:
                    store_k(b - 1)

            kv_batch(0, 0, True, False, False)
            with sp.Fori(0, NB // 2 - 2) as g:
                kv_batch(2 * g + 1, 1, False, False, False)
                kv_batch(2 * g + 2, 0, False, False, False)
            kv_batch(NB - 3, 1, False, False, False)
            kv_batch(NB - 2, 0, False, False, True)
            kv_batch(NB - 1, 1, False, True, True)
            sp.wait_ge(c_turned, NB - 1)
            sp.dma_start(xr[:], x_rows[0:S, :]).then_inc(x_loaded, 16)
            store_v(NB - 1)
            store_k(NB - 1)
            for i in range(NRAW):
                sp.wait_ge(kv_w_hi, DC * (i + 1))
                sp.wait_ge(kv_w_lo, DC * (i + 1))
                sp.dma_start(raw[i][:], PIECES[i]).then_inc(raw_loaded[i], 16)

            keys_over(sp)

            def load_x(b):
                sp.dma_start(xr[:], x_rows[bass.ds(b * S, S), :]).then_inc(x_loaded, 16)

            def load_k(b):
                sp.dma_start(k_raw[:], k_store[bass.ds(b * P, P), :]).then_inc(k_loaded, 16)

            def load_v(b):
                sp.dma_start(v_raw[:], v_store[bass.ds(b * P, P), :]).then_inc(v_loaded, 16)

            spread(bq_row[:], bq).then_inc(bq_loaded, 16)
            load_k(0)
            load_v(0)
            sp.dma_start(mask[:], attn_mask.rearrange("a s t -> (a s) t")).then_inc(rows_loaded, 16)
            spread(wr_row[:], w_router).then_inc(rows_loaded, 16)
            sp.dma_start(x_res[:], x_rows[0:S, :]).then_inc(res_loaded, 16)

            def store_rows(b):
                sp.wait_ge(h_made, b + 1)
                sp.dma_start(h_store[bass.ds(b * S, S), :], h_row[:]).then_inc(h_stored, 16)
                sp.wait_ge(base_made, b + 1)
                sp.dma_start(out_rows[bass.ds(b * S, S), :], x1[:]).then_inc(base_stored, 16)

            def attend(b, first, last):
                if not last:
                    sp.wait_ge(x_normed, b + 1)
                    load_x(b + 1)
                    sp.wait_ge(kT_hi_done, b + 1)
                    sp.wait_ge(kT_lo_done, b + 1)
                    load_k(b + 1)
                if not first:
                    sp.wait_ge(x1_made, b)
                    sp.dma_start(x_res[:], x_rows[bass.ds(b * S, S), :]).then_inc(res_loaded, 16)
                if not last:
                    sp.wait_ge(v_hi_done, b + 1)
                    sp.wait_ge(v_lo_done, b + 1)
                    load_v(b + 1)
                if not first:
                    store_rows(b - 1)

            attend(0, True, False)
            with sp.Fori(1, NB - 1) as b:
                attend(b, False, False)
            attend(NB - 1, False, True)
            store_rows(NB - 1)

            def load_piece(n):
                sp.wait_ge(piece_hi, n - NRAW + 1)
                sp.wait_ge(piece_lo_dve, n - NRAW + 1)
                sp.wait_ge(piece_lo_pool, n - NRAW + 1)
                sp.dma_start(raw[n % NRAW][:], PIECES[n]).then_inc(raw_loaded[n % NRAW], 16)

            load_piece(2)
            load_piece(3)
            layer1_over(sp)
            spread(ln1_row[:], ln1_w).then_inc(f_rows_loaded, 16)
            spread(ln2_row[:], ln2_w).then_inc(f_rows_loaded, 16)
            spread(wr2_row[:], w_router).then_inc(f_rows_loaded, 16)
            BIASES = [ffn_bk[n * W:(n + 1) * W] for n in range(FK)]
            BIASES += [ffn_bv[n * W:(n + 1) * W] for n in range(FK)]
            BIASES += [ffn_bq[n * W:(n + 1) * W] for n in range(FQ)]
            bias_before = {P_WK + n: n for n in range(FK)}
            bias_before.update({P_WV + n: FK + n for n in range(FK)})
            bias_before.update({p_wq(n): 2 * FK + n for n in range(FQ)})

            def load_bias(i):
                if i >= 2:
                    sp.wait_ge(f_biased, NJ * (i - 1))
                spread(bias_row[i % 2][:], BIASES[i]).then_inc(bias_loaded[i % 2], 16)

            load_bias(0)
            load_bias(1)
            for n in range(4, NP):
                if n - 2 in bias_before and bias_before[n - 2] >= 2:
                    load_bias(bias_before[n - 2])
                load_piece(n)
            for j in range(NJ):
                sp.wait_ge(out_stored[j], 16)

        @block.gpsimd
        def _(pool):
            pool.memset(ident[:], 0.0).then_inc(const_made, 1)
            pool.memset(earlier[:], 1.0).then_inc(const_made, 1)
            pool.memset(later[:], 1.0).then_inc(const_made, 1)
            pool.memset(causal[:], 0.0).then_inc(const_made, 1)
            pool.memset(half[:], -0.5).then_inc(const_made, 1)
            pool.memset(eps_head[:], HD * EPS_RMS).then_inc(const_made, 1)
            pool.memset(eps_ln[:], EPS_LN).then_inc(const_made, 1)
            pool.iota(slots[:], pattern=[[1, PICK]], base=0, channel_multiplier=0,
                      allow_small_or_imprecise_dtypes=True).then_inc(const_made, 1)
            pool.iota(token[:], pattern=[[0, 1]], base=0, channel_multiplier=1,
                      allow_small_or_imprecise_dtypes=True).then_inc(const_made, 1)
            pool.wait_ge(const_made, 9)
            pool.affine_select(out=ident[:], in_=ident[:], compare_op=ALU.not_equal, fill=1.0,
                               base=0, pattern=[[-1, P]], channel_multiplier=1).then_inc(const_made, 1)
            pool.affine_select(out=earlier[:], in_=earlier[:], compare_op=ALU.is_gt, fill=0.0,
                               base=0, pattern=[[-1, P]], channel_multiplier=1).then_inc(const_made, 1)
            pool.affine_select(out=later[:], in_=later[:], compare_op=ALU.is_gt, fill=0.0,
                               base=0, pattern=[[1, P]], channel_multiplier=-1).then_inc(const_made, 1)
            pool.affine_select(out=causal[:, P:2 * P], in_=causal[:, P:2 * P], compare_op=ALU.is_ge,
                               fill=MASKED, base=0, pattern=[[-1, P]],
                               channel_multiplier=1).then_inc(const_made, 1)
            pool.wait_ge(const_made, 13)

            def rsqrt(src, dst, eps, summed, rooted, count):
                pool.tensor_tensor(dst, src, eps, ALU.add).then_inc(summed, 1)
                pool.wait_ge(summed, count)
                pool.tensor_tensor(dst, dst, half[:, 0:dst.shape[1]], ALU.pow).then_inc(rooted, 1)

            def per_head(stat, width):
                return stat[:, :].unsqueeze(2).to_broadcast([P, stat.shape[1], width])

            def kv_batch(b):
                pool.wait_ge(k_squared, b + 1)
                rsqrt(k_ss[:], k_rs[:], eps_head[:], k_summed, k_rooted, b + 1)
                pool.wait_ge(k_rooted, b + 1)
                pool.tensor_tensor(k_row[:], k_row[:], per_head(k_rs, HD), ALU.mult).then_inc(k_normed, 1)

            with pool.Fori(0, NB) as b:
                kv_batch(b)

            def x_norm_stat(b):
                pool.wait_ge(x_mean, b + 1)
                rsqrt(mv[:, 1:2], rstd[:], eps_ln[:], x_eps, x_rstd, b + 1)

            def k_low(b):
                pool.wait_ge(kT_hi_done, b + 1)
                pool.tensor_tensor(kT_lo[:], k_raw[:], kT_hi[:].bitcast(fp32),
                                   ALU.subtract).then_inc(kT_lo_done, 1)

            def v_low(b):
                pool.wait_ge(v_hi_done, b + 1)
                pool.tensor_tensor(v_lo[:], v_raw[:], v_hi[:].bitcast(fp32),
                                   ALU.subtract).then_inc(v_lo_done, 1)

            def q_norm(t):
                pool.wait_ge(q_squared, t + 1)
                rsqrt(q_ss[:], q_rs[:], eps_head[:], q_summed, q_rooted, t + 1)
                pool.wait_ge(q_rooted, t + 1)
                wait(pool, q_turned, t)
                pool.tensor_tensor(q_nrm[:], q_row[:], per_head(q_rs, HD), ALU.mult).then_inc(q_normed, 1)

            def p_norm(t):
                pool.wait_ge(p_inverted, t + 1)
                pool.tensor_tensor(p_row[:], p_row[:], per_head(p_inv, S), ALU.mult).then_inc(p_normed, 1)

            def out_stat(b):
                pool.wait_ge(x1_mean, b + 1)
                rsqrt(mv1[:, 1:2], rstd1[:], eps_ln[:], x1_eps, x1_rstd, b + 1)

            def base_rows(b):
                pool.wait_ge(h_made, b + 1)
                pool.tensor_tensor(x1[:], x1[:], h_row[:], ALU.add).then_inc(base_made, 1)

            x_norm_stat(0)
            pool.wait_ge(w_lo, 2 * NB)
            q_norm(0)
            keys_over(pool)
            k_low(0)

            def attend(b, first, last):
                for i in range(NQUAD):
                    t = NQUAD * b + i
                    if i == 0 and not last:
                        x_norm_stat(b + 1)
                    if not (last and i == NQUAD - 1):
                        q_norm(t + 1)
                    p_norm(t)
                    if i == 0:
                        v_low(b)
                    if i == 1 and not first:
                        out_stat(b - 1)
                    if i == 2 and not first:
                        base_rows(b - 1)
                    if i == NQUAD - 1 and not last:
                        k_low(b + 1)

            attend(0, True, False)
            with pool.Fori(1, NB - 1) as b:
                attend(b, False, False)
            attend(NB - 1, False, True)
            out_stat(NB - 1)
            base_rows(NB - 1)

            def split_low(n):
                pool.wait_ge(piece_hi, n + 1)
                pool.tensor_tensor(wp_lo[n % NSLOT][:, 0:2, :], raw[n % NRAW][:, 0:2, :],
                                   wp_hi[n % NSLOT][:, 0:2, :].bitcast(fp32),
                                   ALU.subtract).then_inc(piece_lo_pool, 1)

            for n in range(NSLOT):
                split_low(n)
            pool.wait_ge(idx_made, 2 * NJ)
            layer1_over(pool)
            for j in range(NJ):
                pool.indirect_dma_start(h_sel[j][:], None, h_store,
                                        bass.IndirectOffsetOnAxis(ap=row_idx[j][:, 0:1], axis=0)
                                        ).then_inc(gathered_h[j], 16)
            for j in range(NJ):
                pool.indirect_dma_start(rope[j][:], None, rope_table,
                                        bass.IndirectOffsetOnAxis(ap=pos_idx[j][:, 0:1], axis=0)
                                        ).then_inc(gathered_rope[j], 16)
            for j in range(NJ):
                pool.indirect_dma_start(base[j][:], None, out_rows,
                                        bass.IndirectOffsetOnAxis(ap=row_idx[j][:, 0:1], axis=0)
                                        ).then_inc(gathered_base[j], 16)

            def row_rsqrt(i):
                pool.wait_ge(f_squared, i + 1)
                pool.tensor_scalar(f_ms[:, i:i + 1], f_ss[:, i:i + 1], 1.0 / D, EPS_RMS,
                                   ALU.mult, ALU.add).then_inc(f_meaned, 1)
                pool.wait_ge(f_meaned, i + 1)
                pool.tensor_tensor(f_rs[:, i:i + 1], f_ms[:, i:i + 1], half[:, 0:1],
                                   ALU.pow).then_inc(f_rooted, 1)

            for j in range(NJ):
                row_rsqrt(j)

            def by_cosine(r, k):
                j = r % NJ
                pool.wait_ge(f_biased, r + 1)
                pool.wait_ge(gathered_rope[j], 16)
                wait(pool, f_roped, k)
                pool.tensor_tensor(by_cos[:].rearrange("p (h d) -> p h d", h=QUAD),
                                   proj[r % 2][:].rearrange("p (h d) -> p h d", h=QUAD),
                                   rope[j][:, 0:HD].unsqueeze(1).to_broadcast([P, QUAD, HD]),
                                   ALU.mult).then_inc(cos_done, 1)

            for r in range(NJ * FK):
                by_cosine(r, r)
                if r % NJ == NJ - 1:
                    split_low(NSLOT + r // NJ)
            for r in range(NJ * FK, 2 * NJ * FK):
                pool.wait_ge(fv_hi_done, r - NJ * FK + 1)
                c = (r - NJ * FK) // NJ
                pool.tensor_tensor(fv_lo[:, r % NJ, c * W:(c + 1) * W], proj[r % 2][:],
                                   fv_hi[:, r % NJ, c * W:(c + 1) * W].bitcast(fp32),
                                   ALU.subtract).then_inc(fv_lo_done, 1)
                if r % NJ == NJ - 1:
                    split_low(NSLOT + r // NJ)
            for j in range(NJ):
                by_cosine(2 * NJ * FK + j, NJ * FK + j)
            split_low(P_WQ0 + NSLOT)
            done = P_WQ0 + NSLOT + 1
            for n in range(FQ):
                if n < FQ - 1:
                    for j in range(NJ):
                        by_cosine(2 * NJ * FK + NJ * (n + 1) + j, NJ * FK + NJ * (n + 1) + j)
                for i in range(3):
                    tile = 3 * n + i
                    heads = QUAD if i == 0 else QUAD // 2
                    col = 0 if i == 0 else QUAD // 2 * i + 2
                    pool.wait_ge(f_inverted, tile + 1)
                    pool.tensor_tensor(
                        fs[i][:].rearrange("p (h t) -> p h t", h=heads),
                        fs[i][:].rearrange("p (h t) -> p h t", h=heads),
                        f_inv[:, col:col + heads].unsqueeze(2).to_broadcast([P, heads, W // heads]),
                        ALU.mult).then_inc(f_normed, 1)
                for _ in range(2 if 0 < n < FQ - 1 else 1):
                    split_low(done)
                    done += 1
            while done < P_MLP + 4:
                split_low(done)
                done += 1
            for j in range(NJ):
                row_rsqrt(NJ + j)
            for n in range(done, NP):
                split_low(n)
            for j in range(NJ):
                pool.wait_ge(final_made, j + 1)
                pool.indirect_dma_start(out_rows, bass.IndirectOffsetOnAxis(ap=row_idx[j][:, 0:1], axis=0),
                                        final[j][:], None).then_inc(out_stored[j], 16)
            for j in range(NJ):
                pool.wait_ge(out_stored[j], 16)

        @block.scalar
        def _(act):
            def copy(dst, src):
                return act.activation(dst, src, ACT.Copy)

            def turn_c(b, par):
                act.wait_ge(c_turned, b + 1)
                wait(act, v_projected, b - 1)
                copy(cT_hi[par][:].rearrange("p c t -> p (c t)"), b_c[:]).then_inc(c_hi, 1)

            turn_c(0, 0)
            for hi, rw, loaded in ((wk_hi, raw[0], wk_loaded), (wv_hi, raw[1], wv_loaded)):
                for c in range(DC):
                    act.wait_ge(loaded[c * len(loaded) // DC], 16)
                    copy(hi[:, c, :], rw[:, c, :]).then_inc(kv_w_hi, 1)
            act.wait_ge(const_loaded, 48)
            act.wait_ge(kw_scaled, 1)

            def weigh_k(b):
                act.wait_ge(k_turned, b + 1)
                wait(act, k_stored, 16 * b)
                act.activation(k_out[:], b_kT[:], ACT.Copy, scale=kw[:, 0:1]).then_inc(k_weighted, 1)

            def kv_batch(b, par, first, last):
                if not last:
                    turn_c(b + 1, 1 - par)
                act.wait_ge(k_biased, b + 1)
                wait(act, k_rooted, b)
                for h in range(NKV):
                    sq = act.activation(k_sq[:, h, :], k_row[:, h, :], ACT.Square, accum_out=k_ss[:, h:h + 1])
                sq.then_inc(k_squared, 1)
                if not first:
                    weigh_k(b - 1)
                act.wait_ge(wq_loaded, 16 * (b + 1))
                copy(wq_hi[:, :, bass.ds(b * HD, HD)], wq_raw[:]).then_inc(w_hi, 1)
                act.wait_ge(wo_loaded, 16 * (b + 1))
                copy(wo_hi[:, bass.ds(b, 1), :], wo_raw[:].unsqueeze(1)).then_inc(w_hi, 1)

            kv_batch(0, 0, True, False)
            with act.Fori(0, NB // 2 - 1) as g:
                kv_batch(2 * g + 1, 1, False, False)
                kv_batch(2 * g + 2, 0, False, False)
            kv_batch(NB - 1, 1, False, True)
            weigh_k(NB - 1)

            def x_high(b):
                act.wait_ge(x_turned, b + 1)
                copy(xT_hi[:].rearrange("p c t -> p (c t)"), b_xT[:]).then_inc(xT_hi_done, 1)

            def k_high(b):
                act.wait_ge(k_loaded, 16 * (b + 1))
                wait(act, scored, NQUAD * b)
                copy(kT_hi[:], k_raw[:]).then_inc(kT_hi_done, 1)

            def v_high(b):
                act.wait_ge(v_loaded, 16 * (b + 1))
                wait(act, mixed, NQUAD * b)
                copy(v_hi[:], v_raw[:]).then_inc(v_hi_done, 1)

            def q_high(t):
                act.wait_ge(q_turned, t + 1)
                wait(act, scored, t)
                act.activation(qT_hi[:], b_qT[:], ACT.Copy, scale=qw[:, 0:1]).then_inc(qT_hi_done, 1)

            def p_high(t):
                act.wait_ge(p_turned, t + 1)
                wait(act, mixed, t)
                copy(pT_hi[:], b_pT[:]).then_inc(pT_hi_done, 1)

            def o_high(t):
                act.wait_ge(mixed, t + 1)
                wait(act, y_added, t)
                copy(oT_hi[:], b_o[:]).then_inc(oT_hi_done, 1)

            def squares(t):
                act.wait_ge(q_biased, t + 1)
                wait(act, q_rooted, t)
                for h in range(QUAD):
                    sq = act.activation(sq_junk[:, h, :], q_row[:, h, :], ACT.Square, accum_out=q_ss[:, h:h + 1])
                sq.then_inc(q_squared, 1)

            def exps(t):
                act.wait_ge(s_maxed, t + 1)
                wait(act, p_turned, t)
                for h in range(QUAD):
                    e = act.activation(p_row[:, h, :], s_row[:, h, :], ACT.Exp,
                                       bias=neg_max[:, h:h + 1], accum_out=p_sum[:, h:h + 1])
                e.then_inc(p_exped, 1)

            x_high(0)
            keys_over(act)
            squares(0)
            k_high(0)

            def attend(b, first, last):
                for i in range(NQUAD):
                    t = NQUAD * b + i
                    q_high(t)
                    if i == 2 and not last:
                        x_high(b + 1)
                    if not (last and i == NQUAD - 1):
                        squares(t + 1)
                    if not (first and i == 0):
                        p_high(t - 1)
                    exps(t)
                    if not (first and i == 0):
                        o_high(t - 1)
                    if i == 0:
                        v_high(b)
                    if i == NQUAD - 1 and not last:
                        k_high(b + 1)

            attend(0, True, False)
            with act.Fori(1, NB - 1) as b:
                attend(b, False, False)
            attend(NB - 1, False, True)
            p_high(STEPS - 1)

            def split_high(n):
                act.wait_ge(raw_loaded[n % NRAW], 16 * (n // NRAW + 1))
                if n >= NSLOT:
                    act.wait_ge(*used_up[n - NSLOT])
                copy(wp_hi[n % NSLOT][:], raw[n % NRAW][:]).then_inc(piece_hi, 1)

            act.wait_ge(q_projected, STEPS)
            split_high(0)
            o_high(STEPS - 1)
            for n in range(1, NSLOT):
                split_high(n)
            layer1_over(act)

            def row_squares(i, src):
                act.activation(hn_row[i % NJ][:], src, ACT.Square, accum_out=f_ss[:, i:i + 1]).then_inc(f_squared, 1)

            for j in range(NJ):
                act.wait_ge(gathered_h[j], 16)
                row_squares(j, h_sel[j][:])

            def h_high(i):
                act.wait_ge(h_turned, i + 1)
                copy(hT_hi[:, i % NJ].rearrange("p c t -> p (c t)"), (f_T, f_T2)[i % NJ][:]
                     ).then_inc(hT_hi_done, 1)

            for j in range(NJ):
                h_high(j)

            def fk_high(i):
                kp, j = i // NJ, i % NJ
                act.wait_ge(fk_turned, i + 1)
                copy(fkT_hi[:, kp * QUAD:(kp + 1) * QUAD, j * P:(j + 1) * P],
                     (f_T, f_T2)[j][:].rearrange("p (h t) -> p h t", h=QUAD)).then_inc(fk_hi_done, 1)

            split_high(NSLOT)
            fk_high(0)
            fk_high(1)
            split_high(NSLOT + 1)
            for i in range(NJ * FK):
                r = NJ * FK + i
                act.wait_ge(f_biased, r + 1)
                c = i // NJ
                copy(fv_hi[:, i % NJ, c * W:(c + 1) * W], proj[r % 2][:]).then_inc(fv_hi_done, 1)
                if i < 2:
                    fk_high(2 + i)
                if i % NJ == NJ - 1:
                    split_high(NSLOT + 2 + i // NJ)
            split_high(P_WQ0 + NSLOT)
            done = P_WQ0 + NSLOT + 1
            for n in range(FQ):
                for j in range(NJ):
                    act.wait_ge(fq_turned, NJ * n + j + 1)
                    wait(act, f_scored, 3 * n)
                    copy(fqT_hi[:, j].rearrange("p h t -> p (h t)"), (f_T, f_T2)[j][:]
                         ).then_inc(fq_hi_done, 1)
                for i in range(3):
                    tile = 3 * n + i
                    heads = QUAD if i == 0 else QUAD // 2
                    width = W // heads
                    col = 0 if i == 0 else QUAD // 2 * i + 2
                    act.wait_ge(f_maxed, tile + 1)
                    for h in range(heads):
                        e = act.activation(fs[i][:, h * width:(h + 1) * width],
                                           fs[i][:, h * width:(h + 1) * width], ACT.Exp,
                                           bias=f_max[:, col + h:col + h + 1],
                                           accum_out=f_sum[:, col + h:col + h + 1])
                    e.then_inc(f_exped, 1)
                for _ in range(2 if 0 < n < FQ - 1 else 1):
                    split_high(done)
                    done += 1
                act.wait_ge(fp_turned, 3 * n + 1)
                wait(act, f_mixed, 2 * n)
                copy(fp0_hi[:, 0:2, :].rearrange("p h t -> p (h t)"), f_T[:]).then_inc(fp_hi_done, 1)
                act.wait_ge(fp_turned, 3 * n + 2)
                copy(fp0_hi[:, 2:4, :].rearrange("p h t -> p (h t)"), f_T2[:]).then_inc(fp_hi_done, 1)
                act.wait_ge(fp_turned, 3 * n + 3)
                copy(fp1_hi[:].rearrange("p h t -> p (h t)"), f_S[:]).then_inc(fp_hi_done, 1)
                for g in range(2):
                    act.wait_ge(f_mixed, 2 * n + g + 1)
                    wait(act, attn_done, NJ * n)
                    copy(foT_hi[:, 2 * g:2 * g + 2, :].rearrange("p h t -> p (h t)"),
                         (f_O, f_T)[g][:]).then_inc(fo_hi_done, 1)
            while done < P_MLP + 4:
                split_high(done)
                done += 1
            for j in range(NJ):
                act.wait_ge(attn_done, NJ * (FQ - 1) + j + 1)
                copy(attn_row[j][:], f_W[j][:]).then_inc(attn_copied, 1)
            for j in range(NJ):
                act.wait_ge(x2_made, j + 1)
                row_squares(NJ + j, x2_row[j][:])
            for j in range(NJ):
                h_high(NJ + j)
            for j in range(NJ):
                act.wait_ge(g_dotted, j + 1)
            act.activation(g_exp[:], g_dot[:], ACT.Exp, scale=-1.0).then_inc(g_exped, 1)
            for m in range(FI):
                for j in range(NJ):
                    act.wait_ge(gated, NJ * m + j + 1)
                    wait(act, act_done, NJ * (m - 1) + j + 1)
                    act.activation(tanh_row[j][:], f_proj[j][:], ACT.Tanh, scale=0.5).then_inc(tanh_done, 1)
                split_more = [n for n in range(done, min(done + 3, NP))]
                for n in split_more:
                    if n < p_down(m) + 3 or m == FI - 1:
                        split_high(n)
                        done += 1
                for j in range(NJ):
                    act.wait_ge(act_turned, NJ * m + j + 1)
                    wait(act, mlp_done, NJ * m)
                    copy(fqT_hi[:, j].rearrange("p h t -> p (h t)"), (f_T, f_T2)[j][:]
                         ).then_inc(aT_hi_done, 1)
            assert done == NP

        @block.vector
        def _(dve):
            def low(dst, src, hi):
                return dve.tensor_tensor(dst, src, hi.bitcast(fp32), ALU.subtract)

            def turn_c(b, par):
                dve.wait_ge(c_hi, b + 1)
                low(cT_lo[par][:].rearrange("p c t -> p (c t)"), b_c[:],
                    cT_hi[par][:].rearrange("p c t -> p (c t)")).then_inc(c_lo, 1)

            turn_c(0, 0)
            for i, (hi, lo, rw) in enumerate(((wk_hi, wk_lo, raw[0]), (wv_hi, wv_lo, raw[1]))):
                for c in range(DC):
                    dve.wait_ge(kv_w_hi, DC * i + c + 1)
                    low(lo[:, c, :], rw[:, c, :], hi[:, c, :]).then_inc(kv_w_lo, 1)
            dve.wait_ge(const_loaded, 48)
            dve.tensor_scalar(kw[:], kw[:], 1.0 / SCALE, None, ALU.mult).then_inc(kw_scaled, 1)
            dve.wait_ge(kv_bias_loaded, 32)

            def kv_batch(b, par, last):
                if not last:
                    turn_c(b + 1, 1 - par)
                dve.wait_ge(k_projected, b + 1)
                wait(dve, k_turned, b)
                dve.tensor_tensor(k_row[:].rearrange("p h d -> p (h d)"), b_k[:], bk_row[:],
                                  ALU.add).then_inc(k_biased, 1)
                dve.wait_ge(v_projected, b + 1)
                wait(dve, v_stored, 16 * b)
                dve.tensor_tensor(v_out[:], b_v[:], bv_row[:], ALU.add).then_inc(v_biased, 1)
                dve.wait_ge(w_hi, 2 * b + 1)
                low(wq_lo[:, :, bass.ds(b * HD, HD)], wq_raw[:],
                    wq_hi[:, :, bass.ds(b * HD, HD)]).then_inc(w_lo, 1)
                dve.wait_ge(w_hi, 2 * b + 2)
                low(wo_lo[:, bass.ds(b, 1), :], wo_raw[:].unsqueeze(1),
                    wo_hi[:, bass.ds(b, 1), :]).then_inc(w_lo, 1)

            kv_batch(0, 0, False)
            with dve.Fori(0, NB // 2 - 1) as g:
                kv_batch(2 * g + 1, 1, False)
                kv_batch(2 * g + 2, 0, False)
            kv_batch(NB - 1, 1, True)

            def x_statistics(b):
                dve.wait_ge(x_loaded, 16 * (b + 1))
                wait(dve, x_rstd, b)
                dve.bn_stats(bn[:], xr[:]).then_inc(x_stats, 1)

            def x_moments(b):
                dve.bn_aggr(mv[:], bn[:]).then_inc(x_mean, 1)

            def x_norm(b):
                dve.wait_ge(x_rstd, b + 1)
                wait(dve, x_turned, b)
                dve.tensor_scalar(xn[:], xr[:], mv[:, 0:1], rstd[:, 0:1],
                                  ALU.subtract, ALU.mult).then_inc(x_normed, 1)

            def x_low(b):
                dve.wait_ge(xT_hi_done, b + 1)
                low(xT_lo[:].rearrange("p c t -> p (c t)"), b_xT[:],
                    xT_hi[:].rearrange("p c t -> p (c t)")).then_inc(xT_lo_done, 1)

            def q_bias(t, quad):
                dve.wait_ge(q_projected, t + 1)
                wait(dve, q_normed, t)
                dve.tensor_tensor(q_row[:].rearrange("p h d -> p (h d)"), b_q[:],
                                  bq_row[:, quad * W:(quad + 1) * W], ALU.add).then_inc(q_biased, 1)

            def q_low(t):
                dve.wait_ge(qT_hi_done, t + 1)
                dve.scalar_tensor_tensor(qT_lo[:], b_qT[:], qw[:, 0:1], qT_hi[:].bitcast(fp32),
                                         ALU.mult, ALU.subtract).then_inc(qT_lo_done, 1)

            def s_mask(t):
                dve.wait_ge(scored, t + 1)
                wait(dve, p_exped, t)
                dve.tensor_tensor(s_row[:], b_s[:].rearrange("p (h t) -> p h t", h=QUAD),
                                  mask[:].unsqueeze(1).to_broadcast([P, QUAD, S]),
                                  ALU.add).then_inc(s_masked, 1)

            def s_max(t):
                dve.wait_ge(s_masked, t + 1)
                dve.tensor_reduce(neg_max[:], s_row[:], AX.X, ALU.max, negate=True).then_inc(s_maxed, 1)

            def p_low(t):
                dve.wait_ge(pT_hi_done, t + 1)
                low(pT_lo[:], b_pT[:], pT_hi[:]).then_inc(pT_lo_done, 1)

            def p_invert(t):
                dve.wait_ge(p_exped, t + 1)
                wait(dve, p_normed, t)
                dve.reciprocal(p_inv[:], p_sum[:]).then_inc(p_inverted, 1)

            def o_low(t):
                dve.wait_ge(oT_hi_done, t + 1)
                low(oT_lo[:], b_o[:], oT_hi[:]).then_inc(oT_lo_done, 1)

            def add_residual(b):
                dve.wait_ge(y_added, NQUAD * (b + 1))
                dve.wait_ge(res_loaded, 16 * (b + 1))
                wait(dve, base_stored, 16 * b)
                dve.tensor_tensor(x1[:], b_y[:], x_res[:], ALU.add).then_inc(x1_made, 1)
                dve.wait_ge(x1_made, b + 1)
                dve.bn_stats(bn1[:], x1[:]).then_inc(x1_stats, 1)

            def x1_moments(b):
                dve.bn_aggr(mv1[:], bn1[:]).then_inc(x1_mean, 1)

            def norm_out(b):
                dve.wait_ge(x1_rstd, b + 1)
                wait(dve, h_stored, 16 * b)
                dve.tensor_scalar(h_row[:], x1[:], mv1[:, 0:1], rstd1[:, 0:1],
                                  ALU.subtract, ALU.mult).then_inc(h_made, 1)
                dve.wait_ge(h_made, b + 1)
                dve.tensor_tensor_reduce(dot_junk[:], h_row[:], wr_row[:], 1.0, 0.0, ALU.mult,
                                         ALU.add, accum_out=score[:, 0:1]).then_inc(scored_row, 1)
                dve.wait_ge(scored_row, b + 1)
                dve.tensor_copy(score_wide[:], score[:, 0:1].to_broadcast([P, S])).then_inc(score_spread, 1)

            def rank(b):
                dve.wait_ge(score_turned, b + 1)
                dve.tensor_scalar(rank_junk[:, 0, :], b_rank[:, 0:S], score[:, 0:1], 0.0, ALU.is_gt,
                                  ALU.add, accum_out=above[:, 0:1]).then_inc(counted_above, 1)
                dve.scalar_tensor_tensor(rank_junk[:, 1, :], b_rank[:, 0:S], score[:, 0:1], earlier[:],
                                         ALU.is_equal, ALU.mult,
                                         accum_out=tied[:, 0:1]).then_inc(counted_tied, 1)
                dve.wait_ge(counted_above, b + 1)
                dve.wait_ge(counted_tied, b + 1)
                dve.tensor_scalar(picked[:, bass.ds(b, 1)], above[:, 0:1], tied[:, 0:1], float(PICK),
                                  ALU.add, ALU.is_lt).then_inc(picks_made, 1)

            dve.wait_ge(const_made, 13)
            dve.wait_ge(w_lo, 2 * NB)
            dve.wait_ge(c_turned, NB)
            dve.wait_ge(v_projected, NB - 1)
            x_statistics(0)
            dve.wait_ge(x_stats, 1)
            x_moments(0)
            x_norm(0)
            x_low(0)
            dve.wait_ge(bq_loaded, 16)
            q_bias(0, 0)
            keys_over(dve)
            dve.wait_ge(rows_loaded, 32)

            def attend(b, first, last):
                for i in range(NQUAD):
                    t = NQUAD * b + i
                    if i == 0 and not last:
                        x_statistics(b + 1)
                        dve.wait_ge(x_stats, b + 2)
                    q_low(t)
                    if i == 0 and not last:
                        x_moments(b + 1)
                    if i == 1 and not last:
                        x_norm(b + 1)
                    if i == 2 and not last:
                        x_low(b + 1)
                    if not (last and i == NQUAD - 1):
                        q_bias(t + 1, (i + 1) % NQUAD)
                    s_mask(t)
                    s_max(t)
                    if not (first and i == 0):
                        p_low(t - 1)
                    if i == 1 and not first:
                        add_residual(b - 1)
                    if i == 2 and not first:
                        norm_out(b - 1)
                    if i == NQUAD - 1 and not first:
                        rank(b - 1)
                    if i == 1 and not first:
                        dve.wait_ge(x1_stats, b)
                    p_invert(t)
                    if i == 1 and not first:
                        x1_moments(b - 1)
                    if not (first and i == 0):
                        o_low(t - 1)

            attend(0, True, False)
            with dve.Fori(1, NB - 1) as b:
                attend(b, False, False)
            attend(NB - 1, False, True)
            p_low(STEPS - 1)

            def split_low(n):
                dve.wait_ge(piece_hi, n + 1)
                low(wp_lo[n % NSLOT][:, 2:4, :], raw[n % NRAW][:, 2:4, :],
                    wp_hi[n % NSLOT][:, 2:4, :]).then_inc(piece_lo_dve, 1)

            split_low(0)
            o_low(STEPS - 1)
            add_residual(NB - 1)
            dve.wait_ge(x1_stats, NB)
            x1_moments(NB - 1)
            norm_out(NB - 1)
            rank(NB - 1)

            layer1_over(dve)
            dve.wait_ge(place_found, 1)
            dve.tensor_tensor(onehot[:], b_y[:, 0:NB].unsqueeze(2).to_broadcast([P, NB, PICK]),
                              slots[:].unsqueeze(1).to_broadcast([P, NB, PICK]),
                              ALU.is_equal).then_inc(onehot_raw, 1)
            dve.wait_ge(onehot_raw, 1)
            dve.tensor_tensor(onehot[:], onehot[:], picked[:].unsqueeze(2).to_broadcast([P, NB, PICK]),
                              ALU.mult).then_inc(onehot_made, 1)
            dve.wait_ge(rows_found, 1)
            for j in range(NJ):
                dve.tensor_tensor(row_idx[j][:], b_q[:, j:j + 1], base_row[:, j:j + 1],
                                  ALU.add).then_inc(idx_made, 1)
                dve.tensor_copy(pos_idx[j][:], b_q[:, j:j + 1]).then_inc(idx_made, 1)
            for n in range(1, NSLOT):
                split_low(n)
            dve.wait_ge(f_rows_loaded, 48)

            def weigh(i, src, ln):
                dve.wait_ge(f_rooted, i + 1)
                dve.scalar_tensor_tensor(hn_row[i % NJ][:], src, f_rs[:, i:i + 1], ln,
                                         ALU.mult, ALU.mult).then_inc(hn_made, 1)

            for j in range(NJ):
                weigh(j, h_sel[j][:], ln1_row[:])

            def h_low(i):
                dve.wait_ge(hT_hi_done, i + 1)
                low(hT_lo[:, i % NJ].rearrange("p c t -> p (c t)"), (f_T, f_T2)[i % NJ][:],
                    hT_hi[:, i % NJ].rearrange("p c t -> p (c t)")).then_inc(hT_lo_done, 1)

            for j in range(NJ):
                h_low(j)
            for j in range(NJ):
                dve.tensor_tensor_reduce(x2_row[j][:], h_sel[j][:], wr2_row[:], 1.0, 0.0, ALU.mult,
                                         ALU.add, accum_out=g_dot[:, j:j + 1]).then_inc(g_dotted, 1)

            def bias(r, i):
                dve.wait_ge(f_projected, r + 1)
                dve.wait_ge(bias_loaded[i % 2], 16 * (i // 2 + 1))
                dve.tensor_tensor(proj[r % 2][:], f_proj[r % 2][:], bias_row[i % 2][:],
                                  ALU.add).then_inc(f_biased, 1)

            def rope_tile(r, k):
                j = r % NJ
                q = proj[r % 2][:].rearrange("p (h a d) -> p h a d", h=QUAD, a=2)
                s = by_sin[:].rearrange("p (h a d) -> p h a d", h=QUAD, a=2)
                dve.wait_ge(gathered_rope[j], 16)
                dve.wait_ge(f_biased, r + 1)
                wait(dve, f_roped, k)
                for a in range(2):
                    sin = rope[j][:, HD + a * (HD // 2):HD + (a + 1) * (HD // 2)]
                    last = dve.tensor_tensor(s[:, :, a, :], q[:, :, 1 - a, :],
                                             sin.unsqueeze(1).to_broadcast([P, QUAD, HD // 2]), ALU.mult)
                last.then_inc(sin_done, 1)
                dve.wait_ge(sin_done, k + 1)
                dve.wait_ge(cos_done, k + 1)
                if NJ <= k < NJ * (FK + 1):
                    dve.wait_ge(fk_turned, k - NJ + 1)
                elif k >= NJ * (FK + 1):
                    dve.wait_ge(fq_turned, k - NJ * (FK + 1) + 1)
                dve.tensor_tensor(turned[j][:], by_cos[:], by_sin[:], ALU.add).then_inc(f_roped, 1)

            def fk_low(i):
                kp, j = i // NJ, i % NJ
                dve.wait_ge(fk_hi_done, i + 1)
                low(fkT_lo[:, kp * QUAD:(kp + 1) * QUAD, j * P:(j + 1) * P],
                    (f_T, f_T2)[j][:].rearrange("p (h t) -> p h t", h=QUAD),
                    fkT_hi[:, kp * QUAD:(kp + 1) * QUAD, j * P:(j + 1) * P]).then_inc(fk_lo_done, 1)

            r = 0
            for kp in range(FK):
                for j in range(NJ):
                    bias(r, kp)
                    rope_tile(r, r)
                    if kp > 0:
                        fk_low(r - NJ)
                    r += 1
                split_low(NSLOT + kp)
            for vp in range(FK):
                for j in range(NJ):
                    if r >= NJ * FK + 2:
                        dve.wait_ge(fv_hi_done, r - NJ * FK - 1)
                        dve.wait_ge(fv_lo_done, r - NJ * FK - 1)
                    bias(r, FK + vp)
                    if vp == 0:
                        fk_low(NJ * (FK - 1) + j)
                    r += 1
                split_low(NSLOT + FK + vp)
            for j in range(NJ):
                dve.wait_ge(fv_lo_done, NJ * (FK - 1) + j + 1)
                bias(r, 2 * FK)
                rope_tile(r, NJ * FK + j)
                r += 1
            split_low(P_WQ0 + NSLOT)
            done = P_WQ0 + NSLOT + 1
            for n in range(FQ):
                for j in range(NJ):
                    dve.wait_ge(fq_hi_done, NJ * n + j + 1)
                    low(fqT_lo[:, j].rearrange("p h t -> p (h t)"), (f_T, f_T2)[j][:],
                        fqT_hi[:, j].rearrange("p h t -> p (h t)")).then_inc(fq_lo_done, 1)
                for i in range(3):
                    tile = 3 * n + i
                    heads = QUAD if i == 0 else QUAD // 2
                    width = W // heads
                    col = 0 if i == 0 else QUAD // 2 * i + 2
                    bank = (f_S, f_T, f_T2)[i]
                    dve.wait_ge(f_scored, tile + 1)
                    wait(dve, fp_turned, 3 * n)
                    dve.scalar_tensor_tensor(
                        fs[i][:].rearrange("p (h t) -> p h t", h=heads),
                        bank[:].rearrange("p (h t) -> p h t", h=heads), SCALE,
                        causal[:, 2 * P - width:2 * P].unsqueeze(1).to_broadcast([P, heads, width]),
                        ALU.mult, ALU.add).then_inc(f_masked, 1)
                    dve.wait_ge(f_masked, tile + 1)
                    dve.tensor_reduce(f_max[:, col:col + heads],
                                      fs[i][:].rearrange("p (h t) -> p h t", h=heads),
                                      AX.X, ALU.max, negate=True).then_inc(f_maxed, 1)
                if n < FQ - 1:
                    for j in range(NJ):
                        bias(r, 2 * FK + n + 1)
                        rope_tile(r, NJ * FK + NJ * (n + 1) + j)
                        r += 1
                for i in range(3):
                    tile = 3 * n + i
                    heads = QUAD if i == 0 else QUAD // 2
                    col = 0 if i == 0 else QUAD // 2 * i + 2
                    dve.wait_ge(f_exped, tile + 1)
                    dve.reciprocal(f_inv[:, col:col + heads],
                                   f_sum[:, col:col + heads]).then_inc(f_inverted, 1)
                for _ in range(2 if 0 < n < FQ - 1 else 1):
                    split_low(done)
                    done += 1
                for i, (hi, lo, bank) in enumerate((
                        (fp0_hi[:, 0:2, :], fp0_lo[:, 0:2, :], f_T),
                        (fp0_hi[:, 2:4, :], fp0_lo[:, 2:4, :], f_T2),
                        (fp1_hi[:], fp1_lo[:], f_S))):
                    dve.wait_ge(fp_hi_done, 3 * n + i + 1)
                    low(lo.rearrange("p h t -> p (h t)"), bank[:],
                        hi.rearrange("p h t -> p (h t)")).then_inc(fp_lo_done, 1)
                for g in range(2):
                    dve.wait_ge(fo_hi_done, 2 * n + g + 1)
                    low(foT_lo[:, 2 * g:2 * g + 2, :].rearrange("p h t -> p (h t)"), (f_O, f_T)[g][:],
                        foT_hi[:, 2 * g:2 * g + 2, :].rearrange("p h t -> p (h t)")
                        ).then_inc(fo_lo_done, 1)
            while done < P_MLP + 4:
                split_low(done)
                done += 1
            for j in range(NJ):
                dve.wait_ge(attn_copied, j + 1)
                dve.tensor_tensor(x2_row[j][:], attn_row[j][:], h_sel[j][:], ALU.add).then_inc(x2_made, 1)
            for j in range(NJ):
                weigh(NJ + j, x2_row[j][:], ln2_row[:])
            for j in range(NJ):
                h_low(NJ + j)
            dve.wait_ge(g_exped, 1)
            dve.tensor_scalar(g_one[:], g_exp[:], 1.0, None, ALU.add).then_inc(g_plus, 1)
            dve.wait_ge(g_plus, 1)
            dve.reciprocal(gate[:], g_one[:]).then_inc(g_made, 1)
            for m in range(FI):
                for j in range(NJ):
                    dve.wait_ge(tanh_done, NJ * m + j + 1)
                    wait(dve, act_turned, NJ * (m - 1) + j + 1)
                    dve.scalar_tensor_tensor(act_row[j][:], tanh_row[j][:], 1.0, f_proj[j][:],
                                             ALU.add, ALU.mult).then_inc(silu_done, 1)
                    dve.wait_ge(silu_done, NJ * m + j + 1)
                    dve.wait_ge(upped, NJ * m + j + 1)
                    dve.scalar_tensor_tensor(act_row[j][:], act_row[j][:], 0.5, (f_S, f_O)[j][:],
                                             ALU.mult, ALU.mult).then_inc(act_done, 1)
                split_more = [n for n in range(done, min(done + 3, NP))]
                for n in split_more:
                    if n < p_down(m) + 3 or m == FI - 1:
                        split_low(n)
                        done += 1
                for j in range(NJ):
                    dve.wait_ge(aT_hi_done, NJ * m + j + 1)
                    low(fqT_lo[:, j].rearrange("p h t -> p (h t)"), (f_T, f_T2)[j][:],
                        fqT_hi[:, j].rearrange("p h t -> p (h t)")).then_inc(aT_lo_done, 1)
            for j in range(NJ):
                dve.wait_ge(mlp_done, NJ * (FI - 1) + j + 1)
                dve.tensor_tensor(attn_row[j][:], attn_row[j][:], f_W[j][:], ALU.add).then_inc(delta_made, 1)
                dve.wait_ge(delta_made, j + 1)
                dve.wait_ge(g_made, 1)
                dve.wait_ge(gathered_base[j], 16)
                dve.scalar_tensor_tensor(final[j][:], attn_row[j][:], gate[:, j:j + 1], base[j][:],
                                         ALU.mult, ALU.add).then_inc(final_made, 1)

        @block.tensor
        def _(pe):
            def product(dst, left, right, start, stop):
                pe.matmul(dst, left[0], right[0], start=start, stop=False)
                pe.matmul(dst, left[0], right[1], start=False, stop=False)
                return pe.matmul(dst, left[1], right[0], start=False, stop=stop)

            def turn(dst, src, n=4):
                for i in range(n):
                    last = pe.transpose(dst[:, i * P:(i + 1) * P], src[:, i * P:(i + 1) * P], ident[:])
                return last

            pe.wait_ge(const_made, 13)

            def turn_c(b, par, nth):
                pe.wait_ge(cx_loaded[par], 16 * nth)
                wait(pe, c_lo, b)
                turn(b_c, cx[par]).then_inc(c_turned, 1)

            def turn_k(b):
                pe.wait_ge(k_normed, b + 1)
                wait(pe, k_weighted, b)
                turn(b_kT, k_row[:].rearrange("p h d -> p (h d)")).then_inc(k_turned, 1)

            def kv_project(bank, par, w_hi_, w_lo_, split_at=None):
                for c in range(DC):
                    if split_at is not None:
                        pe.wait_ge(kv_w_lo, split_at + c + 1)
                    last = product(bank[:], (cT_hi[par][:, c, :], cT_lo[par][:, c, :]),
                                   (w_hi_[:, c, :], w_lo_[:, c, :]), c == 0, c == DC - 1)
                return last

            def kv_batch(b, par, next_nth, first=False, last=False):
                if not last:
                    turn_c(b + 1, 1 - par, next_nth)
                pe.wait_ge(c_lo, b + 1)
                wait(pe, k_biased, b)
                kv_project(b_k, par, wk_hi, wk_lo, 0 if first else None).then_inc(k_projected, 1)
                if not first:
                    turn_k(b - 1)
                wait(pe, v_biased, b)
                kv_project(b_v, par, wv_hi, wv_lo, DC if first else None).then_inc(v_projected, 1)

            turn_c(0, 0, 1)
            kv_batch(0, 0, 1, first=True)
            with pe.Fori(0, NB // 2 - 1) as g:
                kv_batch(2 * g + 1, 1, g + 2)
                kv_batch(2 * g + 2, 0, g + 2)
            kv_batch(NB - 1, 1, None, last=True)


            def turn_x(b):
                pe.wait_ge(x_normed, b + 1)
                wait(pe, xT_lo_done, b)
                turn(b_xT, xn).then_inc(x_turned, 1)

            def project_q(t, b, quad):
                pe.wait_ge(xT_lo_done, b + 1)
                wait(pe, q_biased, t)
                for c in range(DC):
                    last = product(b_q[:], (xT_hi[:, c, :], xT_lo[:, c, :]),
                                   (wq_hi[:, c, quad * W:(quad + 1) * W], wq_lo[:, c, quad * W:(quad + 1) * W]),
                                   c == 0, c == DC - 1)
                last.then_inc(q_projected, 1)

            def turn_q(t):
                pe.wait_ge(q_normed, t + 1)
                wait(pe, qT_lo_done, t)
                turn(b_qT, q_nrm[:].rearrange("p h d -> p (h d)")).then_inc(q_turned, 1)

            def score_quad(t, b, quad):
                pe.wait_ge(qT_lo_done, t + 1)
                if quad == 0:
                    pe.wait_ge(kT_lo_done, b + 1)
                wait(pe, s_masked, t)
                ks = slice(quad * S, (quad + 1) * S)
                for h in range(QUAD):
                    hs = slice(h * P, (h + 1) * P)
                    last = product(b_s[:, hs], (qT_hi[:, hs], qT_lo[:, hs]),
                                   (kT_hi[:, ks], kT_lo[:, ks]), True, True)
                last.then_inc(scored, 1)

            def turn_p(t):
                pe.wait_ge(p_normed, t + 1)
                wait(pe, pT_lo_done, t)
                turn(b_pT, p_row[:].rearrange("p h t -> p (h t)")).then_inc(p_turned, 1)

            def mix(t, b, quad):
                pe.wait_ge(pT_lo_done, t + 1)
                if quad == 0:
                    pe.wait_ge(v_lo_done, b + 1)
                wait(pe, oT_lo_done, t)
                vs = slice(quad * HD, (quad + 1) * HD)
                product(b_o[:], (v_hi[:, vs], v_lo[:, vs]), (pT_hi[:], pT_lo[:]), True, True
                        ).then_inc(mixed, 1)

            def add_y(t, b, quad):
                pe.wait_ge(oT_lo_done, t + 1)
                if quad == 0:
                    wait(pe, x1_made, b)
                for h in range(QUAD):
                    hs = slice(h * P, (h + 1) * P)
                    head = quad * QUAD + h
                    last = product(b_y[:], (oT_hi[:, hs], oT_lo[:, hs]),
                                   (wo_hi[:, head, :], wo_lo[:, head, :]),
                                   quad == 0 and h == 0, quad == NQUAD - 1 and h == QUAD - 1)
                last.then_inc(y_added, 1)

            def spread_scores(b):
                pe.wait_ge(score_spread, b + 1)
                wait(pe, picks_made, b)
                pe.transpose(b_rank[:, 0:S], score_wide[:], ident[:]).then_inc(score_turned, 1)

            turn_x(0)
            turn_k(NB - 1)
            pe.wait_ge(w_lo, 2 * NB)
            pe.wait_ge(k_biased, NB)
            project_q(0, 0, 0)
            keys_over(pe)

            def attend(b, first, last):
                for i in range(NQUAD):
                    t = NQUAD * b + i
                    turn_q(t)
                    if not (last and i == NQUAD - 1):
                        project_q(t + 1, b if i < NQUAD - 1 else b + 1, (i + 1) % NQUAD)
                    if i == 2 and not last:
                        turn_x(b + 1)
                    score_quad(t, b, i)
                    if not (first and i == 0):
                        turn_p(t - 1)
                    if i == NQUAD - 1 and not first:
                        spread_scores(b - 1)
                    if not (first and i < 2):
                        add_y(t - 2, b if i >= 2 else b - 1, (i - 2) % NQUAD)
                    if not (first and i == 0):
                        mix(t - 1, b if i >= 1 else b - 1, (i - 1) % NQUAD)

            attend(0, True, False)
            with pe.Fori(1, NB - 1) as b:
                attend(b, False, False)
            attend(NB - 1, False, True)
            turn_p(STEPS - 1)
            add_y(STEPS - 2, NB - 1, NQUAD - 2)
            mix(STEPS - 1, NB - 1, NQUAD - 1)
            add_y(STEPS - 1, NB - 1, NQUAD - 1)
            spread_scores(NB - 1)

            pe.wait_ge(picks_made, NB)
            pe.wait_ge(x1_made, NB)
            pe.matmul(b_y[:, 0:NB], later[:], picked[:], start=True, stop=True).then_inc(place_found, 1)
            pe.wait_ge(onehot_made, 1)
            for j in range(NJ):
                last = pe.matmul(b_q[:, j:j + 1],
                                 onehot[:, j * BPJ:(j + 1) * BPJ, :].rearrange("p b s -> p (b s)"),
                                 token[:], start=True, stop=True)
            last.then_inc(rows_found, 1)

            def turn_h(i):
                pe.wait_ge(hn_made, i + 1)
                turn((f_T, f_T2)[i % NJ], hn_row[i % NJ]).then_inc(h_turned, 1)

            for j in range(NJ):
                turn_h(j)

            def piece_ready(n):
                pe.wait_ge(piece_lo_dve, n + 1)
                pe.wait_ge(piece_lo_pool, n + 1)

            def piece_rows(n, c):
                return wp_hi[n % NSLOT][:, c, :], wp_lo[n % NSLOT][:, c, :]

            def project(bank, j, n):
                for c in range(DC):
                    last = product(bank[:], (hT_hi[:, j, c, :], hT_lo[:, j, c, :]), piece_rows(n, c),
                                   c == 0, c == DC - 1)
                return last

            def project_tile(r, n):
                j = r % NJ
                if j == 0:
                    piece_ready(n)
                if r < NJ:
                    pe.wait_ge(hT_lo_done, r + 1)
                if r == 0:
                    pe.wait_ge(idx_made, 2 * NJ)
                wait(pe, f_biased, r - 1)
                project(f_proj[r % 2], j, n).then_inc(f_projected, 1)

            def turn_fk(i):
                j = i % NJ
                pe.wait_ge(f_roped, i + 1)
                if i < NJ:
                    pe.wait_ge(hT_lo_done, i + 1)
                else:
                    pe.wait_ge(fk_lo_done, i - NJ + 1)
                turn((f_T, f_T2)[j], turned[j]).then_inc(fk_turned, 1)

            r = 0
            for kp in range(FK):
                for j in range(NJ):
                    project_tile(r, P_WK + kp)
                    if kp > 0:
                        turn_fk(r - NJ)
                    r += 1
            for vp in range(FK):
                for j in range(NJ):
                    project_tile(r, P_WV + vp)
                    if vp == 0:
                        turn_fk(NJ * (FK - 1) + j)
                    r += 1
            for j in range(NJ):
                project_tile(r, p_wq(0))
                r += 1

            def attend_out(n):
                piece_ready(p_wo(n))
                pe.wait_ge(fo_lo_done, 2 * n + 2)
                for j in range(NJ):
                    for h in range(QUAD):
                        hs = slice(j * P, (j + 1) * P)
                        last = product(f_W[j][:], (foT_hi[:, h, hs], foT_lo[:, h, hs]),
                                       piece_rows(p_wo(n), h),
                                       n == 0 and h == 0, n == FQ - 1 and h == QUAD - 1)
                    last.then_inc(attn_done, 1)

            for n in range(FQ):
                for j in range(NJ):
                    pe.wait_ge(f_roped, NJ * FK + NJ * n + j + 1)
                    if n == 0:
                        pe.wait_ge(fk_lo_done, NJ * FK)
                    else:
                        pe.wait_ge(fo_lo_done, 2 * n)
                        pe.wait_ge(fp_lo_done, 3 * n)
                    turn((f_T, f_T2)[j], turned[j]).then_inc(fq_turned, 1)
                if n > 0:
                    attend_out(n - 1)
                pe.wait_ge(fq_lo_done, NJ * n + NJ)
                if n == 0:
                    pe.wait_ge(fk_lo_done, NJ * FK)
                for h in range(QUAD):
                    g = 2 * n + h // 2
                    last = product(f_S[:, h * P:(h + 1) * P], (fqT_hi[:, 0, h, :], fqT_lo[:, 0, h, :]),
                                   (fkT_hi[:, g, 0:P], fkT_lo[:, g, 0:P]), True, True)
                last.then_inc(f_scored, 1)
                for half_quad in range(2):
                    for a in range(2):
                        h, g = 2 * half_quad + a, 2 * n + half_quad
                        last = product((f_T, f_T2)[half_quad][:, a * NSEL:(a + 1) * NSEL],
                                       (fqT_hi[:, 1, h, :], fqT_lo[:, 1, h, :]),
                                       (fkT_hi[:, g, :], fkT_lo[:, g, :]), True, True)
                    last.then_inc(f_scored, 1)
                if n < FQ - 1:
                    for j in range(NJ):
                        project_tile(r, p_wq(n + 1))
                        r += 1
                pe.wait_ge(f_normed, 3 * n + 3)
                for half_quad in range(2):
                    bank = (f_T, f_T2)[half_quad]
                    for a in range(2):
                        h = 2 * half_quad + a
                        pe.transpose(bank[:, a * NSEL:a * NSEL + P], fs[0][:, h * P:(h + 1) * P], ident[:])
                        last = pe.transpose(bank[:, a * NSEL + P:(a + 1) * NSEL],
                                            fs[1 + half_quad][:, a * NSEL:a * NSEL + P], ident[:])
                    last.then_inc(fp_turned, 1)
                for h in range(QUAD):
                    last = pe.transpose(f_S[:, h * P:(h + 1) * P],
                                        fs[1 + h // 2][:, (h % 2) * NSEL + P:(h % 2 + 1) * NSEL], ident[:])
                last.then_inc(fp_turned, 1)
                pe.wait_ge(fp_lo_done, 3 * n + 3)
                if n == 0:
                    pe.wait_ge(fv_lo_done, NJ * FK)
                for g in range(2):
                    bank = (f_O, f_T)[g]
                    vs = slice((2 * n + g) * HD, (2 * n + g + 1) * HD)
                    product(bank[:], (fv_hi[:, 0, vs], fv_lo[:, 0, vs]),
                            (fp0_hi[:, 2 * g:2 * g + 2, :].rearrange("p h t -> p (h t)"),
                             fp0_lo[:, 2 * g:2 * g + 2, :].rearrange("p h t -> p (h t)")), True, False)
                    product(bank[:].rearrange("p (h t) -> p h t", h=2)[:, :, P:NSEL],
                            (fv_hi[:, 1, vs], fv_lo[:, 1, vs]),
                            (fp1_hi[:, 2 * g:2 * g + 2, :], fp1_lo[:, 2 * g:2 * g + 2, :]), False, True
                            ).then_inc(f_mixed, 1)
            attend_out(FQ - 1)

            for j in range(NJ):
                turn_h(NJ + j)

            def gate_rows(m):
                piece_ready(p_gate(m))
                for j in range(NJ):
                    if m == 0:
                        pe.wait_ge(hT_lo_done, NJ + j + 1)
                    wait(pe, silu_done, NJ * (m - 1) + j + 1)
                    last = project(f_proj[j], j, p_gate(m))
                    last.then_inc(gated, 1)

            def up_rows(m):
                piece_ready(p_up(m))
                for j in range(NJ):
                    wait(pe, act_done, NJ * (m - 1) + j + 1)
                    last = project((f_S, f_O)[j], j, p_up(m))
                    last.then_inc(upped, 1)

            gate_rows(0)
            up_rows(0)
            for m in range(FI):
                if m < FI - 1:
                    gate_rows(m + 1)
                for j in range(NJ):
                    pe.wait_ge(act_done, NJ * m + j + 1)
                    wait(pe, aT_lo_done, NJ * (m - 1) + j + 1)
                    turn((f_T, f_T2)[j], act_row[j]).then_inc(act_turned, 1)
                if m < FI - 1:
                    up_rows(m + 1)
                piece_ready(p_down(m))
                if m == 0:
                    pe.wait_ge(attn_copied, NJ)
                for j in range(NJ):
                    pe.wait_ge(aT_lo_done, NJ * m + j + 1)
                    for c in range(4):
                        last = product(f_W[j][:], (fqT_hi[:, j, c, :], fqT_lo[:, j, c, :]),
                                       piece_rows(p_down(m), c),
                                       m == 0 and c == 0, m == FI - 1 and c == 3)
                    last.then_inc(mlp_done, 1)


_INS = ['x', 'ctx_2048', 'mask_1xSxS2_ff0', 'L0_xattn_Wq', 'L0_xattn_bq', 'L0_xattn_Wk', 'L0_xattn_bk',
        'L0_xattn_Wv', 'L0_xattn_bv', 'L0_xattn_Wo', 'L0_xattn_qn_w', 'L0_xattn_kn_w', 'L0_ffn_w_router',
        'L0_ffn_wq', 'L0_ffn_bq', 'L0_ffn_wk', 'L0_ffn_bk', 'L0_ffn_wv', 'L0_ffn_bv', 'L0_ffn_wo',
        'L0_ffn_w_gate', 'L0_ffn_w_up', 'L0_ffn_w_down', 'L0_ffn_ln1_w', 'L0_ffn_ln2_w']


def _rope_table(positions, head_dim, theta=10000.0):
    import numpy as np
    inv = (1.0 / np.float32(theta) ** (np.arange(0, head_dim, 2, dtype=np.float32) / np.float32(head_dim)))
    ang = np.arange(positions, dtype=np.float32)[:, None] * inv.astype(np.float32)
    c, s = np.cos(ang), np.sin(ang)
    return np.concatenate([c, c, -s, s], axis=1).astype(np.float32)


def kernel(**inputs):
    import numpy as _np
    import concourse.bacc as _bacc
    from concourse import mybir as _mybir
    from concourse.bass_utils import run_bass_kernel_spmd as _run

    nc = _bacc.Bacc("TRN2", target_bir_lowering=False, num_devices=1)
    arrays, args = {}, []
    named = [(n, _np.ascontiguousarray(inputs[n])) for n in _INS]
    batches, seq, _ = named[0][1].shape
    pick = seq // 8
    blocks = batches * pick // 128
    slot = _np.arange(blocks)[None, :] * 128 + _np.arange(128)[:, None]
    named += [("rope_table", _rope_table(seq, 128)),
              ("slot_base", (slot // pick * seq).astype(_np.float32))]
    for name, a in named:
        arrays[f"in_{name}_dram"] = a
        args.append(nc.dram_tensor(f"in_{name}_dram", a.shape, _mybir.dt.from_np(a.dtype), kind="ExternalInput").ap())
    out = nc.dram_tensor("out_0_dram", (batches, seq, 512), _mybir.dt.float32, kind="ExternalOutput").ap()
    xattn_then_routed_ffn(nc, *args, out)
    r = _run(nc, [arrays], core_ids=[0])
    return r.results[0]["out_0_dram"]
```

```python
import concourse.bass as bass
from concourse import mybir
from contextlib import ExitStack


def xattn_then_routed_ffn(
    nc: bass.Bass,
    x: bass.AP,
    context: bass.AP,
    attn_mask: bass.AP,
    Wq: bass.AP,
    bq: bass.AP,
    Wk: bass.AP,
    bk: bass.AP,
    Wv: bass.AP,
    bv: bass.AP,
    Wo: bass.AP,
    qn_w: bass.AP,
    kn_w: bass.AP,
    w_router: bass.AP,
    ffn_wq: bass.AP,
    ffn_bq: bass.AP,
    ffn_wk: bass.AP,
    ffn_bk: bass.AP,
    ffn_wv: bass.AP,
    ffn_bv: bass.AP,
    ffn_wo: bass.AP,
    w_gate: bass.AP,
    w_up: bass.AP,
    w_down: bass.AP,
    ln1_w: bass.AP,
    ln2_w: bass.AP,
    rope_table: bass.AP,
    slot_base: bass.AP,
    out: bass.AP,
):
    fp32 = mybir.dt.float32
    f32r = mybir.dt.float32r
    bf16 = mybir.dt.bfloat16
    u32 = mybir.dt.uint32
    ALU = mybir.AluOpType
    ACT = mybir.ActivationFunctionType
    AX = mybir.AxisListType

    P = 128
    NB, S, D = x.shape
    DC = D // P
    HD = qn_w.shape[0]
    NH = Wq.shape[1] // HD
    NKV = Wk.shape[1] // HD
    QUAD = NH // NKV
    NQUAD = NKV
    STEPS = NB * NQUAD
    W = QUAD * HD
    PICK = S // 8
    NSEL = NB * PICK
    NJ = NSEL // P
    BPJ = NB // NJ
    SCALE = float(HD) ** -0.5
    EPS_LN, EPS_RMS = 1e-5, 1e-6
    MASKED = -3.0e38
    FH = ffn_wq.shape[1] // HD
    FKV = ffn_wk.shape[1] // HD
    FQ = FH // QUAD
    FK = FKV // QUAD
    FI = w_gate.shape[1] // W
    NSLOT = 4

    x_rows = x.rearrange("b s d -> (b s) d")
    ctx_rows = context.rearrange("b s d -> (b s) d")
    out_rows = out.rearrange("b s d -> (b s) d")
    k_store = nc.dram_tensor("k_store", [NB * P, NKV * S], fp32, kind="Internal").ap()
    v_store = nc.dram_tensor("v_store", [NB * P, NKV * HD], fp32, kind="Internal").ap()
    h_store = nc.dram_tensor("h_store", [NB * S, D], fp32, kind="Internal").ap()

    def chunked(w):
        return w.rearrange("(c p) n -> p c n", p=P)

    def columns(w, n):
        return chunked(w)[:, :, n * W:(n + 1) * W]

    def rows(w, g):
        return chunked(w[g * 4 * P:(g + 1) * 4 * P, :])

    ATTENTION = [("k", 0), ("v", 0), ("k", 1), ("q", 0), ("q", 1), ("v", 1), ("q", 2), ("o", 0),
                 ("q", 3), ("o", 1), ("o", 2), ("o", 3)]
    MATRIX = {"k": ffn_wk, "v": ffn_wv, "q": ffn_wq}
    PIECES = [rows(ffn_wo, n) if kind == "o" else columns(MATRIX[kind], n) for kind, n in ATTENTION]
    PIECES += [columns(w_gate, 0), columns(w_up, 0)]
    for m in range(FI - 1):
        PIECES += [columns(w_gate, m + 1), columns(w_up, m + 1), rows(w_down, m)]
    PIECES += [rows(w_down, FI - 1)]
    NP = len(PIECES)
    PROJECTIONS = [piece for piece in ATTENTION if piece[0] != "o"]
    AHEAD = PROJECTIONS.index(("q", 0)) + 1

    def p_wq(n):
        return ATTENTION.index(("q", n))

    def p_wo(n):
        return ATTENTION.index(("o", n))

    P_MLP = len(ATTENTION)

    def p_gate(m):
        return P_MLP if m == 0 else P_MLP + 3 * m - 1

    def p_up(m):
        return p_gate(m) + 1

    def p_down(m):
        return P_MLP + 3 * m + 4 if m < FI - 1 else NP - 1

    RAW_OF = [n % 2 if n < NSLOT else (n - 2) % 3 for n in range(NP)]
    NTH_RAW = [RAW_OF[:n + 1].count(RAW_OF[n]) for n in range(NP)]
    RAW_BEFORE = [max([k for k in range(n) if RAW_OF[k] == RAW_OF[n]] + [-1]) for n in range(NP)]

    ctx = ExitStack()
    with ctx:
        def sem(name):
            return ctx.enter_context(nc.semaphore(name))

        def sb_in(stack, name, shape, dt=fp32):
            return stack.enter_context(nc.sbuf_tensor(name, shape, dt))

        def split_in(stack, name, shape):
            return (sb_in(stack, name + "_hi", shape, f32r), sb_in(stack, name + "_lo", shape, f32r))

        ident = sb_in(ctx, "ident", [P, P])
        earlier = sb_in(ctx, "earlier", [P, P])
        later = sb_in(ctx, "later", [P, P])
        causal = sb_in(ctx, "causal", [P, 2 * P])
        slots = sb_in(ctx, "slots", [P, PICK])
        token = sb_in(ctx, "token", [P, 1])
        half = sb_in(ctx, "half", [P, QUAD])
        eps_head = sb_in(ctx, "eps_head", [P, QUAD])
        eps_ln = sb_in(ctx, "eps_ln", [P, 1])
        qw = sb_in(ctx, "qw", [P, 1])
        kw = sb_in(ctx, "kw", [P, 1])
        base_row = sb_in(ctx, "base_row", [P, NJ])
        picked = sb_in(ctx, "picked", [P, NB])
        bn = sb_in(ctx, "bn", [P, 6])
        mv = sb_in(ctx, "mv", [P, 2])
        rstd = sb_in(ctx, "rstd", [P, 1])
        raw = [sb_in(ctx, f"raw{i}", [P, 4, W]) for i in range(2)]

        wq_place = ExitStack()
        wq_hi, wq_lo = split_in(wq_place, "wq", [P, DC, NH * HD])
        wo_place = ExitStack()
        wo_hi, wo_lo = split_in(wo_place, "wo", [P, NH, D])

        with ExitStack() as st:
            cx = [sb_in(st, f"cx{i}", [P, D]) for i in range(2)]
            cT_hi, cT_lo = zip(*[split_in(st, f"cT{i}", [P, DC, P]) for i in range(2)])
            wq_raw = sb_in(st, "wq_raw", [P, DC, HD])
            wo_raw = sb_in(st, "wo_raw", [P, D])
            wk_hi, wk_lo = split_in(st, "wk", [P, DC, W])
            wv_hi, wv_lo = split_in(st, "wv", [P, DC, W])
            k_row = sb_in(st, "k_row", [P, NKV, HD])
            k_out = sb_in(st, "k_out", [P, NKV * S])
            v_out = sb_in(st, "v_out", [P, NKV * HD])
            bk_row = sb_in(st, "bk_row", [P, NKV * HD])
            bv_row = sb_in(st, "bv_row", [P, NKV * HD])
            k_sq = sb_in(st, "k_sq", [P, NKV, HD], bf16)
            k_ss = sb_in(st, "k_ss", [P, NKV])
            k_rs = sb_in(st, "k_rs", [P, NKV])

        with ExitStack() as st:
            xr = sb_in(st, "xr", [P, D])
            xn = sb_in(st, "xn", [P, D])
            xT_hi, xT_lo = split_in(st, "xT", [P, DC, P])
            k_raw = sb_in(st, "k_raw", [P, NKV * S])
            v_raw = sb_in(st, "v_raw", [P, NKV * HD])
            q_row = sb_in(st, "q_row", [P, QUAD, HD])
            q_nrm = sb_in(st, "q_nrm", [P, QUAD, HD])
            kT = sb_in(st, "kT", [P, NKV, 2, S], f32r)
            v_hi, v_lo = split_in(st, "v", [P, NKV * HD])
            bq_row = sb_in(st, "bq_row", [P, NH * HD])
            qT_hi, qT_lo = split_in(st, "qT", [P, W])
            s_row = sb_in(st, "s_row", [P, QUAD, S])
            p_row = sb_in(st, "p_row", [P, QUAD, S])
            pT_hi, pT_lo = split_in(st, "pT", [P, W])
            x_res = sb_in(st, "x_res", [P, D])
            mask = sb_in(st, "mask", [P, S])
            sq_junk = sb_in(st, "sq_junk", [P, QUAD, HD], bf16)
            q_ss = sb_in(st, "q_ss", [P, QUAD])
            q_rs = sb_in(st, "q_rs", [P, QUAD])
            neg_max = sb_in(st, "neg_max", [P, QUAD])
            p_sum = sb_in(st, "p_sum", [P, QUAD])
            p_inv = sb_in(st, "p_inv", [P, QUAD])
            score_wide = sb_in(st, "score_wide", [P, S])
            oT_hi, oT_lo = split_in(st, "oT", [P, W])
            x1 = sb_in(st, "x1", [P, D])
            h_row = sb_in(st, "h_row", [P, D])
            wr_row = sb_in(st, "wr_row", [P, D])
            dot_junk = sb_in(st, "dot_junk", [P, D], bf16)
            rank_junk = sb_in(st, "rank_junk", [P, 2, S], bf16)
            bn1 = sb_in(st, "bn1", [P, 6])
            mv1 = sb_in(st, "mv1", [P, 2])
            rstd1 = sb_in(st, "rstd1", [P, 1])
            score = sb_in(st, "score", [P, 1])
            above = sb_in(st, "above", [P, 1])
            tied = sb_in(st, "tied", [P, 1])
        wo_place.close()
        wq_place.close()

        with ExitStack() as st:
            wp_hi = [sb_in(st, f"wp_hi{i}", [P, 4, W], f32r) for i in range(NSLOT)]
            wp_lo = [sb_in(st, f"wp_lo{i}", [P, 4, W], f32r) for i in range(NSLOT)]
            raw.append(sb_in(st, "raw2", [P, 4, W]))
            hT_hi, hT_lo = split_in(st, "hT", [P, NJ, DC, P])
            fkT_hi, fkT_lo = split_in(st, "fkT", [P, FKV, NSEL])
            fv_hi, fv_lo = split_in(st, "fv", [P, NJ, FKV * HD])
            fqT_hi, fqT_lo = split_in(st, "fqT", [P, NJ, QUAD, P])
            foT_hi, foT_lo = split_in(st, "foT", [P, QUAD, NSEL])
            fp0_hi, fp0_lo = split_in(st, "fp0", [P, QUAD, NSEL])
            fp1_hi, fp1_lo = split_in(st, "fp1", [P, QUAD, P])
            fs = [sb_in(st, f"fs{i}", [P, W]) for i in range(3)]
            h_sel = [sb_in(st, f"h_sel{j}", [P, D]) for j in range(NJ)]
            rope = [sb_in(st, f"rope{j}", [P, 4 * (HD // 2)]) for j in range(NJ)]
            hn_row = [sb_in(st, f"hn_row{j}", [P, D]) for j in range(NJ)]
            proj = [sb_in(st, f"proj{i}", [P, W]) for i in range(2)]
            turned = [sb_in(st, f"turned{j}", [P, W]) for j in range(NJ)]
            by_cos = sb_in(st, "by_cos", [P, W])
            by_sin = sb_in(st, "by_sin", [P, W])
            x2_row = [sb_in(st, f"x2_row{j}", [P, D]) for j in range(NJ)]
            bias_row = [sb_in(st, f"bias_row{i}", [P, W]) for i in range(2)]
            ln1_row = sb_in(st, "ln1_row", [P, D])
            ln2_row = sb_in(st, "ln2_row", [P, D])
            wr2_row = sb_in(st, "wr2_row", [P, D])
            onehot = sb_in(st, "onehot", [P, NB, PICK])
            row_idx = [sb_in(st, f"row_idx{j}", [P, 1], u32) for j in range(NJ)]
            pos_idx = [sb_in(st, f"pos_idx{j}", [P, 1], u32) for j in range(NJ)]
            f_ss = sb_in(st, "f_ss", [P, 2 * NJ])
            f_ms = sb_in(st, "f_ms", [P, 2 * NJ])
            f_rs = sb_in(st, "f_rs", [P, 2 * NJ])
            f_max = sb_in(st, "f_max", [P, 8])
            f_sum = sb_in(st, "f_sum", [P, 8])
            f_inv = sb_in(st, "f_inv", [P, 8])
            g_dot = sb_in(st, "g_dot", [P, NJ])
            g_exp = sb_in(st, "g_exp", [P, NJ])
            g_one = sb_in(st, "g_one", [P, NJ])
            gate = sb_in(st, "gate", [P, NJ])
        act_row = turned
        tanh_row = proj
        final = hn_row
        attn_row = h_sel
        base = [by_cos, by_sin]

        banks = {n: ctx.enter_context(nc.psum_tensor(n, [P, W], fp32))
                 for n in ("b_q", "b_qT", "b_pT", "b_o", "b_y", "b_xT")}
        b_q, b_qT, b_pT, b_o, b_y, b_xT = banks.values()
        b_scores = ctx.enter_context(nc.psum_tensor("b_scores", [P, QUAD, 2 * S], fp32))
        b_s, b_s2 = [b_scores[:, i * QUAD // 2:(i + 1) * QUAD // 2, :].rearrange("p h t -> p (h t)")
                     for i in range(2)]
        b_rank = b_xT
        b_c, b_k, b_v, b_kT = b_xT, b_q, b_s, b_qT
        f_proj = [b_q, b_y]
        f_T, f_T2, f_S, f_O = b_qT, b_pT, b_s, b_o
        f_W = [b_xT, b_s2]

        const_made = sem("const_made")
        const_loaded = sem("const_loaded")
        kw_scaled = sem("kw_scaled")
        wk_loaded = [sem(f"wk_loaded{i}") for i in range(2)]
        wv_loaded = [sem("wv_loaded")]
        kv_w_hi = sem("kv_w_hi")
        kv_w_lo = sem("kv_w_lo")
        kv_bias_loaded = sem("kv_bias_loaded")
        cx_loaded = [sem(f"cx_loaded{i}") for i in range(2)]
        c_turned = sem("c_turned")
        c_hi = sem("c_hi")
        c_lo = sem("c_lo")
        k_projected = sem("k_projected")
        v_projected = sem("v_projected")
        k_biased = sem("k_biased")
        v_biased = sem("v_biased")
        k_squared = sem("k_squared")
        k_summed = sem("k_summed")
        k_rooted = sem("k_rooted")
        k_normed = sem("k_normed")
        k_turned = sem("k_turned")
        k_weighted = sem("k_weighted")
        k_stored = sem("k_stored")
        v_stored = sem("v_stored")
        wq_loaded = sem("wq_loaded")
        wo_loaded = sem("wo_loaded")
        w_hi = sem("w_hi")
        w_lo = sem("w_lo")
        wr_loaded = sem("wr_loaded")
        rows_loaded = sem("rows_loaded")
        x_loaded = sem("x_loaded")
        x_stats = sem("x_stats")
        x_mean = sem("x_mean")
        x_eps = sem("x_eps")
        x_rstd = sem("x_rstd")
        x_normed = sem("x_normed")
        x_turned = sem("x_turned")
        xT_hi_done = sem("xT_hi_done")
        xT_lo_done = sem("xT_lo_done")
        k_loaded = sem("k_loaded")
        v_loaded = sem("v_loaded")
        kT_hi_done = sem("kT_hi_done")
        kT_lo_done = sem("kT_lo_done")
        v_hi_done = sem("v_hi_done")
        v_lo_done = sem("v_lo_done")
        q_projected = sem("q_projected")
        q_biased = sem("q_biased")
        q_squared = sem("q_squared")
        q_summed = sem("q_summed")
        q_rooted = sem("q_rooted")
        q_normed = sem("q_normed")
        q_turned = sem("q_turned")
        qT_hi_done = sem("qT_hi_done")
        qT_lo_done = sem("qT_lo_done")
        scored = sem("scored")
        s_masked = sem("s_masked")
        s_summed = sem("s_summed")
        s_maxed = sem("s_maxed")
        p_exped = sem("p_exped")
        p_inverted = sem("p_inverted")
        p_normed = sem("p_normed")
        p_turned = sem("p_turned")
        pT_hi_done = sem("pT_hi_done")
        pT_lo_done = sem("pT_lo_done")
        mixed = sem("mixed")
        oT_hi_done = sem("oT_hi_done")
        oT_lo_done = sem("oT_lo_done")
        y_added = sem("y_added")
        res_loaded = sem("res_loaded")
        x1_made = sem("x1_made")
        x1_stats = sem("x1_stats")
        x1_mean = sem("x1_mean")
        x1_eps = sem("x1_eps")
        x1_rstd = sem("x1_rstd")
        h_made = sem("h_made")
        h_stored = sem("h_stored")
        base_made = sem("base_made")
        base_stored = sem("base_stored")
        scored_row = sem("scored_row")
        score_spread = sem("score_spread")
        score_turned = sem("score_turned")
        counted_above = sem("counted_above")
        counted_tied = sem("counted_tied")
        picks_made = sem("picks_made")
        raw_loaded = [sem(f"raw_loaded{i}") for i in range(3)]
        piece_hi = sem("piece_hi")
        piece_lo_dve = sem("piece_lo_dve")
        piece_lo_pool = sem("piece_lo_pool")
        place_found = sem("place_found")
        onehot_raw = sem("onehot_raw")
        onehot_made = sem("onehot_made")
        rows_found = sem("rows_found")
        idx_made = sem("idx_made")
        gathered_h = [sem(f"gathered_h{j}") for j in range(NJ)]
        gathered_rope = [sem(f"gathered_rope{j}") for j in range(NJ)]
        gathered_base = sem("gathered_base")
        f_rows_loaded = sem("f_rows_loaded")
        bias_loaded = [sem(f"bias_loaded{i}") for i in range(2)]
        f_squared = sem("f_squared")
        f_meaned = sem("f_meaned")
        f_rooted = sem("f_rooted")
        hn_made = sem("hn_made")
        h_turned = sem("h_turned")
        hT_hi_done = sem("hT_hi_done")
        hT_lo_done = sem("hT_lo_done")
        f_projected = sem("f_projected")
        f_biased = sem("f_biased")
        cos_done = sem("cos_done")
        sin_done = sem("sin_done")
        f_roped = sem("f_roped")
        fv_hi_done = sem("fv_hi_done")
        fv_lo_done = sem("fv_lo_done")
        fk_turned = sem("fk_turned")
        fk_hi_done = sem("fk_hi_done")
        fk_lo_done = sem("fk_lo_done")
        fq_turned = sem("fq_turned")
        fq_hi_done = sem("fq_hi_done")
        fq_lo_done = sem("fq_lo_done")
        f_scored = sem("f_scored")
        f_masked = sem("f_masked")
        f_maxed = sem("f_maxed")
        f_exped = sem("f_exped")
        f_inverted = sem("f_inverted")
        f_normed = sem("f_normed")
        fp_turned = sem("fp_turned")
        fp_hi_done = sem("fp_hi_done")
        fp_lo_done = sem("fp_lo_done")
        f_mixed = sem("f_mixed")
        fo_hi_done = sem("fo_hi_done")
        fo_lo_done = sem("fo_lo_done")
        attn_done = sem("attn_done")
        attn_copied = sem("attn_copied")
        x2_made = sem("x2_made")
        gated = sem("gated")
        upped = sem("upped")
        tanh_done = sem("tanh_done")
        silu_done = sem("silu_done")
        act_done = sem("act_done")
        act_turned = sem("act_turned")
        aT_hi_done = sem("aT_hi_done")
        aT_lo_done = sem("aT_lo_done")
        mlp_done = sem("mlp_done")
        g_dotted = sem("g_dotted")
        g_exped = sem("g_exped")
        g_plus = sem("g_plus")
        g_made = sem("g_made")
        delta_made = sem("delta_made")
        final_made = sem("final_made")
        out_stored = [sem(f"out_stored{j}") for j in range(NJ)]

        block = ctx.enter_context(nc.Block())

        def wait(eng, s, n):
            if not isinstance(n, int) or n > 0:
                eng.wait_ge(s, n)

        used_up = {}
        for o, piece in enumerate(PROJECTIONS):
            used_up[ATTENTION.index(piece)] = (f_projected, NJ * (o + 1))
        for n in range(FQ):
            used_up[p_wo(n)] = (attn_done, NJ * (n + 1))
        for m in range(FI):
            used_up[p_gate(m)] = (gated, NJ * (m + 1))
            used_up[p_up(m)] = (upped, NJ * (m + 1))
            used_up[p_down(m)] = (mlp_done, NJ * (m + 1))

        def split_early(n):
            return p_wq(0) + NSLOT + 2 * n

        def split_late(n):
            return [p_wq(0) + NSLOT + 2 * n + 1] if n < FQ - 1 else []

        def split_mlp(m):
            return range(P_MLP + 4 + 3 * m, min(P_MLP + 4 + 3 * (m + 1), NP))

        SCORE_TILES = ((QUAD, 0), (QUAD // 2, QUAD), (QUAD // 2, QUAD + QUAD // 2))

        def weights_over(eng):
            eng.wait_ge(v_projected, NB)

        def keys_over(eng):
            eng.wait_ge(k_stored, 16 * NB)
            eng.wait_ge(v_stored, 16 * NB)
            eng.wait_ge(w_lo, 2 * NB)
            eng.wait_ge(w_hi, 2 * NB)

        def layer1_over(eng):
            eng.wait_ge(h_stored, 16 * NB)
            eng.wait_ge(base_stored, 16 * NB)
            eng.wait_ge(picks_made, NB)

        def layer1_batches(one_batch):
            def run(eng):
                one_batch(0, True, False)
                with eng.Fori(1, NB - 1) as b:
                    one_batch(b, False, False)
                one_batch(NB - 1, False, True)
            return run

        @block.sync
        def _(sp):
            def spread(dst, vec):
                return sp.dma_start(dst, vec.partition_broadcast(P))

            sp.dma_start(cx[0][:], ctx_rows[0:S, :]).then_inc(cx_loaded[0], 16)
            for i in range(2):
                half_chunks = slice(i * DC // 2, (i + 1) * DC // 2)
                sp.dma_start(raw[0][:, half_chunks, :], chunked(Wk)[:, half_chunks, :]).then_inc(wk_loaded[i], 16)
            sp.dma_start(cx[1][:], ctx_rows[S:2 * S, :]).then_inc(cx_loaded[1], 16)
            sp.dma_start(raw[1][:], chunked(Wv)).then_inc(wv_loaded[0], 16)
            spread(bk_row[:], bk).then_inc(kv_bias_loaded, 16)
            spread(bv_row[:], bv).then_inc(kv_bias_loaded, 16)
            sp.dma_start(qw[:], qn_w.rearrange("(p a) -> p a", a=1)).then_inc(const_loaded, 16)
            sp.dma_start(kw[:], kn_w.rearrange("(p a) -> p a", a=1)).then_inc(const_loaded, 16)
            sp.dma_start(base_row[:], slot_base).then_inc(const_loaded, 16)

            def store_v(b):
                sp.wait_ge(v_biased, b + 1)
                sp.dma_start(v_store[bass.ds(b * P, P), :], v_out[:]).then_inc(v_stored, 16)

            def store_k(b):
                sp.wait_ge(k_weighted, b + 1)
                sp.dma_start(k_store[bass.ds(b * P, P), :], k_out[:]).then_inc(k_stored, 16)

            def kv_batch(b, par, first, last_two, beside=None):
                if not last_two:
                    sp.wait_ge(c_turned, b + 1)
                    sp.dma_start(cx[par][:], ctx_rows[bass.ds((b + 2) * S, S), :]
                                 ).then_inc(cx_loaded[par], 16)
                wait(sp, w_lo, 2 * b)
                sp.dma_start(wq_raw[:], chunked(Wq)[:, :, bass.ds(b * HD, HD)]).then_inc(wq_loaded, 16)
                sp.dma_start(wo_raw[:], Wo[bass.ds(b * P, P), :]).then_inc(wo_loaded, 16)
                if beside is not None:
                    beside()
                if not first:
                    store_v(b - 1)
                    store_k(b - 1)

            def first_rows():
                sp.wait_ge(c_turned, NB - 1)
                sp.dma_start(xr[:], x_rows[0:S, :]).then_inc(x_loaded, 16)

            kv_batch(0, 0, True, False)
            with sp.Fori(0, NB // 2 - 2) as g:
                kv_batch(2 * g + 1, 1, False, False)
                kv_batch(2 * g + 2, 0, False, False)
            kv_batch(NB - 3, 1, False, False)
            kv_batch(NB - 2, 0, False, True, first_rows)

            def query_bias():
                weights_over(sp)
                spread(bq_row[:, 0:W], bq[0:W]).then_inc(rows_loaded, 16)
                sp.dma_start(mask[:], attn_mask.rearrange("a s t -> (a s) t")).then_inc(rows_loaded, 16)

            kv_batch(NB - 1, 1, False, True, query_bias)

            def load_x(b):
                sp.dma_start(xr[:], x_rows[bass.ds(b * S, S), :]).then_inc(x_loaded, 16)

            def load_k(b):
                sp.dma_start(k_raw[:], k_store[bass.ds(b * P, P), :]).then_inc(k_loaded, 16)

            def load_v(b):
                sp.dma_start(v_raw[:], v_store[bass.ds(b * P, P), :]).then_inc(v_loaded, 16)

            sp.wait_ge(k_stored, 16 * (NB - 1))
            sp.wait_ge(v_stored, 16 * (NB - 1))
            load_k(0)
            load_v(0)
            spread(bq_row[:, W:NH * HD], bq[W:NH * HD]).then_inc(kv_bias_loaded, 16)
            sp.dma_start(x_res[:], x_rows[0:S, :]).then_inc(res_loaded, 16)
            store_v(NB - 1)
            store_k(NB - 1)

            def store_rows(b):
                sp.wait_ge(h_made, b + 1)
                sp.dma_start(h_store[bass.ds(b * S, S), :], h_row[:]).then_inc(h_stored, 16)
                sp.wait_ge(base_made, b + 1)
                sp.dma_start(out_rows[bass.ds(b * S, S), :], x1[:]).then_inc(base_stored, 16)

            def attend(b, first, last):
                if not last:
                    sp.wait_ge(x_normed, b + 1)
                    load_x(b + 1)
                    sp.wait_ge(kT_hi_done, b + 1)
                    sp.wait_ge(kT_lo_done, b + 1)
                    load_k(b + 1)
                if not first:
                    sp.wait_ge(x1_made, b)
                    sp.dma_start(x_res[:], x_rows[bass.ds(b * S, S), :]).then_inc(res_loaded, 16)
                if not last:
                    sp.wait_ge(v_hi_done, b + 1)
                    sp.wait_ge(v_lo_done, b + 1)
                    load_v(b + 1)
                if not first:
                    store_rows(b - 1)

            attend(0, True, False)
            keys_over(sp)
            spread(wr_row[:], w_router).then_inc(wr_loaded, 16)
            for i in range(2):
                sp.wait_ge(kv_w_hi, DC * (i + 1))
                sp.wait_ge(kv_w_lo, DC * (i + 1))
                sp.dma_start(raw[i][:], PIECES[i]).then_inc(raw_loaded[i], 16)
            with sp.Fori(1, NB - 1) as b:
                attend(b, False, False)
            attend(NB - 1, False, True)

            def load_piece(n):
                if RAW_BEFORE[n] >= 0:
                    sp.wait_ge(piece_hi, RAW_BEFORE[n] + 1)
                    sp.wait_ge(piece_lo_dve, RAW_BEFORE[n] + 1)
                    sp.wait_ge(piece_lo_pool, RAW_BEFORE[n] + 1)
                sp.dma_start(raw[RAW_OF[n]][:], PIECES[n]).then_inc(raw_loaded[RAW_OF[n]], 16)

            load_piece(2)
            store_rows(NB - 1)

            layer1_over(sp)
            spread(ln1_row[:], ln1_w).then_inc(f_rows_loaded, 16)
            spread(ln2_row[:], ln2_w).then_inc(f_rows_loaded, 16)
            spread(wr2_row[:], w_router).then_inc(f_rows_loaded, 16)
            VECTOR = {"k": ffn_bk, "v": ffn_bv, "q": ffn_bq}
            BIASES = [VECTOR[kind][n * W:(n + 1) * W] for kind, n in PROJECTIONS]

            def load_bias(i):
                if i >= 2:
                    sp.wait_ge(f_biased, NJ * (i - 1))
                spread(bias_row[i % 2][:], BIASES[i]).then_inc(bias_loaded[i % 2], 16)

            load_bias(0)
            load_bias(1)
            for j in range(NJ):
                sp.wait_ge(gathered_h[j], 16)
            load_piece(3)
            load_piece(NSLOT)
            for n in range(NSLOT + 1, NP):
                if 2 <= n - NSLOT < len(BIASES):
                    load_bias(n - NSLOT)
                load_piece(n)
            for j in range(NJ):
                sp.wait_ge(out_stored[j], 16)

        @block.gpsimd
        def _(pool):
            pool.memset(ident[:], 0.0).then_inc(const_made, 1)
            pool.memset(earlier[:], 1.0).then_inc(const_made, 1)
            pool.memset(later[:], 1.0).then_inc(const_made, 1)
            pool.memset(causal[:], 0.0).then_inc(const_made, 1)
            pool.memset(half[:], -0.5).then_inc(const_made, 1)
            pool.memset(eps_head[:], HD * EPS_RMS).then_inc(const_made, 1)
            pool.memset(eps_ln[:], EPS_LN).then_inc(const_made, 1)
            pool.iota(slots[:], pattern=[[1, PICK]], base=0, channel_multiplier=0,
                      allow_small_or_imprecise_dtypes=True).then_inc(const_made, 1)
            pool.iota(token[:], pattern=[[0, 1]], base=0, channel_multiplier=1,
                      allow_small_or_imprecise_dtypes=True).then_inc(const_made, 1)
            pool.wait_ge(const_made, 9)
            pool.affine_select(out=ident[:], in_=ident[:], compare_op=ALU.not_equal, fill=1.0,
                               base=0, pattern=[[-1, P]], channel_multiplier=1).then_inc(const_made, 1)
            pool.affine_select(out=earlier[:], in_=earlier[:], compare_op=ALU.is_gt, fill=0.0,
                               base=0, pattern=[[-1, P]], channel_multiplier=1).then_inc(const_made, 1)
            pool.affine_select(out=later[:], in_=later[:], compare_op=ALU.is_gt, fill=0.0,
                               base=0, pattern=[[1, P]], channel_multiplier=-1).then_inc(const_made, 1)
            pool.affine_select(out=causal[:, P:2 * P], in_=causal[:, P:2 * P], compare_op=ALU.is_ge,
                               fill=MASKED, base=0, pattern=[[-1, P]],
                               channel_multiplier=1).then_inc(const_made, 1)
            pool.wait_ge(const_made, 13)

            def rsqrt(src, dst, eps, summed, rooted, count):
                pool.tensor_tensor(dst, src, eps, ALU.add).then_inc(summed, 1)
                pool.wait_ge(summed, count)
                pool.tensor_tensor(dst, dst, half[:, 0:dst.shape[1]], ALU.pow).then_inc(rooted, 1)

            def per_head(stat, width):
                return stat[:, :].unsqueeze(2).to_broadcast([P, stat.shape[1], width])

            def kv_batch(b):
                pool.wait_ge(k_squared, b + 1)
                rsqrt(k_ss[:], k_rs[:], eps_head[:], k_summed, k_rooted, b + 1)
                pool.wait_ge(k_rooted, b + 1)
                pool.tensor_tensor(k_row[:], k_row[:], per_head(k_rs, HD), ALU.mult).then_inc(k_normed, 1)

            with pool.Fori(0, NB - 1) as b:
                kv_batch(b)

            def x_norm_stat(b):
                pool.wait_ge(x_mean, b + 1)
                rsqrt(mv[:, 1:2], rstd[:], eps_ln[:], x_eps, x_rstd, b + 1)

            def k_low(b):
                pool.wait_ge(kT_hi_done, b + 1)
                pool.tensor_tensor(kT[:, :, 1, :], k_raw[:].rearrange("p (g s) -> p g s", g=NKV),
                                   kT[:, :, 0, :].bitcast(fp32), ALU.subtract).then_inc(kT_lo_done, 1)

            def v_low(b):
                pool.wait_ge(v_hi_done, b + 1)
                pool.tensor_tensor(v_lo[:], v_raw[:], v_hi[:].bitcast(fp32),
                                   ALU.subtract).then_inc(v_lo_done, 1)

            def q_norm(t):
                pool.wait_ge(q_squared, t + 1)
                rsqrt(q_ss[:], q_rs[:], eps_head[:], q_summed, q_rooted, t + 1)
                pool.wait_ge(q_rooted, t + 1)
                wait(pool, q_turned, t)
                pool.tensor_tensor(q_nrm[:], q_row[:], per_head(q_rs, HD), ALU.mult).then_inc(q_normed, 1)

            def p_norm(t):
                pool.wait_ge(p_inverted, t + 1)
                pool.tensor_tensor(p_row[:], p_row[:], per_head(p_inv, S), ALU.mult).then_inc(p_normed, 1)

            def out_stat(b):
                pool.wait_ge(x1_mean, b + 1)
                rsqrt(mv1[:, 1:2], rstd1[:], eps_ln[:], x1_eps, x1_rstd, b + 1)

            def base_rows(b):
                pool.wait_ge(h_made, b + 1)
                pool.tensor_tensor(x1[:], x1[:], h_row[:], ALU.add).then_inc(base_made, 1)

            x_norm_stat(0)
            kv_batch(NB - 1)
            pool.wait_ge(w_lo, 2 * NB)
            weights_over(pool)
            q_norm(0)
            k_low(0)

            def attend(b, first, last):
                for i in range(NQUAD):
                    t = NQUAD * b + i
                    if i == 0 and not last:
                        x_norm_stat(b + 1)
                    if not (last and i == NQUAD - 1):
                        q_norm(t + 1)
                    p_norm(t)
                    if i == 0:
                        v_low(b)
                    if i == 0 and first:
                        keys_over(pool)
                    if i == 1 and not first:
                        out_stat(b - 1)
                    if i == 2 and not first:
                        base_rows(b - 1)
                    if i == NQUAD - 1 and not last:
                        k_low(b + 1)

            attend(0, True, False)
            with pool.Fori(1, NB - 1) as b:
                attend(b, False, False)
            attend(NB - 1, False, True)

            def split_low(n):
                pool.wait_ge(piece_hi, n + 1)
                pool.tensor_tensor(wp_lo[n % NSLOT][:, 0:2, :], raw[RAW_OF[n]][:, 0:2, :],
                                   wp_hi[n % NSLOT][:, 0:2, :].bitcast(fp32),
                                   ALU.subtract).then_inc(piece_lo_pool, 1)

            split_low(0)
            split_low(1)
            out_stat(NB - 1)
            base_rows(NB - 1)

            pool.wait_ge(idx_made, 2 * NJ)
            layer1_over(pool)
            for j in range(NJ):
                pool.indirect_dma_start(h_sel[j][:], None, h_store,
                                        bass.IndirectOffsetOnAxis(ap=row_idx[j][:, 0:1], axis=0)
                                        ).then_inc(gathered_h[j], 16)
            for j in range(NJ):
                pool.indirect_dma_start(rope[j][:], None, rope_table,
                                        bass.IndirectOffsetOnAxis(ap=pos_idx[j][:, 0:1], axis=0)
                                        ).then_inc(gathered_rope[j], 16)

            def row_rsqrt(i):
                pool.wait_ge(f_squared, i + 1)
                pool.tensor_scalar(f_ms[:, i:i + 1], f_ss[:, i:i + 1], 1.0 / D, EPS_RMS,
                                   ALU.mult, ALU.add).then_inc(f_meaned, 1)
                pool.wait_ge(f_meaned, i + 1)
                pool.tensor_tensor(f_rs[:, i:i + 1], f_ms[:, i:i + 1], half[:, 0:1],
                                   ALU.pow).then_inc(f_rooted, 1)

            for j in range(NJ):
                row_rsqrt(j)
            split_low(2)
            split_low(3)

            def by_cosine(r, k):
                j = r % NJ
                pool.wait_ge(f_biased, r + 1)
                pool.wait_ge(gathered_rope[j], 16)
                wait(pool, f_roped, k)
                pool.tensor_tensor(by_cos[:].rearrange("p (h d) -> p h d", h=QUAD),
                                   proj[r % 2][:].rearrange("p (h d) -> p h d", h=QUAD),
                                   rope[j][:, 0:HD].unsqueeze(1).to_broadcast([P, QUAD, HD]),
                                   ALU.mult).then_inc(cos_done, 1)

            def v_low_rows(r, i):
                pool.wait_ge(fv_hi_done, i + 1)
                c = i // NJ
                pool.tensor_tensor(fv_lo[:, i % NJ, c * W:(c + 1) * W], proj[r % 2][:],
                                   fv_hi[:, i % NJ, c * W:(c + 1) * W].bitcast(fp32),
                                   ALU.subtract).then_inc(fv_lo_done, 1)

            for o, (kind, n) in enumerate(PROJECTIONS[:AHEAD]):
                for j in range(NJ):
                    if kind == "v":
                        v_low_rows(NJ * o + j, NJ * n + j)
                    else:
                        by_cosine(NJ * o + j, NJ * (n if kind == "k" else FK + n) + j)
                if o > 0:
                    split_low(NSLOT + o - 1)

            def next_query_cosine(n, j):
                o = PROJECTIONS.index(("q", n + 1))
                by_cosine(NJ * o + j, NJ * (FK + n + 1) + j)

            for n in range(FQ):
                if n < FQ - 1:
                    next_query_cosine(n, 0)
                    next_query_cosine(n, 1)
                    split_low(split_early(n))
                for piece in split_late(n):
                    split_low(piece)
                for i, (heads, col) in enumerate(SCORE_TILES):
                    pool.wait_ge(f_inverted, 3 * n + i + 1)
                    pool.tensor_tensor(
                        fs[i][:].rearrange("p (h t) -> p h t", h=heads),
                        fs[i][:].rearrange("p (h t) -> p h t", h=heads),
                        f_inv[:, col:col + heads].unsqueeze(2).to_broadcast([P, heads, W // heads]),
                        ALU.mult).then_inc(f_normed, 1)
                if n == 0:
                    for j in range(NJ):
                        v_low_rows(NJ * PROJECTIONS.index(("v", 1)) + j, NJ + j)
            split_low(split_early(FQ - 1))
            pool.wait_ge(f_roped, NJ * (FK + FQ))
            for j in range(NJ):
                pool.indirect_dma_start(base[j][:], None, out_rows,
                                        bass.IndirectOffsetOnAxis(ap=row_idx[j][:, 0:1], axis=0)
                                        ).then_inc(gathered_base, 16)
            split_low(P_MLP + 2)
            for j in range(NJ):
                row_rsqrt(NJ + j)
            split_low(P_MLP + 3)
            for n in range(P_MLP + 4, NP):
                split_low(n)
            for j in range(NJ):
                pool.wait_ge(final_made, j + 1)
                pool.indirect_dma_start(out_rows, bass.IndirectOffsetOnAxis(ap=row_idx[j][:, 0:1], axis=0),
                                        final[j][:], None).then_inc(out_stored[j], 16)
            for j in range(NJ):
                pool.wait_ge(out_stored[j], 16)

        @block.scalar
        def _(act):
            def copy(dst, src):
                return act.activation(dst, src, ACT.Copy)

            def turn_c(b, par):
                act.wait_ge(c_turned, b + 1)
                wait(act, v_projected, b - 1)
                copy(cT_hi[par][:].rearrange("p c t -> p (c t)"), b_c[:]).then_inc(c_hi, 1)

            turn_c(0, 0)
            for hi, rw, loaded in ((wk_hi, raw[0], wk_loaded), (wv_hi, raw[1], wv_loaded)):
                for c in range(DC):
                    act.wait_ge(loaded[c * len(loaded) // DC], 16)
                    copy(hi[:, c, :], rw[:, c, :]).then_inc(kv_w_hi, 1)
            act.wait_ge(const_loaded, 48)
            act.wait_ge(kw_scaled, 1)

            def weigh_k(b):
                act.wait_ge(k_turned, b + 1)
                wait(act, k_stored, 16 * b)
                act.activation(k_out[:], b_kT[:], ACT.Copy, scale=kw[:, 0:1]).then_inc(k_weighted, 1)

            def kv_batch(b, par, first, last):
                if not last:
                    turn_c(b + 1, 1 - par)
                act.wait_ge(k_biased, b + 1)
                wait(act, k_rooted, b)
                for h in range(NKV):
                    sq = act.activation(k_sq[:, h, :], k_row[:, h, :], ACT.Square, accum_out=k_ss[:, h:h + 1])
                sq.then_inc(k_squared, 1)
                if not first:
                    weigh_k(b - 1)
                act.wait_ge(wq_loaded, 16 * (b + 1))
                copy(wq_hi[:, :, bass.ds(b * HD, HD)], wq_raw[:]).then_inc(w_hi, 1)
                act.wait_ge(wo_loaded, 16 * (b + 1))
                copy(wo_hi[:, bass.ds(b, 1), :], wo_raw[:].unsqueeze(1)).then_inc(w_hi, 1)

            kv_batch(0, 0, True, False)
            with act.Fori(0, NB // 2 - 1) as g:
                kv_batch(2 * g + 1, 1, False, False)
                kv_batch(2 * g + 2, 0, False, False)
            def x_high(b):
                act.wait_ge(x_turned, b + 1)
                copy(xT_hi[:].rearrange("p c t -> p (c t)"), b_xT[:]).then_inc(xT_hi_done, 1)


            def first_rows():
                act.wait_ge(v_projected, NB - 1)
                x_high(0)

            first_rows()
            kv_batch(NB - 1, 1, False, True)

            def k_high(b):
                act.wait_ge(k_loaded, 16 * (b + 1))
                wait(act, scored, NQUAD * b)
                copy(kT[:, :, 0, :], k_raw[:].rearrange("p (g s) -> p g s", g=NKV)).then_inc(kT_hi_done, 1)

            def v_high(b):
                act.wait_ge(v_loaded, 16 * (b + 1))
                wait(act, mixed, NQUAD * b)
                copy(v_hi[:], v_raw[:]).then_inc(v_hi_done, 1)

            def q_high(t):
                act.wait_ge(q_turned, t + 1)
                wait(act, scored, t)
                act.activation(qT_hi[:], b_qT[:], ACT.Copy, scale=qw[:, 0:1]).then_inc(qT_hi_done, 1)

            def p_high(t):
                act.wait_ge(p_turned, t + 1)
                wait(act, mixed, t)
                copy(pT_hi[:], b_pT[:]).then_inc(pT_hi_done, 1)

            def o_high(t):
                act.wait_ge(mixed, t + 1)
                wait(act, y_added, t)
                copy(oT_hi[:], b_o[:]).then_inc(oT_hi_done, 1)

            def squares(t):
                act.wait_ge(q_biased, t + 1)
                wait(act, q_rooted, t)
                for h in range(QUAD):
                    sq = act.activation(sq_junk[:, h, :], q_row[:, h, :], ACT.Square, accum_out=q_ss[:, h:h + 1])
                sq.then_inc(q_squared, 1)

            def exps(t):
                act.wait_ge(s_maxed, t + 1)
                wait(act, p_turned, t)
                for h in range(QUAD):
                    e = act.activation(p_row[:, h, :], s_row[:, h, :], ACT.Exp,
                                       bias=neg_max[:, h:h + 1], accum_out=p_sum[:, h:h + 1])
                e.then_inc(p_exped, 1)

            weights_over(act)
            weigh_k(NB - 1)
            squares(0)
            k_high(0)

            def attend(b, first, last):
                for i in range(NQUAD):
                    t = NQUAD * b + i
                    q_high(t)
                    if not (last and i == NQUAD - 1):
                        squares(t + 1)
                    if not (first and i == 0):
                        p_high(t - 1)
                    if i == 2 and not last:
                        x_high(b + 1)
                    exps(t)
                    if first and i == 0:
                        keys_over(act)
                    if not (first and i == 0):
                        o_high(t - 1)
                    if i == 0:
                        v_high(b)
                    if i == NQUAD - 1 and not last:
                        k_high(b + 1)

            attend(0, True, False)
            with act.Fori(1, NB - 1) as b:
                attend(b, False, False)
            attend(NB - 1, False, True)
            p_high(STEPS - 1)

            def split_high(n):
                act.wait_ge(raw_loaded[RAW_OF[n]], 16 * NTH_RAW[n])
                if n >= NSLOT:
                    act.wait_ge(*used_up[n - NSLOT])
                copy(wp_hi[n % NSLOT][:], raw[RAW_OF[n]][:]).then_inc(piece_hi, 1)

            act.wait_ge(q_projected, STEPS)
            split_high(0)
            o_high(STEPS - 1)
            split_high(1)
            split_high(2)
            layer1_over(act)

            def row_squares(i, src):
                act.activation(hn_row[i % NJ][:], src, ACT.Square, accum_out=f_ss[:, i:i + 1]).then_inc(f_squared, 1)

            for j in range(NJ):
                act.wait_ge(gathered_h[j], 16)
                row_squares(j, h_sel[j][:])

            def h_high(i):
                act.wait_ge(h_turned, i + 1)
                copy(hT_hi[:, i % NJ].rearrange("p c t -> p (c t)"), (f_T, f_T2)[i % NJ][:]
                     ).then_inc(hT_hi_done, 1)

            for j in range(NJ):
                h_high(j)

            def fk_high(i):
                kp, j = i // NJ, i % NJ
                act.wait_ge(fk_turned, i + 1)
                copy(fkT_hi[:, kp * QUAD:(kp + 1) * QUAD, j * P:(j + 1) * P],
                     (f_T, f_T2)[j][:].rearrange("p (h t) -> p h t", h=QUAD)).then_inc(fk_hi_done, 1)

            def v_high_rows(r, i):
                act.wait_ge(f_biased, r + 1)
                c = i // NJ
                copy(fv_hi[:, i % NJ, c * W:(c + 1) * W], proj[r % 2][:]).then_inc(fv_hi_done, 1)

            split_high(3)
            for o, (kind, n) in enumerate(PROJECTIONS[:AHEAD]):
                for j in range(NJ):
                    if kind == "v":
                        v_high_rows(NJ * o + j, NJ * n + j)
                    if o > 0 and PROJECTIONS[o - 1][0] == "k":
                        fk_high(NJ * PROJECTIONS[o - 1][1] + j)
                if o < AHEAD - 1:
                    split_high(NSLOT + o)

            def probs_high(n):
                act.wait_ge(fp_turned, 3 * n + 1)
                wait(act, f_mixed, 2 * n)
                copy(fp0_hi[:, 0:2, :].rearrange("p h t -> p (h t)"), f_T[:]).then_inc(fp_hi_done, 1)
                act.wait_ge(fp_turned, 3 * n + 2)
                copy(fp0_hi[:, 2:4, :].rearrange("p h t -> p (h t)"), f_T2[:]).then_inc(fp_hi_done, 1)
                act.wait_ge(fp_turned, 3 * n + 3)
                copy(fp1_hi[:].rearrange("p h t -> p (h t)"), f_S[:]).then_inc(fp_hi_done, 1)

            def mixed_high(n):
                for g in range(2):
                    act.wait_ge(f_mixed, 2 * n + g + 1)
                    wait(act, attn_done, NJ * n)
                    copy(foT_hi[:, 2 * g:2 * g + 2, :].rearrange("p h t -> p (h t)"),
                         (f_O, f_T)[g][:]).then_inc(fo_hi_done, 1)

            for n in range(FQ):
                for j in range(NJ):
                    act.wait_ge(fq_turned, NJ * n + j + 1)
                    wait(act, f_scored, 3 * n)
                    copy(fqT_hi[:, j].rearrange("p h t -> p (h t)"), (f_T, f_T2)[j][:]
                         ).then_inc(fq_hi_done, 1)
                if n > 0:
                    probs_high(n - 1)
                if n < FQ - 1:
                    split_high(split_early(n))
                if n > 0:
                    mixed_high(n - 1)
                for piece in split_late(n):
                    split_high(piece)
                for i, (heads, col) in enumerate(SCORE_TILES):
                    width = W // heads
                    act.wait_ge(f_maxed, 3 * n + i + 1)
                    for h in range(heads):
                        e = act.activation(fs[i][:, h * width:(h + 1) * width],
                                           fs[i][:, h * width:(h + 1) * width], ACT.Exp,
                                           bias=f_max[:, col + h:col + h + 1],
                                           accum_out=f_sum[:, col + h:col + h + 1])
                    e.then_inc(f_exped, 1)
                if n == FQ - 1:
                    split_high(split_early(n))
                if n == 0:
                    for j in range(NJ):
                        v_high_rows(NJ * PROJECTIONS.index(("v", 1)) + j, NJ + j)
            probs_high(FQ - 1)
            mixed_high(FQ - 1)
            split_high(P_MLP + 2)
            for j in range(NJ):
                act.wait_ge(x2_made, j + 1)
                row_squares(NJ + j, x2_row[j][:])
            for j in range(NJ):
                h_high(NJ + j)
            for j in range(NJ):
                copy(attn_row[j][:], f_W[j][:]).then_inc(attn_copied, 1)
            split_high(P_MLP + 3)
            act.wait_ge(g_dotted, NJ)
            act.activation(g_exp[:], g_dot[:], ACT.Exp, scale=-1.0).then_inc(g_exped, 1)
            for m in range(FI):
                for j in range(NJ):
                    act.wait_ge(gated, NJ * m + j + 1)
                    wait(act, act_done, NJ * (m - 1) + j + 1)
                    act.activation(tanh_row[j][:], f_proj[j][:], ACT.Tanh, scale=0.5).then_inc(tanh_done, 1)
                for piece in split_mlp(m):
                    split_high(piece)
                for j in range(NJ):
                    act.wait_ge(act_turned, NJ * m + j + 1)
                    wait(act, mlp_done, NJ * m)
                    copy(fqT_hi[:, j].rearrange("p h t -> p (h t)"), (f_T, f_T2)[j][:]
                         ).then_inc(aT_hi_done, 1)

        @block.vector
        def _(dve):
            def low(dst, src, hi):
                return dve.tensor_tensor(dst, src, hi.bitcast(fp32), ALU.subtract)

            def turn_c(b, par):
                dve.wait_ge(c_hi, b + 1)
                low(cT_lo[par][:].rearrange("p c t -> p (c t)"), b_c[:],
                    cT_hi[par][:].rearrange("p c t -> p (c t)")).then_inc(c_lo, 1)

            turn_c(0, 0)
            for i, (hi, lo, rw) in enumerate(((wk_hi, wk_lo, raw[0]), (wv_hi, wv_lo, raw[1]))):
                for c in range(DC):
                    dve.wait_ge(kv_w_hi, DC * i + c + 1)
                    low(lo[:, c, :], rw[:, c, :], hi[:, c, :]).then_inc(kv_w_lo, 1)
            dve.wait_ge(const_loaded, 48)
            dve.tensor_scalar(kw[:], kw[:], 1.0 / SCALE, None, ALU.mult).then_inc(kw_scaled, 1)
            dve.wait_ge(kv_bias_loaded, 32)

            def kv_batch(b, par, last, beside=None):
                if not last:
                    turn_c(b + 1, 1 - par)
                dve.wait_ge(k_projected, b + 1)
                wait(dve, k_turned, b)
                dve.tensor_tensor(k_row[:].rearrange("p h d -> p (h d)"), b_k[:], bk_row[:],
                                  ALU.add).then_inc(k_biased, 1)
                dve.wait_ge(v_projected, b + 1)
                wait(dve, v_stored, 16 * b)
                dve.tensor_tensor(v_out[:], b_v[:], bv_row[:], ALU.add).then_inc(v_biased, 1)
                if beside is not None:
                    beside()
                dve.wait_ge(w_hi, 2 * b + 1)
                low(wq_lo[:, :, bass.ds(b * HD, HD)], wq_raw[:],
                    wq_hi[:, :, bass.ds(b * HD, HD)]).then_inc(w_lo, 1)
                dve.wait_ge(w_hi, 2 * b + 2)
                low(wo_lo[:, bass.ds(b, 1), :], wo_raw[:].unsqueeze(1),
                    wo_hi[:, bass.ds(b, 1), :]).then_inc(w_lo, 1)

            kv_batch(0, 0, False)
            with dve.Fori(0, NB // 2 - 2) as g:
                kv_batch(2 * g + 1, 1, False)
                kv_batch(2 * g + 2, 0, False)
            kv_batch(NB - 3, 1, False)

            def x_statistics(b):
                dve.wait_ge(x_loaded, 16 * (b + 1))
                wait(dve, x_rstd, b)
                dve.bn_stats(bn[:], xr[:]).then_inc(x_stats, 1)

            def x_moments(b):
                dve.bn_aggr(mv[:], bn[:]).then_inc(x_mean, 1)

            def x_norm(b):
                dve.wait_ge(x_rstd, b + 1)
                wait(dve, x_turned, b)
                dve.tensor_scalar(xn[:], xr[:], mv[:, 0:1], rstd[:, 0:1],
                                  ALU.subtract, ALU.mult).then_inc(x_normed, 1)

            def x_low(b):
                dve.wait_ge(xT_hi_done, b + 1)
                low(xT_lo[:].rearrange("p c t -> p (c t)"), b_xT[:],
                    xT_hi[:].rearrange("p c t -> p (c t)")).then_inc(xT_lo_done, 1)

            def q_bias(t, quad):
                dve.wait_ge(q_projected, t + 1)
                wait(dve, q_normed, t)
                dve.tensor_tensor(q_row[:].rearrange("p h d -> p (h d)"), b_q[:],
                                  bq_row[:, quad * W:(quad + 1) * W], ALU.add).then_inc(q_biased, 1)

            def q_low(t):
                dve.wait_ge(qT_hi_done, t + 1)
                dve.scalar_tensor_tensor(qT_lo[:], b_qT[:], qw[:, 0:1], qT_hi[:].bitcast(fp32),
                                         ALU.mult, ALU.subtract).then_inc(qT_lo_done, 1)

            def s_mask(t):
                dve.wait_ge(scored, t + 1)
                wait(dve, p_exped, t)
                dve.tensor_tensor(s_row[:], b_scores[:, :, 0:S],
                                  mask[:].unsqueeze(1).to_broadcast([P, QUAD, S]),
                                  ALU.add).then_inc(s_masked, 1)

            def s_sum(t):
                dve.wait_ge(s_masked, t + 1)
                dve.tensor_tensor(s_row[:], s_row[:], b_scores[:, :, S:2 * S], ALU.add).then_inc(s_summed, 1)

            def s_max(t):
                dve.wait_ge(s_summed, t + 1)
                dve.tensor_reduce(neg_max[:], s_row[:], AX.X, ALU.max, negate=True).then_inc(s_maxed, 1)

            def p_low(t):
                dve.wait_ge(pT_hi_done, t + 1)
                low(pT_lo[:], b_pT[:], pT_hi[:]).then_inc(pT_lo_done, 1)

            def p_invert(t):
                dve.wait_ge(p_exped, t + 1)
                wait(dve, p_normed, t)
                dve.reciprocal(p_inv[:], p_sum[:]).then_inc(p_inverted, 1)

            def o_low(t):
                dve.wait_ge(oT_hi_done, t + 1)
                low(oT_lo[:], b_o[:], oT_hi[:]).then_inc(oT_lo_done, 1)

            def add_residual(b):
                dve.wait_ge(y_added, NQUAD * (b + 1))
                dve.wait_ge(res_loaded, 16 * (b + 1))
                wait(dve, base_stored, 16 * b)
                dve.tensor_tensor(x1[:], b_y[:], x_res[:], ALU.add).then_inc(x1_made, 1)
                dve.wait_ge(x1_made, b + 1)
                dve.bn_stats(bn1[:], x1[:]).then_inc(x1_stats, 1)

            def x1_moments(b):
                dve.bn_aggr(mv1[:], bn1[:]).then_inc(x1_mean, 1)

            def norm_out(b):
                dve.wait_ge(x1_rstd, b + 1)
                wait(dve, h_stored, 16 * b)
                dve.tensor_scalar(h_row[:], x1[:], mv1[:, 0:1], rstd1[:, 0:1],
                                  ALU.subtract, ALU.mult).then_inc(h_made, 1)
                dve.wait_ge(h_made, b + 1)
                dve.tensor_tensor_reduce(dot_junk[:], h_row[:], wr_row[:], 1.0, 0.0, ALU.mult,
                                         ALU.add, accum_out=score[:, 0:1]).then_inc(scored_row, 1)
                dve.wait_ge(scored_row, b + 1)
                dve.tensor_copy(score_wide[:], score[:, 0:1].to_broadcast([P, S])).then_inc(score_spread, 1)

            def rank(b):
                dve.wait_ge(score_turned, b + 1)
                dve.tensor_scalar(rank_junk[:, 0, :], b_rank[:, 0:S], score[:, 0:1], 0.0, ALU.is_gt,
                                  ALU.add, accum_out=above[:, 0:1]).then_inc(counted_above, 1)
                dve.scalar_tensor_tensor(rank_junk[:, 1, :], b_rank[:, 0:S], score[:, 0:1], earlier[:],
                                         ALU.is_equal, ALU.mult,
                                         accum_out=tied[:, 0:1]).then_inc(counted_tied, 1)
                dve.wait_ge(counted_above, b + 1)
                dve.wait_ge(counted_tied, b + 1)
                dve.tensor_scalar(picked[:, bass.ds(b, 1)], above[:, 0:1], tied[:, 0:1], float(PICK),
                                  ALU.add, ALU.is_lt).then_inc(picks_made, 1)

            dve.wait_ge(const_made, 13)

            def norm_first_rows():
                dve.wait_ge(c_turned, NB)
                x_statistics(0)
                dve.wait_ge(x_stats, 1)
                x_moments(0)
                x_norm(0)

            def split_first_rows():
                dve.wait_ge(v_projected, NB - 1)
                x_low(0)

            kv_batch(NB - 2, 0, False, norm_first_rows)
            split_first_rows()
            kv_batch(NB - 1, 1, True)
            weights_over(dve)
            dve.wait_ge(w_lo, 2 * NB)
            dve.wait_ge(rows_loaded, 32)
            q_bias(0, 0)
            dve.wait_ge(kv_bias_loaded, 48)

            def attend(b, first, last):
                for i in range(NQUAD):
                    t = NQUAD * b + i
                    if i == 0 and not last:
                        x_statistics(b + 1)
                        dve.wait_ge(x_stats, b + 2)
                    q_low(t)
                    if i == 0 and not last:
                        x_moments(b + 1)
                    if i == 1 and not last:
                        x_norm(b + 1)
                    if not (last and i == NQUAD - 1):
                        q_bias(t + 1, (i + 1) % NQUAD)
                    s_mask(t)
                    s_sum(t)
                    s_max(t)
                    if not (first and i == 0):
                        p_low(t - 1)
                    if i == 2 and not last:
                        x_low(b + 1)
                    if i == 1 and not first:
                        add_residual(b - 1)
                    if i == 2 and not first:
                        norm_out(b - 1)
                    if i == NQUAD - 1 and not first:
                        rank(b - 1)
                    if i == 1 and not first:
                        dve.wait_ge(x1_stats, b)
                    p_invert(t)
                    if first and i == 0:
                        keys_over(dve)
                    if i == 1 and not first:
                        x1_moments(b - 1)
                    if not (first and i == 0):
                        o_low(t - 1)

            attend(0, True, False)
            dve.wait_ge(wr_loaded, 16)
            with dve.Fori(1, NB - 1) as b:
                attend(b, False, False)
            attend(NB - 1, False, True)
            p_low(STEPS - 1)

            def split_low(n):
                dve.wait_ge(piece_hi, n + 1)
                low(wp_lo[n % NSLOT][:, 2:4, :], raw[RAW_OF[n]][:, 2:4, :],
                    wp_hi[n % NSLOT][:, 2:4, :]).then_inc(piece_lo_dve, 1)

            split_low(0)
            o_low(STEPS - 1)
            split_low(1)
            add_residual(NB - 1)
            dve.wait_ge(x1_stats, NB)
            x1_moments(NB - 1)
            norm_out(NB - 1)
            rank(NB - 1)

            layer1_over(dve)
            dve.wait_ge(place_found, 1)
            dve.tensor_tensor(onehot[:], b_y[:, 0:NB].unsqueeze(2).to_broadcast([P, NB, PICK]),
                              slots[:].unsqueeze(1).to_broadcast([P, NB, PICK]),
                              ALU.is_equal).then_inc(onehot_raw, 1)
            dve.wait_ge(onehot_raw, 1)
            dve.tensor_tensor(onehot[:], onehot[:], picked[:].unsqueeze(2).to_broadcast([P, NB, PICK]),
                              ALU.mult).then_inc(onehot_made, 1)
            dve.wait_ge(rows_found, 1)
            for j in range(NJ):
                dve.tensor_tensor(row_idx[j][:], b_q[:, j:j + 1], base_row[:, j:j + 1],
                                  ALU.add).then_inc(idx_made, 1)
                dve.tensor_copy(pos_idx[j][:], b_q[:, j:j + 1]).then_inc(idx_made, 1)
            dve.wait_ge(f_rows_loaded, 48)

            def weigh(i, src, ln):
                dve.wait_ge(f_rooted, i + 1)
                dve.scalar_tensor_tensor(hn_row[i % NJ][:], src, f_rs[:, i:i + 1], ln,
                                         ALU.mult, ALU.mult).then_inc(hn_made, 1)

            for j in range(NJ):
                weigh(j, h_sel[j][:], ln1_row[:])

            def h_low(i):
                dve.wait_ge(hT_hi_done, i + 1)
                low(hT_lo[:, i % NJ].rearrange("p c t -> p (c t)"), (f_T, f_T2)[i % NJ][:],
                    hT_hi[:, i % NJ].rearrange("p c t -> p (c t)")).then_inc(hT_lo_done, 1)

            for j in range(NJ):
                h_low(j)
            split_low(2)
            for j in range(NJ):
                dve.tensor_tensor_reduce(x2_row[j][:], h_sel[j][:], wr2_row[:], 1.0, 0.0, ALU.mult,
                                         ALU.add, accum_out=g_dot[:, j:j + 1]).then_inc(g_dotted, 1)
            split_low(3)

            def bias(r, i):
                dve.wait_ge(f_projected, r + 1)
                dve.wait_ge(bias_loaded[i % 2], 16 * (i // 2 + 1))
                dve.tensor_tensor(proj[r % 2][:], f_proj[r % 2][:], bias_row[i % 2][:],
                                  ALU.add).then_inc(f_biased, 1)

            def rotate(r, k):
                j = r % NJ
                q = proj[r % 2][:].rearrange("p (h a d) -> p h a d", h=QUAD, a=2)
                s = by_sin[:].rearrange("p (h a d) -> p h a d", h=QUAD, a=2)
                dve.wait_ge(gathered_rope[j], 16)
                dve.wait_ge(f_biased, r + 1)
                wait(dve, f_roped, k)
                for a in range(2):
                    sin = rope[j][:, HD + a * (HD // 2):HD + (a + 1) * (HD // 2)]
                    last = dve.tensor_tensor(s[:, :, a, :], q[:, :, 1 - a, :],
                                             sin.unsqueeze(1).to_broadcast([P, QUAD, HD // 2]), ALU.mult)
                last.then_inc(sin_done, 1)

            def add_rotated(r, k):
                j = r % NJ
                dve.wait_ge(sin_done, k + 1)
                dve.wait_ge(cos_done, k + 1)
                if NJ <= k < NJ * (FK + 1):
                    dve.wait_ge(fk_turned, k - NJ + 1)
                elif k >= NJ * (FK + 1):
                    dve.wait_ge(fq_turned, k - NJ * (FK + 1) + 1)
                dve.tensor_tensor(turned[j][:], by_cos[:], by_sin[:], ALU.add).then_inc(f_roped, 1)

            def fk_low(i):
                kp, j = i // NJ, i % NJ
                dve.wait_ge(fk_hi_done, i + 1)
                low(fkT_lo[:, kp * QUAD:(kp + 1) * QUAD, j * P:(j + 1) * P],
                    (f_T, f_T2)[j][:].rearrange("p (h t) -> p h t", h=QUAD),
                    fkT_hi[:, kp * QUAD:(kp + 1) * QUAD, j * P:(j + 1) * P]).then_inc(fk_lo_done, 1)

            def rope_number(o, j):
                kind, n = PROJECTIONS[o]
                return NJ * (n if kind == "k" else FK + n) + j

            def take_rows(o, j):
                kind, n = PROJECTIONS[o]
                if o > 0 and PROJECTIONS[o - 1][0] == "v":
                    dve.wait_ge(fv_hi_done, NJ * PROJECTIONS[o - 1][1] + j + 1)
                    dve.wait_ge(fv_lo_done, NJ * PROJECTIONS[o - 1][1] + j + 1)
                bias(NJ * o + j, o)
                if kind != "v":
                    rotate(NJ * o + j, rope_number(o, j))

            def finish_rows(o, j):
                if PROJECTIONS[o][0] != "v":
                    add_rotated(NJ * o + j, rope_number(o, j))

            for o in range(AHEAD):
                for j in range(NJ):
                    take_rows(o, j)
                    if o > 0 and PROJECTIONS[o - 1][0] == "k":
                        fk_low(NJ * PROJECTIONS[o - 1][1] + j)
                    finish_rows(o, j)
                if o > 0:
                    split_low(NSLOT + o - 1)

            def probs_low(n):
                for i, (hi, lo, bank) in enumerate((
                        (fp0_hi[:, 0:2, :], fp0_lo[:, 0:2, :], f_T),
                        (fp0_hi[:, 2:4, :], fp0_lo[:, 2:4, :], f_T2),
                        (fp1_hi[:], fp1_lo[:], f_S))):
                    dve.wait_ge(fp_hi_done, 3 * n + i + 1)
                    low(lo.rearrange("p h t -> p (h t)"), bank[:],
                        hi.rearrange("p h t -> p (h t)")).then_inc(fp_lo_done, 1)

            def mixed_low(n):
                for g in range(2):
                    dve.wait_ge(fo_hi_done, 2 * n + g + 1)
                    low(foT_lo[:, 2 * g:2 * g + 2, :].rearrange("p h t -> p (h t)"), (f_O, f_T)[g][:],
                        foT_hi[:, 2 * g:2 * g + 2, :].rearrange("p h t -> p (h t)")
                        ).then_inc(fo_lo_done, 1)

            for n in range(FQ):
                if n < FQ - 1:
                    o = PROJECTIONS.index(("q", n + 1))
                if n == 0:
                    take_rows(o, 0)
                for j in range(NJ):
                    dve.wait_ge(fq_hi_done, NJ * n + j + 1)
                    low(fqT_lo[:, j].rearrange("p h t -> p (h t)"), (f_T, f_T2)[j][:],
                        fqT_hi[:, j].rearrange("p h t -> p (h t)")).then_inc(fq_lo_done, 1)
                if 0 < n < FQ - 1:
                    take_rows(o, 0)
                if n > 0:
                    probs_low(n - 1)
                if n < FQ - 1:
                    finish_rows(o, 0)
                    take_rows(o, 1)
                    finish_rows(o, 1)
                if n > 0:
                    mixed_low(n - 1)
                if 0 < n < FQ - 1:
                    split_low(split_early(n))
                for i, (heads, col) in enumerate(SCORE_TILES):
                    width = W // heads
                    bank = (f_S, f_T2, f_T)[i]
                    dve.wait_ge(f_scored, 3 * n + i + 1)
                    wait(dve, fp_turned, 3 * n)
                    dve.scalar_tensor_tensor(
                        fs[i][:].rearrange("p (h t) -> p h t", h=heads),
                        bank[:].rearrange("p (h t) -> p h t", h=heads), SCALE,
                        causal[:, 2 * P - width:2 * P].unsqueeze(1).to_broadcast([P, heads, width]),
                        ALU.mult, ALU.add).then_inc(f_masked, 1)
                    dve.wait_ge(f_masked, 3 * n + i + 1)
                    dve.tensor_reduce(f_max[:, col:col + heads],
                                      fs[i][:].rearrange("p (h t) -> p h t", h=heads),
                                      AX.X, ALU.max, negate=True).then_inc(f_maxed, 1)
                if n == 0:
                    take_rows(PROJECTIONS.index(("v", 1)), 0)
                    split_low(split_early(n))
                    take_rows(PROJECTIONS.index(("v", 1)), 1)
                else:
                    for piece in split_late(n):
                        split_low(piece)
                for i, (heads, col) in enumerate(SCORE_TILES):
                    dve.wait_ge(f_exped, 3 * n + i + 1)
                    dve.reciprocal(f_inv[:, col:col + heads],
                                   f_sum[:, col:col + heads]).then_inc(f_inverted, 1)
                if n == 0:
                    for piece in split_late(n):
                        split_low(piece)
            split_low(split_early(FQ - 1))
            probs_low(FQ - 1)
            mixed_low(FQ - 1)
            split_low(P_MLP + 2)

            def add_attention(j):
                dve.wait_ge(attn_done, NJ * (FQ - 1) + j + 1)
                dve.tensor_tensor(x2_row[j][:], f_W[j][:], h_sel[j][:], ALU.add).then_inc(x2_made, 1)

            add_attention(0)
            weigh(NJ, x2_row[0][:], ln2_row[:])
            add_attention(1)
            h_low(NJ)
            weigh(NJ + 1, x2_row[1][:], ln2_row[:])
            h_low(NJ + 1)
            split_low(P_MLP + 3)
            dve.wait_ge(g_exped, 1)
            dve.tensor_scalar(g_one[:], g_exp[:], 1.0, None, ALU.add).then_inc(g_plus, 1)
            dve.wait_ge(g_plus, 1)
            dve.reciprocal(gate[:], g_one[:]).then_inc(g_made, 1)
            for m in range(FI):
                for j in range(NJ):
                    dve.wait_ge(tanh_done, NJ * m + j + 1)
                    wait(dve, act_turned, NJ * (m - 1) + j + 1)
                    dve.scalar_tensor_tensor(act_row[j][:], tanh_row[j][:], 1.0, f_proj[j][:],
                                             ALU.add, ALU.mult).then_inc(silu_done, 1)
                    dve.wait_ge(silu_done, NJ * m + j + 1)
                    dve.wait_ge(upped, NJ * m + j + 1)
                    dve.scalar_tensor_tensor(act_row[j][:], act_row[j][:], 0.5, (f_S, f_O)[j][:],
                                             ALU.mult, ALU.mult).then_inc(act_done, 1)
                for piece in split_mlp(m):
                    split_low(piece)
                for j in range(NJ):
                    dve.wait_ge(aT_hi_done, NJ * m + j + 1)
                    low(fqT_lo[:, j].rearrange("p h t -> p (h t)"), (f_T, f_T2)[j][:],
                        fqT_hi[:, j].rearrange("p h t -> p (h t)")).then_inc(aT_lo_done, 1)
            for j in range(NJ):
                dve.wait_ge(mlp_done, NJ * (FI - 1) + j + 1)
                dve.tensor_tensor(attn_row[j][:], attn_row[j][:], f_W[j][:], ALU.add).then_inc(delta_made, 1)
                dve.wait_ge(delta_made, j + 1)
                dve.wait_ge(g_made, 1)
                dve.wait_ge(gathered_base, 16 * NJ)
                dve.scalar_tensor_tensor(final[j][:], attn_row[j][:], gate[:, j:j + 1], base[j][:],
                                         ALU.mult, ALU.add).then_inc(final_made, 1)

        @block.tensor
        def _(pe):
            def product(dst, left, right, start, stop):
                pe.matmul(dst, left[0], right[0], start=start, stop=False)
                pe.matmul(dst, left[0], right[1], start=False, stop=False)
                return pe.matmul(dst, left[1], right[0], start=False, stop=stop)

            def turn(dst, src, n=4):
                for i in range(n):
                    last = pe.transpose(dst[:, i * P:(i + 1) * P], src[:, i * P:(i + 1) * P], ident[:])
                return last

            pe.wait_ge(const_made, 13)

            def turn_c(b, par, nth):
                pe.wait_ge(cx_loaded[par], 16 * nth)
                wait(pe, c_lo, b)
                turn(b_c, cx[par]).then_inc(c_turned, 1)

            def turn_k(b):
                pe.wait_ge(k_normed, b + 1)
                wait(pe, k_weighted, b)
                turn(b_kT, k_row[:].rearrange("p h d -> p (h d)")).then_inc(k_turned, 1)

            def turn_x(b):
                pe.wait_ge(x_normed, b + 1)
                wait(pe, xT_lo_done, b)
                turn(b_xT, xn).then_inc(x_turned, 1)

            def kv_project(bank, par, w_hi_, w_lo_, split_at=None):
                for c in range(DC):
                    if split_at is not None:
                        pe.wait_ge(kv_w_lo, split_at + c + 1)
                    last = product(bank[:], (cT_hi[par][:, c, :], cT_lo[par][:, c, :]),
                                   (w_hi_[:, c, :], w_lo_[:, c, :]), c == 0, c == DC - 1)
                return last

            def kv_batch(b, par, next_nth, first=False, last=False):
                if not last:
                    turn_c(b + 1, 1 - par, next_nth)
                pe.wait_ge(c_lo, b + 1)
                wait(pe, k_biased, b)
                kv_project(b_k, par, wk_hi, wk_lo, 0 if first else None).then_inc(k_projected, 1)
                if not first:
                    turn_k(b - 1)
                wait(pe, v_biased, b)
                kv_project(b_v, par, wv_hi, wv_lo, DC if first else None).then_inc(v_projected, 1)
                if last:
                    turn_x(0)

            turn_c(0, 0, 1)
            kv_batch(0, 0, 1, first=True)
            with pe.Fori(0, NB // 2 - 1) as g:
                kv_batch(2 * g + 1, 1, g + 2)
                kv_batch(2 * g + 2, 0, g + 2)
            kv_batch(NB - 1, 1, None, last=True)


            def project_q(t, b, quad):
                pe.wait_ge(xT_lo_done, b + 1)
                wait(pe, q_biased, t)
                for c in range(DC):
                    last = product(b_q[:], (xT_hi[:, c, :], xT_lo[:, c, :]),
                                   (wq_hi[:, c, quad * W:(quad + 1) * W], wq_lo[:, c, quad * W:(quad + 1) * W]),
                                   c == 0, c == DC - 1)
                last.then_inc(q_projected, 1)

            def turn_q(t):
                pe.wait_ge(q_normed, t + 1)
                wait(pe, qT_lo_done, t)
                turn(b_qT, q_nrm[:].rearrange("p h d -> p (h d)")).then_inc(q_turned, 1)

            def score_quad(t, b, quad):
                pe.wait_ge(qT_lo_done, t + 1)
                if quad == 0:
                    pe.wait_ge(kT_lo_done, b + 1)
                wait(pe, s_summed, t)
                keys = kT[:, quad, :, :].rearrange("p a s -> p (a s)")
                for h in range(QUAD):
                    hs = slice(h * P, (h + 1) * P)
                    pe.matmul(b_scores[:, h, :], qT_hi[:, hs], keys, start=True, stop=False)
                    last = pe.matmul(b_scores[:, h, :], qT_lo[:, hs], keys, start=False, stop=True)
                last.then_inc(scored, 1)

            def turn_p(t):
                pe.wait_ge(p_normed, t + 1)
                wait(pe, pT_lo_done, t)
                turn(b_pT, p_row[:].rearrange("p h t -> p (h t)")).then_inc(p_turned, 1)

            def mix(t, b, quad):
                pe.wait_ge(pT_lo_done, t + 1)
                if quad == 0:
                    pe.wait_ge(v_lo_done, b + 1)
                wait(pe, oT_lo_done, t)
                vs = slice(quad * HD, (quad + 1) * HD)
                product(b_o[:], (v_hi[:, vs], v_lo[:, vs]), (pT_hi[:], pT_lo[:]), True, True
                        ).then_inc(mixed, 1)

            def add_y(t, b, quad):
                pe.wait_ge(oT_lo_done, t + 1)
                if quad == 0:
                    wait(pe, x1_made, b)
                for h in range(QUAD):
                    hs = slice(h * P, (h + 1) * P)
                    head = quad * QUAD + h
                    last = product(b_y[:], (oT_hi[:, hs], oT_lo[:, hs]),
                                   (wo_hi[:, head, :], wo_lo[:, head, :]),
                                   quad == 0 and h == 0, quad == NQUAD - 1 and h == QUAD - 1)
                last.then_inc(y_added, 1)

            def spread_scores(b, rows_turned):
                pe.wait_ge(score_spread, b + 1)
                pe.wait_ge(xT_lo_done, rows_turned)
                pe.transpose(b_rank[:, 0:S], score_wide[:], ident[:]).then_inc(score_turned, 1)

            pe.wait_ge(w_lo, 2 * QUAD)
            pe.wait_ge(k_biased, NB)
            project_q(0, 0, 0)
            turn_k(NB - 1)
            pe.wait_ge(w_hi, 2 * NB)
            pe.wait_ge(w_lo, 2 * NB)
            pe.wait_ge(k_weighted, NB)
            pe.wait_ge(v_biased, NB)

            def attend(b, first, last):
                for i in range(NQUAD):
                    t = NQUAD * b + i
                    turn_q(t)
                    if not (last and i == NQUAD - 1):
                        project_q(t + 1, b if i < NQUAD - 1 else b + 1, (i + 1) % NQUAD)
                    score_quad(t, b, i)
                    if not (first and i == 0):
                        turn_p(t - 1)
                    if i == 2 and not last:
                        turn_x(b + 1)
                    if i == NQUAD - 1 and not first:
                        spread_scores(b - 1, NB if last else b + 2)
                    if not (first and i < 2):
                        add_y(t - 2, b if i >= 2 else b - 1, (i - 2) % NQUAD)
                    if not (first and i == 0):
                        mix(t - 1, b if i >= 1 else b - 1, (i - 1) % NQUAD)

            attend(0, True, False)
            with pe.Fori(1, NB - 1) as b:
                attend(b, False, False)
            attend(NB - 1, False, True)
            turn_p(STEPS - 1)
            add_y(STEPS - 2, NB - 1, NQUAD - 2)
            mix(STEPS - 1, NB - 1, NQUAD - 1)
            add_y(STEPS - 1, NB - 1, NQUAD - 1)
            spread_scores(NB - 1, NB)

            pe.wait_ge(picks_made, NB)
            pe.wait_ge(x1_made, NB)
            pe.matmul(b_y[:, 0:NB], later[:], picked[:], start=True, stop=True).then_inc(place_found, 1)
            pe.wait_ge(onehot_made, 1)
            for j in range(NJ):
                last = pe.matmul(b_q[:, j:j + 1],
                                 onehot[:, j * BPJ:(j + 1) * BPJ, :].rearrange("p b s -> p (b s)"),
                                 token[:], start=True, stop=True)
            last.then_inc(rows_found, 1)

            def turn_h(i):
                pe.wait_ge(hn_made, i + 1)
                turn((f_T, f_T2)[i % NJ], hn_row[i % NJ]).then_inc(h_turned, 1)

            for j in range(NJ):
                turn_h(j)

            def piece_ready(n):
                pe.wait_ge(piece_lo_dve, n + 1)
                pe.wait_ge(piece_lo_pool, n + 1)

            def piece_rows(n, c):
                return wp_hi[n % NSLOT][:, c, :], wp_lo[n % NSLOT][:, c, :]

            def project(bank, j, n):
                for c in range(DC):
                    last = product(bank[:], (hT_hi[:, j, c, :], hT_lo[:, j, c, :]), piece_rows(n, c),
                                   c == 0, c == DC - 1)
                return last

            def project_tile(r, n):
                j = r % NJ
                if j == 0:
                    piece_ready(n)
                if r < NJ:
                    pe.wait_ge(hT_lo_done, r + 1)
                if r == 0:
                    pe.wait_ge(idx_made, 2 * NJ)
                wait(pe, f_biased, r - 1)
                project(f_proj[r % 2], j, n).then_inc(f_projected, 1)

            def turn_fk(i):
                j = i % NJ
                pe.wait_ge(f_roped, i + 1)
                if i < NJ:
                    pe.wait_ge(hT_lo_done, i + 1)
                else:
                    pe.wait_ge(fk_lo_done, i - NJ + 1)
                turn((f_T, f_T2)[j], turned[j]).then_inc(fk_turned, 1)

            for o in range(AHEAD):
                for j in range(NJ):
                    project_tile(NJ * o + j, o)
                    if o > 0 and PROJECTIONS[o - 1][0] == "k":
                        turn_fk(NJ * PROJECTIONS[o - 1][1] + j)

            def next_query_rows(n, j):
                project_tile(NJ * PROJECTIONS.index(("q", n + 1)) + j, p_wq(n + 1))

            def turn_queries(n):
                for j in range(NJ):
                    pe.wait_ge(f_roped, NJ * FK + NJ * n + j + 1)
                    if n == 0:
                        pe.wait_ge(fk_lo_done, NJ * FK)
                    else:
                        pe.wait_ge(f_masked, 3 * n)
                    turn((f_T, f_T2)[j], turned[j]).then_inc(fq_turned, 1)

            def score_quad(n):
                pe.wait_ge(fq_lo_done, NJ * n + NJ)
                if n == 0:
                    pe.wait_ge(fk_lo_done, NJ * FK)
                wait(pe, fp_lo_done, 3 * n)
                for h in range(QUAD):
                    g = 2 * n + h // 2
                    last = product(f_S[:, h * P:(h + 1) * P], (fqT_hi[:, 0, h, :], fqT_lo[:, 0, h, :]),
                                   (fkT_hi[:, g, 0:P], fkT_lo[:, g, 0:P]), True, True)
                last.then_inc(f_scored, 1)
                for half_quad in range(2):
                    if half_quad == 1:
                        wait(pe, fo_lo_done, 2 * n)
                    for a in range(2):
                        h, g = 2 * half_quad + a, 2 * n + half_quad
                        last = product((f_T2, f_T)[half_quad][:, a * NSEL:(a + 1) * NSEL],
                                       (fqT_hi[:, 1, h, :], fqT_lo[:, 1, h, :]),
                                       (fkT_hi[:, g, :], fkT_lo[:, g, :]), True, True)
                    last.then_inc(f_scored, 1)

            def turn_probs(n):
                pe.wait_ge(f_normed, 3 * n + 3)
                if n < FQ - 1:
                    pe.wait_ge(fq_lo_done, NJ * (n + 2))
                for half_quad in range(2):
                    bank = (f_T, f_T2)[half_quad]
                    for a in range(2):
                        h = 2 * half_quad + a
                        pe.transpose(bank[:, a * NSEL:a * NSEL + P], fs[0][:, h * P:(h + 1) * P], ident[:])
                        last = pe.transpose(bank[:, a * NSEL + P:(a + 1) * NSEL],
                                            fs[1 + half_quad][:, a * NSEL:a * NSEL + P], ident[:])
                    last.then_inc(fp_turned, 1)
                for h in range(QUAD):
                    last = pe.transpose(f_S[:, h * P:(h + 1) * P],
                                        fs[1 + h // 2][:, (h % 2) * NSEL + P:(h % 2 + 1) * NSEL], ident[:])
                last.then_inc(fp_turned, 1)

            def mix_quad(n):
                pe.wait_ge(fp_lo_done, 3 * n + 3)
                if n == 0:
                    pe.wait_ge(fv_lo_done, NJ * FK)
                wait(pe, fo_lo_done, 2 * n)
                for g in range(2):
                    bank = (f_O, f_T)[g]
                    vs = slice((2 * n + g) * HD, (2 * n + g + 1) * HD)
                    product(bank[:], (fv_hi[:, 0, vs], fv_lo[:, 0, vs]),
                            (fp0_hi[:, 2 * g:2 * g + 2, :].rearrange("p h t -> p (h t)"),
                             fp0_lo[:, 2 * g:2 * g + 2, :].rearrange("p h t -> p (h t)")), True, False)
                    product(bank[:].rearrange("p (h t) -> p h t", h=2)[:, :, P:NSEL],
                            (fv_hi[:, 1, vs], fv_lo[:, 1, vs]),
                            (fp1_hi[:, 2 * g:2 * g + 2, :], fp1_lo[:, 2 * g:2 * g + 2, :]), False, True
                            ).then_inc(f_mixed, 1)

            def attend_out(n):
                piece_ready(p_wo(n))
                pe.wait_ge(fo_lo_done, 2 * n + 2)
                for j in range(NJ):
                    for h in range(QUAD):
                        hs = slice(j * P, (j + 1) * P)
                        last = product(f_W[j][:], (foT_hi[:, h, hs], foT_lo[:, h, hs]),
                                       piece_rows(p_wo(n), h),
                                       n == 0 and h == 0, n == FQ - 1 and h == QUAD - 1)
                    last.then_inc(attn_done, 1)

            next_query_rows(0, 0)
            for n in range(FQ):
                turn_queries(n)
                if 0 < n < FQ - 1:
                    next_query_rows(n, 0)
                if n > 0:
                    turn_probs(n - 1)
                if n < FQ - 1:
                    next_query_rows(n, 1)
                if n > 0:
                    mix_quad(n - 1)
                score_quad(n)
                if n == 0:
                    for j in range(NJ):
                        project_tile(NJ * PROJECTIONS.index(("v", 1)) + j, ATTENTION.index(("v", 1)))
                else:
                    attend_out(n - 1)
            turn_probs(FQ - 1)
            mix_quad(FQ - 1)
            attend_out(FQ - 1)

            def gate_rows(m, j):
                piece_ready(p_gate(m))
                if m == 0:
                    pe.wait_ge(hT_lo_done, NJ + j + 1)
                wait(pe, silu_done, NJ * (m - 1) + j + 1)
                project(f_proj[j], j, p_gate(m)).then_inc(gated, 1)

            def up_rows(m, j):
                piece_ready(p_up(m))
                wait(pe, act_done, NJ * (m - 1) + j + 1)
                project((f_S, f_O)[j], j, p_up(m)).then_inc(upped, 1)

            turn_h(NJ)
            gate_rows(0, 0)
            turn_h(NJ + 1)
            up_rows(0, 0)
            gate_rows(0, 1)
            up_rows(0, 1)
            for m in range(FI):
                if m < FI - 1:
                    for j in range(NJ):
                        gate_rows(m + 1, j)
                for j in range(NJ):
                    pe.wait_ge(act_done, NJ * m + j + 1)
                    wait(pe, aT_lo_done, NJ * (m - 1) + j + 1)
                    turn((f_T, f_T2)[j], act_row[j]).then_inc(act_turned, 1)
                if m < FI - 1:
                    for j in range(NJ):
                        up_rows(m + 1, j)
                piece_ready(p_down(m))
                if m == 0:
                    pe.wait_ge(attn_copied, NJ)
                for j in range(NJ):
                    pe.wait_ge(aT_lo_done, NJ * m + j + 1)
                    for c in range(4):
                        last = product(f_W[j][:], (fqT_hi[:, j, c, :], fqT_lo[:, j, c, :]),
                                       piece_rows(p_down(m), c),
                                       m == 0 and c == 0, m == FI - 1 and c == 3)
                    last.then_inc(mlp_done, 1)


_INS = ['x', 'ctx_2048', 'mask_1xSxS2_ff0', 'L0_xattn_Wq', 'L0_xattn_bq', 'L0_xattn_Wk', 'L0_xattn_bk',
        'L0_xattn_Wv', 'L0_xattn_bv', 'L0_xattn_Wo', 'L0_xattn_qn_w', 'L0_xattn_kn_w', 'L0_ffn_w_router',
        'L0_ffn_wq', 'L0_ffn_bq', 'L0_ffn_wk', 'L0_ffn_bk', 'L0_ffn_wv', 'L0_ffn_bv', 'L0_ffn_wo',
        'L0_ffn_w_gate', 'L0_ffn_w_up', 'L0_ffn_w_down', 'L0_ffn_ln1_w', 'L0_ffn_ln2_w']


def _rope_table(positions, head_dim, theta=10000.0):
    import numpy as np
    inv = (1.0 / np.float32(theta) ** (np.arange(0, head_dim, 2, dtype=np.float32) / np.float32(head_dim)))
    ang = np.arange(positions, dtype=np.float32)[:, None] * inv.astype(np.float32)
    c, s = np.cos(ang), np.sin(ang)
    return np.concatenate([c, c, -s, s], axis=1).astype(np.float32)


def kernel(**inputs):
    import numpy as _np
    import concourse.bacc as _bacc
    from concourse import mybir as _mybir
    from concourse.bass_utils import run_bass_kernel_spmd as _run

    nc = _bacc.Bacc("TRN2", target_bir_lowering=False, num_devices=1)
    arrays, args = {}, []
    named = [(n, _np.ascontiguousarray(inputs[n])) for n in _INS]
    batches, seq, _ = named[0][1].shape
    pick = seq // 8
    blocks = batches * pick // 128
    slot = _np.arange(blocks)[None, :] * 128 + _np.arange(128)[:, None]
    named += [("rope_table", _rope_table(seq, 128)),
              ("slot_base", (slot // pick * seq).astype(_np.float32))]
    for name, a in named:
        arrays[f"in_{name}_dram"] = a
        args.append(nc.dram_tensor(f"in_{name}_dram", a.shape, _mybir.dt.from_np(a.dtype), kind="ExternalInput").ap())
    out = nc.dram_tensor("out_0_dram", (batches, seq, 512), _mybir.dt.float32, kind="ExternalOutput").ap()
    xattn_then_routed_ffn(nc, *args, out)
    r = _run(nc, [arrays], core_ids=[0])
    return r.results[0]["out_0_dram"]
```

```python
import concourse.bass as bass
from concourse import mybir
from contextlib import ExitStack


def xattn_then_routed_ffn(
    nc: bass.Bass,
    x: bass.AP,
    context: bass.AP,
    attn_mask: bass.AP,
    Wq: bass.AP,
    bq: bass.AP,
    Wk: bass.AP,
    bk: bass.AP,
    Wv: bass.AP,
    bv: bass.AP,
    Wo: bass.AP,
    qn_w: bass.AP,
    kn_w: bass.AP,
    w_router: bass.AP,
    ffn_wq: bass.AP,
    ffn_bq: bass.AP,
    ffn_wk: bass.AP,
    ffn_bk: bass.AP,
    ffn_wv: bass.AP,
    ffn_bv: bass.AP,
    ffn_wo: bass.AP,
    w_gate: bass.AP,
    w_up: bass.AP,
    w_down: bass.AP,
    ln1_w: bass.AP,
    ln2_w: bass.AP,
    rope_table: bass.AP,
    slot_base: bass.AP,
    out: bass.AP,
):
    fp32 = mybir.dt.float32
    f32r = mybir.dt.float32r
    bf16 = mybir.dt.bfloat16
    u32 = mybir.dt.uint32
    ALU = mybir.AluOpType
    ACT = mybir.ActivationFunctionType
    AX = mybir.AxisListType

    P = 128
    NB, S, D = x.shape
    DC = D // P
    HD = qn_w.shape[0]
    NH = Wq.shape[1] // HD
    NKV = Wk.shape[1] // HD
    QUAD = NH // NKV
    NQUAD = NKV
    STEPS = NB * NQUAD
    W = QUAD * HD
    PICK = S // 8
    NSEL = NB * PICK
    NJ = NSEL // P
    BPJ = NB // NJ
    SCALE = float(HD) ** -0.5
    EPS_LN, EPS_RMS = 1e-5, 1e-6
    MASKED = -3.0e38
    FH = ffn_wq.shape[1] // HD
    FKV = ffn_wk.shape[1] // HD
    FQ = FH // QUAD
    FK = FKV // QUAD
    FI = w_gate.shape[1] // W
    NSLOT = 4

    x_rows = x.rearrange("b s d -> (b s) d")
    ctx_rows = context.rearrange("b s d -> (b s) d")
    out_rows = out.rearrange("b s d -> (b s) d")
    k_store = nc.dram_tensor("k_store", [NB * P, NKV * S], fp32, kind="Internal").ap()
    v_store = nc.dram_tensor("v_store", [NB * P, NKV * HD], fp32, kind="Internal").ap()
    h_store = nc.dram_tensor("h_store", [NB * S, D], fp32, kind="Internal").ap()

    def chunked(w):
        return w.rearrange("(c p) n -> p c n", p=P)

    def columns(w, n):
        return chunked(w)[:, :, n * W:(n + 1) * W]

    def rows(w, g):
        return chunked(w[g * 4 * P:(g + 1) * 4 * P, :])

    ATTENTION = [("k", 0), ("v", 0), ("k", 1), ("q", 0), ("q", 1), ("v", 1), ("q", 2), ("o", 0),
                 ("q", 3), ("o", 1), ("o", 2), ("o", 3)]
    MATRIX = {"k": ffn_wk, "v": ffn_wv, "q": ffn_wq}
    PIECES = [rows(ffn_wo, n) if kind == "o" else columns(MATRIX[kind], n) for kind, n in ATTENTION]
    PIECES += [columns(w_gate, 0), columns(w_up, 0)]
    for m in range(FI - 1):
        PIECES += [columns(w_gate, m + 1), columns(w_up, m + 1), rows(w_down, m)]
    PIECES += [rows(w_down, FI - 1)]
    NP = len(PIECES)
    PROJECTIONS = [piece for piece in ATTENTION if piece[0] != "o"]
    AHEAD = PROJECTIONS.index(("q", 0)) + 1
    TILES = [(o, j) for j in range(NJ) for o in range(AHEAD)]
    TILES += [(o, j) for o in range(AHEAD, len(PROJECTIONS)) for j in range(NJ)]
    ROPED = [(o, j) for o, j in TILES if PROJECTIONS[o][0] != "v"]
    KEYS = [(PROJECTIONS[o][1], j) for o, j in TILES if PROJECTIONS[o][0] == "k"]
    BIAS_USES = list(range(AHEAD)) * NJ + list(range(AHEAD, len(PROJECTIONS)))

    def bias_use(o, j):
        return AHEAD * j + o if o < AHEAD else AHEAD * (NJ - 1) + o

    def p_wq(n):
        return ATTENTION.index(("q", n))

    def p_wo(n):
        return ATTENTION.index(("o", n))

    P_MLP = len(ATTENTION)

    def p_gate(m):
        return P_MLP if m == 0 else P_MLP + 3 * m - 1

    def p_up(m):
        return p_gate(m) + 1

    def p_down(m):
        return P_MLP + 3 * m + 4 if m < FI - 1 else NP - 1

    RAW_OF = [n % 2 if n < NSLOT else (n - 2) % 3 for n in range(NP)]
    NTH_RAW = [RAW_OF[:n + 1].count(RAW_OF[n]) for n in range(NP)]
    RAW_BEFORE = [max([k for k in range(n) if RAW_OF[k] == RAW_OF[n]] + [-1]) for n in range(NP)]

    ctx = ExitStack()
    with ctx:
        def sem(name):
            return ctx.enter_context(nc.semaphore(name))

        def sb_in(stack, name, shape, dt=fp32):
            return stack.enter_context(nc.sbuf_tensor(name, shape, dt))

        def split_in(stack, name, shape):
            return (sb_in(stack, name + "_hi", shape, f32r), sb_in(stack, name + "_lo", shape, f32r))

        ident = sb_in(ctx, "ident", [P, P])
        earlier = sb_in(ctx, "earlier", [P, P])
        later = sb_in(ctx, "later", [P, P])
        causal = sb_in(ctx, "causal", [P, 2 * P])
        slots = sb_in(ctx, "slots", [P, PICK])
        token = sb_in(ctx, "token", [P, 1])
        half = sb_in(ctx, "half", [P, QUAD])
        eps_head = sb_in(ctx, "eps_head", [P, QUAD])
        eps_ln = sb_in(ctx, "eps_ln", [P, 1])
        qw = sb_in(ctx, "qw", [P, 1])
        kw = sb_in(ctx, "kw", [P, 1])
        base_row = sb_in(ctx, "base_row", [P, NJ])
        picked = sb_in(ctx, "picked", [P, NB])
        bn = sb_in(ctx, "bn", [P, 6])
        mv = sb_in(ctx, "mv", [P, 2])
        rstd = sb_in(ctx, "rstd", [P, 1])
        row_idx = [sb_in(ctx, f"row_idx{j}", [P, 1], u32) for j in range(NJ)]
        pos_idx = [sb_in(ctx, f"pos_idx{j}", [P, 1], u32) for j in range(NJ)]
        f_ss = sb_in(ctx, "f_ss", [P, 2 * NJ])
        f_ms = sb_in(ctx, "f_ms", [P, 2 * NJ])
        f_rs = sb_in(ctx, "f_rs", [P, 2 * NJ])
        raw = [sb_in(ctx, f"raw{i}", [P, 4, W]) for i in range(2)]

        wq_place = ExitStack()
        wq_hi, wq_lo = split_in(wq_place, "wq", [P, DC, NH * HD])
        wo_place = ExitStack()
        wo_hi, wo_lo = split_in(wo_place, "wo", [P, NH, D])

        with ExitStack() as st:
            cx = [sb_in(st, f"cx{i}", [P, D]) for i in range(2)]
            cT_hi, cT_lo = zip(*[split_in(st, f"cT{i}", [P, DC, P]) for i in range(2)])
            wq_raw = sb_in(st, "wq_raw", [P, DC, HD])
            wo_raw = sb_in(st, "wo_raw", [P, D])
            wk_hi, wk_lo = split_in(st, "wk", [P, DC, W])
            wv_hi, wv_lo = split_in(st, "wv", [P, DC, W])
            k_row = sb_in(st, "k_row", [P, NKV, HD])
            k_out = sb_in(st, "k_out", [P, NKV * S])
            v_out = sb_in(st, "v_out", [P, NKV * HD])
            bk_row = sb_in(st, "bk_row", [P, NKV * HD])
            bv_row = sb_in(st, "bv_row", [P, NKV * HD])
            k_sq = sb_in(st, "k_sq", [P, NKV, HD], bf16)
            k_ss = sb_in(st, "k_ss", [P, NKV])
            k_rs = sb_in(st, "k_rs", [P, NKV])

        with ExitStack() as st:
            xr = sb_in(st, "xr", [P, D])
            xn = sb_in(st, "xn", [P, D])
            xT_hi, xT_lo = split_in(st, "xT", [P, DC, P])
            k_raw = sb_in(st, "k_raw", [P, NKV * S])
            v_raw = sb_in(st, "v_raw", [P, NKV * HD])
            q_row = sb_in(st, "q_row", [P, QUAD, HD])
            q_nrm = sb_in(st, "q_nrm", [P, QUAD, HD])
            kT = sb_in(st, "kT", [P, NKV, 2, S], f32r)
            v_hi, v_lo = split_in(st, "v", [P, NKV * HD])
            bq_row = sb_in(st, "bq_row", [P, NH * HD])
            qT_hi, qT_lo = split_in(st, "qT", [P, W])
            s_row = sb_in(st, "s_row", [P, QUAD, S])
            p_row = sb_in(st, "p_row", [P, QUAD, S])
            pT_hi, pT_lo = split_in(st, "pT", [P, W])
            x_res = sb_in(st, "x_res", [P, D])
            mask = sb_in(st, "mask", [P, S])
            sq_junk = sb_in(st, "sq_junk", [P, QUAD, HD], bf16)
            q_ss = sb_in(st, "q_ss", [P, QUAD])
            q_rs = sb_in(st, "q_rs", [P, QUAD])
            neg_max = sb_in(st, "neg_max", [P, QUAD])
            p_sum = sb_in(st, "p_sum", [P, QUAD])
            p_inv = sb_in(st, "p_inv", [P, QUAD])
            score_wide = sb_in(st, "score_wide", [P, S])
            oT_hi, oT_lo = split_in(st, "oT", [P, W])
            x1 = sb_in(st, "x1", [P, D])
            h_row = sb_in(st, "h_row", [P, D])
            wr_row = sb_in(st, "wr_row", [P, D])
            dot_junk = sb_in(st, "dot_junk", [P, D], bf16)
            rank_junk = sb_in(st, "rank_junk", [P, 2, S], bf16)
            bn1 = sb_in(st, "bn1", [P, 6])
            mv1 = sb_in(st, "mv1", [P, 2])
            rstd1 = sb_in(st, "rstd1", [P, 1])
            score = sb_in(st, "score", [P, 1])
            above = sb_in(st, "above", [P, 1])
            tied = sb_in(st, "tied", [P, 1])
        wo_place.close()
        wq_place.close()

        with ExitStack() as st:
            wp_hi = [sb_in(st, f"wp_hi{i}", [P, 4, W], f32r) for i in range(NSLOT)]
            wp_lo = [sb_in(st, f"wp_lo{i}", [P, 4, W], f32r) for i in range(NSLOT)]
            raw.append(sb_in(st, "raw2", [P, 4, W]))
            hT_hi, hT_lo = split_in(st, "hT", [P, NJ, DC, P])
            fkT_hi, fkT_lo = split_in(st, "fkT", [P, FKV, NSEL])
            fv_hi, fv_lo = split_in(st, "fv", [P, NJ, FKV * HD])
            fqT_hi, fqT_lo = split_in(st, "fqT", [P, NJ, QUAD, P])
            foT_hi, foT_lo = split_in(st, "foT", [P, QUAD, NSEL])
            h_sel = [sb_in(st, "h_sel0", [P, D])]
            hn_row = [sb_in(st, "hn_row0", [P, D])]
            bias_row = [sb_in(st, f"bias_row{i}", [P, W]) for i in range(2)]
            ln1_row = sb_in(st, "ln1_row", [P, D])
            rope = [sb_in(st, "rope0", [P, 4 * (HD // 2)])]
            onehot = sb_in(st, "onehot", [P, NB, PICK])
            proj = [sb_in(st, f"proj{i}", [P, W]) for i in range(2)]
            turned = [sb_in(st, f"turned{j}", [P, W]) for j in range(NJ)]
            by_cos = sb_in(st, "by_cos", [P, W])
            by_sin = sb_in(st, "by_sin", [P, W])
            h_sel.append(sb_in(st, "h_sel1", [P, D]))
            hn_row.append(sb_in(st, "hn_row1", [P, D]))
            rope.append(sb_in(st, "rope1", [P, 4 * (HD // 2)]))
            fp0_hi, fp0_lo = split_in(st, "fp0", [P, QUAD, NSEL])
            fp1_hi, fp1_lo = split_in(st, "fp1", [P, QUAD, P])
            fs = [sb_in(st, f"fs{i}", [P, W]) for i in range(3)]
            x2_row = [sb_in(st, f"x2_row{j}", [P, D]) for j in range(NJ)]
            ln2_row = sb_in(st, "ln2_row", [P, D])
            wr2_row = sb_in(st, "wr2_row", [P, D])
            f_max = sb_in(st, "f_max", [P, 8])
            f_sum = sb_in(st, "f_sum", [P, 8])
            f_inv = sb_in(st, "f_inv", [P, 8])
            g_dot = sb_in(st, "g_dot", [P, NJ])
            g_exp = sb_in(st, "g_exp", [P, NJ])
            g_one = sb_in(st, "g_one", [P, NJ])
            gate = sb_in(st, "gate", [P, NJ])
        act_row = turned
        tanh_row = proj
        final = hn_row
        attn_row = h_sel
        base = [by_cos, by_sin]

        banks = {n: ctx.enter_context(nc.psum_tensor(n, [P, W], fp32))
                 for n in ("b_q", "b_qT", "b_pT", "b_o", "b_y", "b_xT")}
        b_q, b_qT, b_pT, b_o, b_y, b_xT = banks.values()
        b_scores = ctx.enter_context(nc.psum_tensor("b_scores", [P, QUAD, 2 * S], fp32))
        b_s, b_s2 = [b_scores[:, i * QUAD // 2:(i + 1) * QUAD // 2, :].rearrange("p h t -> p (h t)")
                     for i in range(2)]
        b_rank = b_xT
        b_c, b_k, b_v, b_kT = b_xT, b_q, b_s, b_qT
        f_proj = [b_q, b_y]
        f_T, f_T2, f_S, f_O = b_qT, b_pT, b_s, b_o
        f_W = [b_xT, b_s2]

        const_made = sem("const_made")
        const_loaded = sem("const_loaded")
        kw_scaled = sem("kw_scaled")
        wk_loaded = [sem(f"wk_loaded{i}") for i in range(2)]
        wv_loaded = [sem("wv_loaded")]
        kv_w_hi = sem("kv_w_hi")
        kv_w_lo = sem("kv_w_lo")
        kv_bias_loaded = sem("kv_bias_loaded")
        cx_loaded = [sem(f"cx_loaded{i}") for i in range(2)]
        c_turned = sem("c_turned")
        c_hi = sem("c_hi")
        c_lo = sem("c_lo")
        k_projected = sem("k_projected")
        v_projected = sem("v_projected")
        k_biased = sem("k_biased")
        v_biased = sem("v_biased")
        k_squared = sem("k_squared")
        k_summed = sem("k_summed")
        k_rooted = sem("k_rooted")
        k_normed = sem("k_normed")
        k_turned = sem("k_turned")
        k_weighted = sem("k_weighted")
        k_stored = sem("k_stored")
        v_stored = sem("v_stored")
        wq_loaded = sem("wq_loaded")
        wo_loaded = sem("wo_loaded")
        w_hi = sem("w_hi")
        w_lo = sem("w_lo")
        wr_loaded = sem("wr_loaded")
        rows_loaded = sem("rows_loaded")
        x_loaded = sem("x_loaded")
        x_stats = sem("x_stats")
        x_mean = sem("x_mean")
        x_eps = sem("x_eps")
        x_rstd = sem("x_rstd")
        x_normed = sem("x_normed")
        x_turned = sem("x_turned")
        xT_hi_done = sem("xT_hi_done")
        xT_lo_done = sem("xT_lo_done")
        k_loaded = sem("k_loaded")
        v_loaded = sem("v_loaded")
        kT_hi_done = sem("kT_hi_done")
        kT_lo_done = sem("kT_lo_done")
        v_hi_done = sem("v_hi_done")
        v_lo_done = sem("v_lo_done")
        q_projected = sem("q_projected")
        q_biased = sem("q_biased")
        q_squared = sem("q_squared")
        q_summed = sem("q_summed")
        q_rooted = sem("q_rooted")
        q_normed = sem("q_normed")
        q_turned = sem("q_turned")
        qT_hi_done = sem("qT_hi_done")
        qT_lo_done = sem("qT_lo_done")
        scored = sem("scored")
        s_masked = sem("s_masked")
        s_summed = sem("s_summed")
        s_maxed = sem("s_maxed")
        p_exped = sem("p_exped")
        p_inverted = sem("p_inverted")
        p_normed = sem("p_normed")
        p_turned = sem("p_turned")
        pT_hi_done = sem("pT_hi_done")
        pT_lo_done = sem("pT_lo_done")
        mixed = sem("mixed")
        oT_hi_done = sem("oT_hi_done")
        oT_lo_done = sem("oT_lo_done")
        y_added = sem("y_added")
        res_loaded = sem("res_loaded")
        x1_made = sem("x1_made")
        x1_stats = sem("x1_stats")
        x1_mean = sem("x1_mean")
        x1_eps = sem("x1_eps")
        x1_rstd = sem("x1_rstd")
        h_made = sem("h_made")
        h_stored = sem("h_stored")
        base_made = sem("base_made")
        base_stored = sem("base_stored")
        scored_row = sem("scored_row")
        score_spread = sem("score_spread")
        score_turned = sem("score_turned")
        counted_above = sem("counted_above")
        counted_tied = sem("counted_tied")
        picks_made = sem("picks_made")
        raw_loaded = [sem(f"raw_loaded{i}") for i in range(3)]
        piece_hi = sem("piece_hi")
        piece_lo_dve = sem("piece_lo_dve")
        piece_lo_pool = sem("piece_lo_pool")
        place_found = sem("place_found")
        onehot_made = sem("onehot_made")
        rows_found = sem("rows_found")
        idx_made = sem("idx_made")
        gathered_h = [sem(f"gathered_h{j}") for j in range(NJ)]
        gathered_rope = [sem(f"gathered_rope{j}") for j in range(NJ)]
        gathered_base = sem("gathered_base")
        ln1_loaded = sem("ln1_loaded")
        f_rows_loaded = sem("f_rows_loaded")
        bias_loaded = [sem(f"bias_loaded{i}") for i in range(2)]
        f_squared = sem("f_squared")
        f_meaned = sem("f_meaned")
        f_rooted = sem("f_rooted")
        hn_made = sem("hn_made")
        h_turned = sem("h_turned")
        hT_hi_done = sem("hT_hi_done")
        hT_lo_done = sem("hT_lo_done")
        f_projected = sem("f_projected")
        f_biased = sem("f_biased")
        cos_done = sem("cos_done")
        sin_done = sem("sin_done")
        f_roped = sem("f_roped")
        fv_hi_done = sem("fv_hi_done")
        fv_lo_done = sem("fv_lo_done")
        fk_turned = sem("fk_turned")
        fk_hi_done = sem("fk_hi_done")
        fk_lo_done = sem("fk_lo_done")
        fq_turned = sem("fq_turned")
        fq_hi_done = sem("fq_hi_done")
        fq_lo_done = sem("fq_lo_done")
        f_scored = sem("f_scored")
        f_masked = sem("f_masked")
        f_maxed = sem("f_maxed")
        f_exped = sem("f_exped")
        f_inverted = sem("f_inverted")
        f_normed = sem("f_normed")
        fp_turned = sem("fp_turned")
        fp_hi_done = sem("fp_hi_done")
        fp_lo_done = sem("fp_lo_done")
        f_mixed = sem("f_mixed")
        fo_hi_done = sem("fo_hi_done")
        fo_lo_done = sem("fo_lo_done")
        attn_done = sem("attn_done")
        attn_copied = sem("attn_copied")
        x2_made = sem("x2_made")
        gated = sem("gated")
        upped = sem("upped")
        tanh_done = sem("tanh_done")
        silu_done = sem("silu_done")
        act_done = sem("act_done")
        act_turned = sem("act_turned")
        aT_hi_done = sem("aT_hi_done")
        aT_lo_done = sem("aT_lo_done")
        mlp_done = sem("mlp_done")
        g_dotted = sem("g_dotted")
        g_exped = sem("g_exped")
        g_made = sem("g_made")
        attn_gated = sem("attn_gated")
        final_made = sem("final_made")
        out_stored = [sem(f"out_stored{j}") for j in range(NJ)]

        block = ctx.enter_context(nc.Block())

        def wait(eng, s, n):
            if not isinstance(n, int) or n > 0:
                eng.wait_ge(s, n)

        used_up = {}
        for o, piece in enumerate(PROJECTIONS):
            used_up[ATTENTION.index(piece)] = (f_projected, TILES.index((o, NJ - 1)) + 1)
        for n in range(FQ):
            used_up[p_wo(n)] = (attn_done, NJ * (n + 1))
        for m in range(FI):
            used_up[p_gate(m)] = (gated, NJ * (m + 1))
            used_up[p_up(m)] = (upped, NJ * (m + 1))
            used_up[p_down(m)] = (mlp_done, NJ * (m + 1))

        def split_early(n):
            return p_wq(0) + NSLOT + 2 * n

        def split_late(n):
            return [p_wq(0) + NSLOT + 2 * n + 1] if n < FQ - 1 else []

        def split_mlp(m):
            return range(P_MLP + 4 + 3 * m, min(P_MLP + 4 + 3 * (m + 1), NP))

        SCORE_TILES = ((QUAD, 0), (QUAD // 2, QUAD), (QUAD // 2, QUAD + QUAD // 2))

        def weights_over(eng):
            eng.wait_ge(v_projected, NB)

        def keys_over(eng):
            eng.wait_ge(k_stored, 16 * NB)
            eng.wait_ge(v_stored, 16 * NB)
            eng.wait_ge(w_lo, 2 * NB)
            eng.wait_ge(w_hi, 2 * NB)

        def layer1_over(eng):
            eng.wait_ge(h_stored, 16 * NB)
            eng.wait_ge(base_stored, 16 * NB)
            eng.wait_ge(picks_made, NB)

        @block.sync
        def _(sp):
            def spread(dst, vec):
                return sp.dma_start(dst, vec.partition_broadcast(P))

            sp.dma_start(cx[0][:], ctx_rows[0:S, :]).then_inc(cx_loaded[0], 16)
            for i in range(2):
                half_chunks = slice(i * DC // 2, (i + 1) * DC // 2)
                sp.dma_start(raw[0][:, half_chunks, :], chunked(Wk)[:, half_chunks, :]).then_inc(wk_loaded[i], 16)
            sp.dma_start(cx[1][:], ctx_rows[S:2 * S, :]).then_inc(cx_loaded[1], 16)
            sp.dma_start(raw[1][:], chunked(Wv)).then_inc(wv_loaded[0], 16)
            spread(bk_row[:], bk).then_inc(kv_bias_loaded, 16)
            spread(bv_row[:], bv).then_inc(kv_bias_loaded, 16)
            sp.dma_start(qw[:], qn_w.rearrange("(p a) -> p a", a=1)).then_inc(const_loaded, 16)
            sp.dma_start(kw[:], kn_w.rearrange("(p a) -> p a", a=1)).then_inc(const_loaded, 16)
            sp.dma_start(base_row[:], slot_base).then_inc(const_loaded, 16)

            def store_v(b):
                sp.wait_ge(v_biased, b + 1)
                sp.dma_start(v_store[bass.ds(b * P, P), :], v_out[:]).then_inc(v_stored, 16)

            def store_k(b):
                sp.wait_ge(k_weighted, b + 1)
                sp.dma_start(k_store[bass.ds(b * P, P), :], k_out[:]).then_inc(k_stored, 16)

            def kv_batch(b, par, first, last_two, beside=None):
                if not last_two:
                    sp.wait_ge(c_turned, b + 1)
                    sp.dma_start(cx[par][:], ctx_rows[bass.ds((b + 2) * S, S), :]
                                 ).then_inc(cx_loaded[par], 16)
                wait(sp, w_lo, 2 * b)
                sp.dma_start(wq_raw[:], chunked(Wq)[:, :, bass.ds(b * HD, HD)]).then_inc(wq_loaded, 16)
                sp.dma_start(wo_raw[:], Wo[bass.ds(b * P, P), :]).then_inc(wo_loaded, 16)
                if beside is not None:
                    beside()
                if not first:
                    store_v(b - 1)
                    store_k(b - 1)

            def first_rows():
                sp.wait_ge(c_turned, NB - 1)
                sp.dma_start(xr[:], x_rows[0:S, :]).then_inc(x_loaded, 16)

            kv_batch(0, 0, True, False)
            with sp.Fori(0, NB // 2 - 2) as g:
                kv_batch(2 * g + 1, 1, False, False)
                kv_batch(2 * g + 2, 0, False, False)
            kv_batch(NB - 3, 1, False, False)
            kv_batch(NB - 2, 0, False, True, first_rows)

            def query_bias():
                weights_over(sp)
                spread(bq_row[:, 0:W], bq[0:W]).then_inc(rows_loaded, 16)
                sp.dma_start(mask[:], attn_mask.rearrange("a s t -> (a s) t")).then_inc(rows_loaded, 16)

            kv_batch(NB - 1, 1, False, True, query_bias)

            def load_x(b):
                sp.dma_start(xr[:], x_rows[bass.ds(b * S, S), :]).then_inc(x_loaded, 16)

            def load_k(b):
                sp.dma_start(k_raw[:], k_store[bass.ds(b * P, P), :]).then_inc(k_loaded, 16)

            def load_v(b):
                sp.dma_start(v_raw[:], v_store[bass.ds(b * P, P), :]).then_inc(v_loaded, 16)

            sp.wait_ge(k_stored, 16 * (NB - 1))
            sp.wait_ge(v_stored, 16 * (NB - 1))
            load_k(0)
            load_v(0)
            spread(bq_row[:, W:NH * HD], bq[W:NH * HD]).then_inc(kv_bias_loaded, 16)
            sp.dma_start(x_res[:], x_rows[0:S, :]).then_inc(res_loaded, 16)
            sp.wait_ge(x_normed, 1)
            load_x(1)
            store_v(NB - 1)
            store_k(NB - 1)

            def store_rows(b):
                sp.wait_ge(h_made, b + 1)
                sp.dma_start(h_store[bass.ds(b * S, S), :], h_row[:]).then_inc(h_stored, 16)
                sp.wait_ge(base_made, b + 1)
                sp.dma_start(out_rows[bass.ds(b * S, S), :], x1[:]).then_inc(base_stored, 16)

            def attend(b, first, last):
                if not first and not last:
                    sp.wait_ge(x_normed, b + 1)
                    load_x(b + 1)
                if not last:
                    sp.wait_ge(kT_hi_done, b + 1)
                    sp.wait_ge(kT_lo_done, b + 1)
                    load_k(b + 1)
                if not first:
                    sp.wait_ge(x1_made, b)
                    sp.dma_start(x_res[:], x_rows[bass.ds(b * S, S), :]).then_inc(res_loaded, 16)
                if not last:
                    sp.wait_ge(v_hi_done, b + 1)
                    sp.wait_ge(v_lo_done, b + 1)
                    load_v(b + 1)
                if not first:
                    store_rows(b - 1)

            attend(0, True, False)
            keys_over(sp)
            spread(wr_row[:], w_router).then_inc(wr_loaded, 16)
            for i in range(2):
                sp.wait_ge(kv_w_hi, DC * (i + 1))
                sp.wait_ge(kv_w_lo, DC * (i + 1))
                sp.dma_start(raw[i][:], PIECES[i]).then_inc(raw_loaded[i], 16)
            with sp.Fori(1, NB - 1) as b:
                attend(b, False, False)
            attend(NB - 1, False, True)

            def load_piece(n):
                if RAW_BEFORE[n] >= 0:
                    sp.wait_ge(piece_hi, RAW_BEFORE[n] + 1)
                    sp.wait_ge(piece_lo_dve, RAW_BEFORE[n] + 1)
                    sp.wait_ge(piece_lo_pool, RAW_BEFORE[n] + 1)
                sp.dma_start(raw[RAW_OF[n]][:], PIECES[n]).then_inc(raw_loaded[RAW_OF[n]], 16)

            sp.wait_ge(kT_hi_done, NB)
            sp.wait_ge(kT_lo_done, NB)
            spread(ln1_row[:], ln1_w).then_inc(ln1_loaded, 16)
            VECTOR = {"k": ffn_bk, "v": ffn_bv, "q": ffn_bq}
            BIASES = [VECTOR[kind][n * W:(n + 1) * W] for kind, n in PROJECTIONS]

            def load_bias(u):
                if u >= 2:
                    before = BIAS_USES[u - 2]
                    j = (u - 2) // AHEAD if u - 2 < NJ * AHEAD else NJ - 1
                    sp.wait_ge(f_biased, TILES.index((before, j)) + 1)
                spread(bias_row[u % 2][:], BIASES[BIAS_USES[u]]).then_inc(bias_loaded[u % 2], 16)

            sp.wait_ge(q_projected, STEPS)
            load_bias(0)
            load_bias(1)
            load_piece(2)
            load_piece(3)
            store_rows(NB - 1)

            layer1_over(sp)
            spread(ln2_row[:], ln2_w).then_inc(f_rows_loaded, 16)
            spread(wr2_row[:], w_router).then_inc(f_rows_loaded, 16)
            load_bias(2)
            load_bias(3)
            sp.wait_ge(gathered_h[1], 16)
            load_piece(NSLOT)
            load_piece(NSLOT + 1)
            load_bias(4)
            load_bias(5)
            load_piece(NSLOT + 2)
            load_bias(6)
            load_bias(7)
            load_piece(NSLOT + 3)
            for n in range(NSLOT + 4, NP):
                if n == NSLOT + 4:
                    load_bias(8)
                if n - NSLOT + 5 < len(BIAS_USES):
                    load_bias(n - NSLOT + 5)
                load_piece(n)
            for j in range(NJ):
                sp.wait_ge(out_stored[j], 16)

        @block.gpsimd
        def _(pool):
            pool.memset(ident[:], 0.0).then_inc(const_made, 1)
            pool.memset(earlier[:], 1.0).then_inc(const_made, 1)
            pool.memset(later[:], 1.0).then_inc(const_made, 1)
            pool.memset(causal[:], 0.0).then_inc(const_made, 1)
            pool.memset(half[:], -0.5).then_inc(const_made, 1)
            pool.memset(eps_head[:], HD * EPS_RMS).then_inc(const_made, 1)
            pool.memset(eps_ln[:], EPS_LN).then_inc(const_made, 1)
            pool.iota(slots[:], pattern=[[1, PICK]], base=0, channel_multiplier=0,
                      allow_small_or_imprecise_dtypes=True).then_inc(const_made, 1)
            pool.iota(token[:], pattern=[[0, 1]], base=0, channel_multiplier=1,
                      allow_small_or_imprecise_dtypes=True).then_inc(const_made, 1)
            pool.wait_ge(const_made, 9)
            pool.affine_select(out=ident[:], in_=ident[:], compare_op=ALU.not_equal, fill=1.0,
                               base=0, pattern=[[-1, P]], channel_multiplier=1).then_inc(const_made, 1)
            pool.affine_select(out=earlier[:], in_=earlier[:], compare_op=ALU.is_gt, fill=0.0,
                               base=0, pattern=[[-1, P]], channel_multiplier=1).then_inc(const_made, 1)
            pool.affine_select(out=later[:], in_=later[:], compare_op=ALU.is_gt, fill=0.0,
                               base=0, pattern=[[1, P]], channel_multiplier=-1).then_inc(const_made, 1)
            pool.affine_select(out=causal[:, P:2 * P], in_=causal[:, P:2 * P], compare_op=ALU.is_ge,
                               fill=MASKED, base=0, pattern=[[-1, P]],
                               channel_multiplier=1).then_inc(const_made, 1)
            pool.wait_ge(const_made, 13)

            def rsqrt(src, dst, eps, summed, rooted, count):
                pool.tensor_tensor(dst, src, eps, ALU.add).then_inc(summed, 1)
                pool.wait_ge(summed, count)
                pool.tensor_tensor(dst, dst, half[:, 0:dst.shape[1]], ALU.pow).then_inc(rooted, 1)

            def per_head(stat, width):
                return stat[:, :].unsqueeze(2).to_broadcast([P, stat.shape[1], width])

            def kv_batch(b):
                pool.wait_ge(k_squared, b + 1)
                rsqrt(k_ss[:], k_rs[:], eps_head[:], k_summed, k_rooted, b + 1)
                pool.wait_ge(k_rooted, b + 1)
                pool.tensor_tensor(k_row[:], k_row[:], per_head(k_rs, HD), ALU.mult).then_inc(k_normed, 1)

            with pool.Fori(0, NB - 1) as b:
                kv_batch(b)

            def x_norm_stat(b):
                pool.wait_ge(x_mean, b + 1)
                rsqrt(mv[:, 1:2], rstd[:], eps_ln[:], x_eps, x_rstd, b + 1)

            def k_low(b):
                pool.wait_ge(kT_hi_done, b + 1)
                pool.tensor_tensor(kT[:, :, 1, :], k_raw[:].rearrange("p (g s) -> p g s", g=NKV),
                                   kT[:, :, 0, :].bitcast(fp32), ALU.subtract).then_inc(kT_lo_done, 1)

            def v_low(b):
                pool.wait_ge(v_hi_done, b + 1)
                pool.tensor_tensor(v_lo[:], v_raw[:], v_hi[:].bitcast(fp32),
                                   ALU.subtract).then_inc(v_lo_done, 1)

            def q_norm(t):
                pool.wait_ge(q_squared, t + 1)
                rsqrt(q_ss[:], q_rs[:], eps_head[:], q_summed, q_rooted, t + 1)
                pool.wait_ge(q_rooted, t + 1)
                wait(pool, q_turned, t)
                pool.tensor_tensor(q_nrm[:], q_row[:], per_head(q_rs, HD), ALU.mult).then_inc(q_normed, 1)

            def p_norm(t):
                pool.wait_ge(p_inverted, t + 1)
                pool.tensor_tensor(p_row[:], p_row[:], per_head(p_inv, S), ALU.mult).then_inc(p_normed, 1)

            def out_stat(b):
                pool.wait_ge(x1_mean, b + 1)
                rsqrt(mv1[:, 1:2], rstd1[:], eps_ln[:], x1_eps, x1_rstd, b + 1)

            def base_rows(b):
                pool.wait_ge(h_made, b + 1)
                pool.tensor_tensor(x1[:], x1[:], h_row[:], ALU.add).then_inc(base_made, 1)

            x_norm_stat(0)
            kv_batch(NB - 1)
            pool.wait_ge(w_lo, 2 * NB)
            weights_over(pool)
            q_norm(0)
            k_low(0)

            def gather_rows(j):
                pool.wait_ge(idx_made, 2 * (j + 1))
                pool.indirect_dma_start(h_sel[j][:], None, h_store[0:(j + 1) * BPJ * S, :],
                                        bass.IndirectOffsetOnAxis(ap=row_idx[j][:, 0:1], axis=0)
                                        ).then_inc(gathered_h[j], 16)
                pool.indirect_dma_start(rope[j][:], None, rope_table,
                                        bass.IndirectOffsetOnAxis(ap=pos_idx[j][:, 0:1], axis=0)
                                        ).then_inc(gathered_rope[j], 16)

            def attend(b, first, last):
                for i in range(NQUAD):
                    t = NQUAD * b + i
                    if last and i == NQUAD - 1:
                        pool.wait_ge(h_stored, 16 * BPJ)
                        pool.wait_ge(x_normed, NB)
                        pool.wait_ge(v_hi_done, NB)
                        pool.wait_ge(v_lo_done, NB)
                        gather_rows(0)
                    if i == 0 and not first and not last:
                        x_norm_stat(b + 1)
                    if not (last and i == NQUAD - 1):
                        q_norm(t + 1)
                    if i == 0 and first:
                        x_norm_stat(1)
                    p_norm(t)
                    if i == 0:
                        v_low(b)
                    if i == 0 and first:
                        keys_over(pool)
                    if i == 1 and not first:
                        out_stat(b - 1)
                    if i == 2 and not first:
                        base_rows(b - 1)
                    if i == NQUAD - 1 and not last:
                        k_low(b + 1)

            attend(0, True, False)
            with pool.Fori(1, NB - 1) as b:
                attend(b, False, False)
            attend(NB - 1, False, True)

            def split_low(n):
                pool.wait_ge(piece_hi, n + 1)
                pool.tensor_tensor(wp_lo[n % NSLOT][:, 0:2, :], raw[RAW_OF[n]][:, 0:2, :],
                                   wp_hi[n % NSLOT][:, 0:2, :].bitcast(fp32),
                                   ALU.subtract).then_inc(piece_lo_pool, 1)

            def row_rsqrt(i):
                pool.wait_ge(f_squared, i + 1)
                pool.tensor_scalar(f_ms[:, i:i + 1], f_ss[:, i:i + 1], 1.0 / D, EPS_RMS,
                                   ALU.mult, ALU.add).then_inc(f_meaned, 1)
                pool.wait_ge(f_meaned, i + 1)
                pool.tensor_tensor(f_rs[:, i:i + 1], f_ms[:, i:i + 1], half[:, 0:1],
                                   ALU.pow).then_inc(f_rooted, 1)

            row_rsqrt(0)
            split_low(0)
            split_low(1)
            out_stat(NB - 1)
            base_rows(NB - 1)
            split_low(2)

            def by_cosine(o, j):
                r, k = TILES.index((o, j)), ROPED.index((o, j))
                pool.wait_ge(f_biased, r + 1)
                pool.wait_ge(gathered_rope[j], 16)
                wait(pool, f_roped, k)
                pool.tensor_tensor(by_cos[:].rearrange("p (h d) -> p h d", h=QUAD),
                                   proj[r % 2][:].rearrange("p (h d) -> p h d", h=QUAD),
                                   rope[j][:, 0:HD].unsqueeze(1).to_broadcast([P, QUAD, HD]),
                                   ALU.mult).then_inc(cos_done, 1)

            def v_low_rows(r, i):
                pool.wait_ge(fv_hi_done, i + 1)
                c = i // NJ
                pool.tensor_tensor(fv_lo[:, i % NJ, c * W:(c + 1) * W], proj[r % 2][:],
                                   fv_hi[:, i % NJ, c * W:(c + 1) * W].bitcast(fp32),
                                   ALU.subtract).then_inc(fv_lo_done, 1)

            def take_rows(o, j):
                kind, n = PROJECTIONS[o]
                if kind == "v":
                    v_low_rows(TILES.index((o, j)), NJ * n + j)
                else:
                    by_cosine(o, j)

            pool.wait_ge(y_added, STEPS)
            take_rows(0, 0)
            split_low(3)
            layer1_over(pool)
            gather_rows(1)
            take_rows(1, 0)
            take_rows(2, 0)
            row_rsqrt(1)
            take_rows(3, 0)
            for o in range(AHEAD):
                take_rows(o, 1)
                if o > 0:
                    split_low(NSLOT + o - 1)

            def next_query_cosine(n, j):
                by_cosine(PROJECTIONS.index(("q", n + 1)), j)

            for n in range(FQ):
                if n < FQ - 1:
                    next_query_cosine(n, 0)
                    next_query_cosine(n, 1)
                    split_low(split_early(n))
                for piece in split_late(n):
                    split_low(piece)
                for i, (heads, col) in enumerate(SCORE_TILES):
                    pool.wait_ge(f_inverted, 3 * n + i + 1)
                    pool.tensor_tensor(
                        fs[i][:].rearrange("p (h t) -> p h t", h=heads),
                        fs[i][:].rearrange("p (h t) -> p h t", h=heads),
                        f_inv[:, col:col + heads].unsqueeze(2).to_broadcast([P, heads, W // heads]),
                        ALU.mult).then_inc(f_normed, 1)
                if n == 0:
                    for j in range(NJ):
                        take_rows(PROJECTIONS.index(("v", 1)), j)
            split_low(split_early(FQ - 1))
            pool.wait_ge(f_roped, NJ * (FK + FQ))
            for j in range(NJ):
                pool.indirect_dma_start(base[j][:], None, out_rows,
                                        bass.IndirectOffsetOnAxis(ap=row_idx[j][:, 0:1], axis=0)
                                        ).then_inc(gathered_base, 16)
            split_low(P_MLP + 2)
            for j in range(NJ):
                row_rsqrt(NJ + j)
            split_low(P_MLP + 3)
            for n in range(P_MLP + 4, NP):
                split_low(n)
            for j in range(NJ):
                pool.wait_ge(final_made, j + 1)
                pool.indirect_dma_start(out_rows, bass.IndirectOffsetOnAxis(ap=row_idx[j][:, 0:1], axis=0),
                                        final[j][:], None).then_inc(out_stored[j], 16)
            for j in range(NJ):
                pool.wait_ge(out_stored[j], 16)

        @block.scalar
        def _(act):
            def copy(dst, src):
                return act.activation(dst, src, ACT.Copy)

            def turn_c(b, par):
                act.wait_ge(c_turned, b + 1)
                wait(act, v_projected, b - 1)
                copy(cT_hi[par][:].rearrange("p c t -> p (c t)"), b_c[:]).then_inc(c_hi, 1)

            turn_c(0, 0)
            for hi, rw, loaded in ((wk_hi, raw[0], wk_loaded), (wv_hi, raw[1], wv_loaded)):
                for c in range(DC):
                    act.wait_ge(loaded[c * len(loaded) // DC], 16)
                    copy(hi[:, c, :], rw[:, c, :]).then_inc(kv_w_hi, 1)
            act.wait_ge(const_loaded, 48)
            act.wait_ge(kw_scaled, 1)

            def weigh_k(b):
                act.wait_ge(k_turned, b + 1)
                wait(act, k_stored, 16 * b)
                act.activation(k_out[:], b_kT[:], ACT.Copy, scale=kw[:, 0:1]).then_inc(k_weighted, 1)

            def kv_batch(b, par, first, last):
                if not last:
                    turn_c(b + 1, 1 - par)
                act.wait_ge(k_biased, b + 1)
                wait(act, k_rooted, b)
                for h in range(NKV):
                    sq = act.activation(k_sq[:, h, :], k_row[:, h, :], ACT.Square, accum_out=k_ss[:, h:h + 1])
                sq.then_inc(k_squared, 1)
                if not first:
                    weigh_k(b - 1)
                act.wait_ge(wq_loaded, 16 * (b + 1))
                copy(wq_hi[:, :, bass.ds(b * HD, HD)], wq_raw[:]).then_inc(w_hi, 1)
                act.wait_ge(wo_loaded, 16 * (b + 1))
                copy(wo_hi[:, bass.ds(b, 1), :], wo_raw[:].unsqueeze(1)).then_inc(w_hi, 1)

            kv_batch(0, 0, True, False)
            with act.Fori(0, NB // 2 - 1) as g:
                kv_batch(2 * g + 1, 1, False, False)
                kv_batch(2 * g + 2, 0, False, False)

            def x_high(b):
                act.wait_ge(x_turned, b + 1)
                copy(xT_hi[:].rearrange("p c t -> p (c t)"), b_xT[:]).then_inc(xT_hi_done, 1)

            def first_rows():
                act.wait_ge(v_projected, NB - 1)
                x_high(0)

            first_rows()
            kv_batch(NB - 1, 1, False, True)

            def k_high(b):
                act.wait_ge(k_loaded, 16 * (b + 1))
                wait(act, scored, NQUAD * b)
                copy(kT[:, :, 0, :], k_raw[:].rearrange("p (g s) -> p g s", g=NKV)).then_inc(kT_hi_done, 1)

            def v_high(b):
                act.wait_ge(v_loaded, 16 * (b + 1))
                wait(act, mixed, NQUAD * b)
                copy(v_hi[:], v_raw[:]).then_inc(v_hi_done, 1)

            def q_high(t):
                act.wait_ge(q_turned, t + 1)
                wait(act, scored, t)
                act.activation(qT_hi[:], b_qT[:], ACT.Copy, scale=qw[:, 0:1]).then_inc(qT_hi_done, 1)

            def p_high(t):
                act.wait_ge(p_turned, t + 1)
                wait(act, mixed, t)
                copy(pT_hi[:], b_pT[:]).then_inc(pT_hi_done, 1)

            def o_high(t):
                act.wait_ge(mixed, t + 1)
                wait(act, y_added, t)
                copy(oT_hi[:], b_o[:]).then_inc(oT_hi_done, 1)

            def squares(t):
                act.wait_ge(q_biased, t + 1)
                wait(act, q_rooted, t)
                for h in range(QUAD):
                    sq = act.activation(sq_junk[:, h, :], q_row[:, h, :], ACT.Square, accum_out=q_ss[:, h:h + 1])
                sq.then_inc(q_squared, 1)

            def exps(t):
                act.wait_ge(s_maxed, t + 1)
                wait(act, p_turned, t)
                for h in range(QUAD):
                    e = act.activation(p_row[:, h, :], s_row[:, h, :], ACT.Exp,
                                       bias=neg_max[:, h:h + 1], accum_out=p_sum[:, h:h + 1])
                e.then_inc(p_exped, 1)

            weights_over(act)
            weigh_k(NB - 1)
            squares(0)
            k_high(0)

            def attend(b, first, last):
                for i in range(NQUAD):
                    t = NQUAD * b + i
                    q_high(t)
                    if not (last and i == NQUAD - 1):
                        squares(t + 1)
                    if not (first and i == 0):
                        p_high(t - 1)
                    if i == 2 and not last:
                        x_high(b + 1)
                    exps(t)
                    if first and i == 0:
                        keys_over(act)
                    if not (first and i == 0):
                        o_high(t - 1)
                    if i == 0:
                        v_high(b)
                    if i == NQUAD - 1 and not last:
                        k_high(b + 1)

            attend(0, True, False)
            with act.Fori(1, NB - 1) as b:
                attend(b, False, False)
            attend(NB - 1, False, True)
            def row_squares(i, src):
                act.activation(hn_row[i % NJ][:], src, ACT.Square, accum_out=f_ss[:, i:i + 1]).then_inc(f_squared, 1)

            act.wait_ge(x_turned, NB)
            act.wait_ge(gathered_h[0], 16)
            row_squares(0, h_sel[0][:])
            p_high(STEPS - 1)

            def split_high(n):
                act.wait_ge(raw_loaded[RAW_OF[n]], 16 * NTH_RAW[n])
                if n >= NSLOT:
                    act.wait_ge(*used_up[n - NSLOT])
                copy(wp_hi[n % NSLOT][:], raw[RAW_OF[n]][:]).then_inc(piece_hi, 1)

            act.wait_ge(q_projected, STEPS)
            split_high(0)

            o_high(STEPS - 1)
            split_high(1)

            def h_high(i):
                act.wait_ge(h_turned, i + 1)
                copy(hT_hi[:, i % NJ].rearrange("p c t -> p (c t)"), (f_T, f_T2)[i % NJ][:]
                     ).then_inc(hT_hi_done, 1)

            act.wait_ge(y_added, STEPS)
            h_high(0)
            split_high(2)
            split_high(3)
            layer1_over(act)

            def fk_high(n, j):
                act.wait_ge(fk_turned, KEYS.index((n, j)) + 1)
                copy(fkT_hi[:, n * QUAD:(n + 1) * QUAD, j * P:(j + 1) * P],
                     (f_T, f_T2)[j][:].rearrange("p (h t) -> p h t", h=QUAD)).then_inc(fk_hi_done, 1)

            def v_high_rows(o, j):
                n = PROJECTIONS[o][1]
                act.wait_ge(f_biased, TILES.index((o, j)) + 1)
                copy(fv_hi[:, j, n * W:(n + 1) * W], proj[TILES.index((o, j)) % 2][:]).then_inc(fv_hi_done, 1)

            v_high_rows(1, 0)
            fk_high(0, 0)
            act.wait_ge(gathered_h[1], 16)
            row_squares(1, h_sel[1][:])
            fk_high(1, 0)
            h_high(1)
            for o, (kind, n) in enumerate(PROJECTIONS[:AHEAD]):
                if kind == "v":
                    v_high_rows(o, 1)
                if o > 0 and PROJECTIONS[o - 1][0] == "k":
                    fk_high(PROJECTIONS[o - 1][1], 1)
                if o < AHEAD - 1:
                    split_high(NSLOT + o)

            def probs_high(n):
                act.wait_ge(fp_turned, 3 * n + 1)
                wait(act, f_mixed, 2 * n)
                copy(fp0_hi[:, 0:2, :].rearrange("p h t -> p (h t)"), f_T[:]).then_inc(fp_hi_done, 1)
                act.wait_ge(fp_turned, 3 * n + 2)
                copy(fp0_hi[:, 2:4, :].rearrange("p h t -> p (h t)"), f_T2[:]).then_inc(fp_hi_done, 1)
                act.wait_ge(fp_turned, 3 * n + 3)
                copy(fp1_hi[:].rearrange("p h t -> p (h t)"), f_S[:]).then_inc(fp_hi_done, 1)

            def mixed_high(n):
                for g in range(2):
                    act.wait_ge(f_mixed, 2 * n + g + 1)
                    wait(act, attn_done, NJ * n)
                    copy(foT_hi[:, 2 * g:2 * g + 2, :].rearrange("p h t -> p (h t)"),
                         (f_O, f_T)[g][:]).then_inc(fo_hi_done, 1)

            for n in range(FQ):
                for j in range(NJ):
                    act.wait_ge(fq_turned, NJ * n + j + 1)
                    wait(act, f_scored, 3 * n)
                    copy(fqT_hi[:, j].rearrange("p h t -> p (h t)"), (f_T, f_T2)[j][:]
                         ).then_inc(fq_hi_done, 1)
                if n > 0:
                    probs_high(n - 1)
                if n < FQ - 1:
                    split_high(split_early(n))
                if n > 0:
                    mixed_high(n - 1)
                for piece in split_late(n):
                    split_high(piece)
                for i, (heads, col) in enumerate(SCORE_TILES):
                    width = W // heads
                    act.wait_ge(f_maxed, 3 * n + i + 1)
                    for h in range(heads):
                        e = act.activation(fs[i][:, h * width:(h + 1) * width],
                                           fs[i][:, h * width:(h + 1) * width], ACT.Exp,
                                           bias=f_max[:, col + h:col + h + 1],
                                           accum_out=f_sum[:, col + h:col + h + 1])
                    e.then_inc(f_exped, 1)
                if n == FQ - 1:
                    split_high(split_early(n))
                if n == 0:
                    for j in range(NJ):
                        v_high_rows(PROJECTIONS.index(("v", 1)), j)
            probs_high(FQ - 1)
            mixed_high(FQ - 1)
            split_high(P_MLP + 2)
            for j in range(NJ):
                act.wait_ge(x2_made, j + 1)
                row_squares(NJ + j, x2_row[j][:])
            for j in range(NJ):
                h_high(NJ + j)
            for j in range(NJ):
                copy(attn_row[j][:], f_W[j][:]).then_inc(attn_copied, 1)
            split_high(P_MLP + 3)
            act.wait_ge(g_dotted, NJ)
            act.activation(g_exp[:], g_dot[:], ACT.Exp, scale=-1.0).then_inc(g_exped, 1)
            for m in range(FI):
                for j in range(NJ):
                    act.wait_ge(gated, NJ * m + j + 1)
                    wait(act, act_done, NJ * (m - 1) + j + 1)
                    act.activation(tanh_row[j][:], f_proj[j][:], ACT.Tanh, scale=0.5).then_inc(tanh_done, 1)
                for piece in split_mlp(m):
                    split_high(piece)
                for j in range(NJ):
                    act.wait_ge(act_turned, NJ * m + j + 1)
                    wait(act, mlp_done, NJ * (m - 1) + j + 1)
                    copy(fqT_hi[:, j].rearrange("p h t -> p (h t)"), (f_T, f_T2)[j][:]
                         ).then_inc(aT_hi_done, 1)

        @block.vector
        def _(dve):
            def low(dst, src, hi):
                return dve.tensor_tensor(dst, src, hi.bitcast(fp32), ALU.subtract)

            def turn_c(b, par):
                dve.wait_ge(c_hi, b + 1)
                low(cT_lo[par][:].rearrange("p c t -> p (c t)"), b_c[:],
                    cT_hi[par][:].rearrange("p c t -> p (c t)")).then_inc(c_lo, 1)

            turn_c(0, 0)
            for i, (hi, lo, rw) in enumerate(((wk_hi, wk_lo, raw[0]), (wv_hi, wv_lo, raw[1]))):
                for c in range(DC):
                    dve.wait_ge(kv_w_hi, DC * i + c + 1)
                    low(lo[:, c, :], rw[:, c, :], hi[:, c, :]).then_inc(kv_w_lo, 1)
            dve.wait_ge(const_loaded, 48)
            dve.tensor_scalar(kw[:], kw[:], 1.0 / SCALE, None, ALU.mult).then_inc(kw_scaled, 1)
            dve.wait_ge(kv_bias_loaded, 32)

            def kv_batch(b, par, last, beside=None):
                if not last:
                    turn_c(b + 1, 1 - par)
                dve.wait_ge(k_projected, b + 1)
                wait(dve, k_turned, b)
                dve.tensor_tensor(k_row[:].rearrange("p h d -> p (h d)"), b_k[:], bk_row[:],
                                  ALU.add).then_inc(k_biased, 1)
                dve.wait_ge(v_projected, b + 1)
                wait(dve, v_stored, 16 * b)
                dve.tensor_tensor(v_out[:], b_v[:], bv_row[:], ALU.add).then_inc(v_biased, 1)
                if beside is not None:
                    beside()
                dve.wait_ge(w_hi, 2 * b + 1)
                low(wq_lo[:, :, bass.ds(b * HD, HD)], wq_raw[:],
                    wq_hi[:, :, bass.ds(b * HD, HD)]).then_inc(w_lo, 1)
                dve.wait_ge(w_hi, 2 * b + 2)
                low(wo_lo[:, bass.ds(b, 1), :], wo_raw[:].unsqueeze(1),
                    wo_hi[:, bass.ds(b, 1), :]).then_inc(w_lo, 1)

            kv_batch(0, 0, False)
            with dve.Fori(0, NB // 2 - 2) as g:
                kv_batch(2 * g + 1, 1, False)
                kv_batch(2 * g + 2, 0, False)
            kv_batch(NB - 3, 1, False)

            def x_statistics(b):
                dve.wait_ge(x_loaded, 16 * (b + 1))
                wait(dve, x_rstd, b)
                dve.bn_stats(bn[:], xr[:]).then_inc(x_stats, 1)

            def x_moments(b):
                dve.bn_aggr(mv[:], bn[:]).then_inc(x_mean, 1)

            def x_norm(b):
                dve.wait_ge(x_rstd, b + 1)
                wait(dve, x_turned, b)
                dve.tensor_scalar(xn[:], xr[:], mv[:, 0:1], rstd[:, 0:1],
                                  ALU.subtract, ALU.mult).then_inc(x_normed, 1)

            def x_low(b):
                dve.wait_ge(xT_hi_done, b + 1)
                low(xT_lo[:].rearrange("p c t -> p (c t)"), b_xT[:],
                    xT_hi[:].rearrange("p c t -> p (c t)")).then_inc(xT_lo_done, 1)

            def q_bias(t, quad, bank=b_q):
                dve.wait_ge(q_projected, t + 1)
                wait(dve, q_normed, t)
                dve.tensor_tensor(q_row[:].rearrange("p h d -> p (h d)"), bank[:],
                                  bq_row[:, quad * W:(quad + 1) * W], ALU.add).then_inc(q_biased, 1)

            def q_low(t):
                dve.wait_ge(qT_hi_done, t + 1)
                dve.scalar_tensor_tensor(qT_lo[:], b_qT[:], qw[:, 0:1], qT_hi[:].bitcast(fp32),
                                         ALU.mult, ALU.subtract).then_inc(qT_lo_done, 1)

            def s_mask(t):
                dve.wait_ge(scored, t + 1)
                wait(dve, p_exped, t)
                dve.tensor_tensor(s_row[:], b_scores[:, :, 0:S],
                                  mask[:].unsqueeze(1).to_broadcast([P, QUAD, S]),
                                  ALU.add).then_inc(s_masked, 1)

            def s_sum(t):
                dve.wait_ge(s_masked, t + 1)
                dve.tensor_tensor(s_row[:], s_row[:], b_scores[:, :, S:2 * S], ALU.add).then_inc(s_summed, 1)

            def s_max(t):
                dve.wait_ge(s_summed, t + 1)
                dve.tensor_reduce(neg_max[:], s_row[:], AX.X, ALU.max, negate=True).then_inc(s_maxed, 1)

            def p_low(t):
                dve.wait_ge(pT_hi_done, t + 1)
                low(pT_lo[:], b_pT[:], pT_hi[:]).then_inc(pT_lo_done, 1)

            def p_invert(t):
                dve.wait_ge(p_exped, t + 1)
                wait(dve, p_normed, t)
                dve.reciprocal(p_inv[:], p_sum[:]).then_inc(p_inverted, 1)

            def o_low(t):
                dve.wait_ge(oT_hi_done, t + 1)
                low(oT_lo[:], b_o[:], oT_hi[:]).then_inc(oT_lo_done, 1)

            def add_residual(b):
                dve.wait_ge(y_added, NQUAD * (b + 1))
                dve.wait_ge(res_loaded, 16 * (b + 1))
                wait(dve, base_stored, 16 * b)
                dve.tensor_tensor(x1[:], b_y[:], x_res[:], ALU.add).then_inc(x1_made, 1)
                dve.wait_ge(x1_made, b + 1)
                dve.bn_stats(bn1[:], x1[:]).then_inc(x1_stats, 1)

            def x1_moments(b):
                dve.bn_aggr(mv1[:], bn1[:]).then_inc(x1_mean, 1)

            def norm_out(b):
                dve.wait_ge(x1_rstd, b + 1)
                wait(dve, h_stored, 16 * b)
                dve.tensor_scalar(h_row[:], x1[:], mv1[:, 0:1], rstd1[:, 0:1],
                                  ALU.subtract, ALU.mult).then_inc(h_made, 1)
                dve.wait_ge(h_made, b + 1)
                dve.tensor_tensor_reduce(dot_junk[:], h_row[:], wr_row[:], 1.0, 0.0, ALU.mult,
                                         ALU.add, accum_out=score[:, 0:1]).then_inc(scored_row, 1)
                dve.wait_ge(scored_row, b + 1)
                dve.tensor_copy(score_wide[:], score[:, 0:1].to_broadcast([P, S])).then_inc(score_spread, 1)

            def rank(b):
                dve.wait_ge(score_turned, b + 1)
                dve.tensor_scalar(rank_junk[:, 0, :], b_rank[:, 0:S], score[:, 0:1], 0.0, ALU.is_gt,
                                  ALU.add, accum_out=above[:, 0:1]).then_inc(counted_above, 1)
                dve.scalar_tensor_tensor(rank_junk[:, 1, :], b_rank[:, 0:S], score[:, 0:1], earlier[:],
                                         ALU.is_equal, ALU.mult,
                                         accum_out=tied[:, 0:1]).then_inc(counted_tied, 1)
                dve.wait_ge(counted_above, b + 1)
                dve.wait_ge(counted_tied, b + 1)
                dve.tensor_scalar(picked[:, bass.ds(b, 1)], above[:, 0:1], tied[:, 0:1], float(PICK),
                                  ALU.add, ALU.is_lt).then_inc(picks_made, 1)

            dve.wait_ge(const_made, 13)

            def norm_first_rows():
                dve.wait_ge(c_turned, NB)
                x_statistics(0)
                dve.wait_ge(x_stats, 1)
                x_moments(0)
                x_norm(0)

            def split_first_rows():
                dve.wait_ge(v_projected, NB - 1)
                x_low(0)

            kv_batch(NB - 2, 0, False, norm_first_rows)
            split_first_rows()
            kv_batch(NB - 1, 1, True)
            weights_over(dve)
            dve.wait_ge(w_lo, 2 * NB)
            dve.wait_ge(rows_loaded, 32)
            q_bias(0, 0)
            dve.wait_ge(kv_bias_loaded, 48)

            def select_rows(j):
                bs = slice(j * BPJ, (j + 1) * BPJ)
                dve.wait_ge(place_found, j + 1)
                dve.tensor_tensor(onehot[:, bs, :], b_xT[:, 0:BPJ].unsqueeze(2).to_broadcast([P, BPJ, PICK]),
                                  slots[:].unsqueeze(1).to_broadcast([P, BPJ, PICK]),
                                  ALU.is_equal).then_inc(onehot_made, 1)
                dve.wait_ge(onehot_made, 2 * j + 1)
                dve.tensor_tensor(onehot[:, bs, :], onehot[:, bs, :],
                                  picked[:, bs].unsqueeze(2).to_broadcast([P, BPJ, PICK]),
                                  ALU.mult).then_inc(onehot_made, 1)

            def number_rows(j):
                dve.wait_ge(rows_found, j + 1)
                dve.tensor_tensor(row_idx[j][:], b_xT[:, BPJ:BPJ + 1], base_row[:, j:j + 1],
                                  ALU.add).then_inc(idx_made, 1)
                dve.tensor_copy(pos_idx[j][:], b_xT[:, BPJ:BPJ + 1]).then_inc(idx_made, 1)

            def attend(b, first, last):
                for i in range(NQUAD):
                    t = NQUAD * b + i
                    if last and i == 1:
                        dve.wait_ge(v_hi_done, NB)
                        dve.wait_ge(v_lo_done, NB)
                    if first and i == 0:
                        q_bias(1, 1, b_y)
                        q_low(0)
                    if i == 0 and not last:
                        x_statistics(b + 1)
                        dve.wait_ge(x_stats, b + 2)
                    if not (first and i == 0):
                        q_low(t)
                    if i == 0 and not last:
                        x_moments(b + 1)
                    if i == 1 and not last:
                        x_norm(b + 1)
                    if not (first and i == 0) and not (last and i == NQUAD - 1):
                        q_bias(t + 1, (i + 1) % NQUAD)
                    s_mask(t)
                    s_sum(t)
                    s_max(t)
                    if not (first and i == 0):
                        p_low(t - 1)
                    if i == 2 and not last:
                        x_low(b + 1)
                    if i == 1 and not first:
                        add_residual(b - 1)
                    if i == 2 and not first:
                        norm_out(b - 1)
                    if i == NQUAD - 1 and not first:
                        rank(b - 1)
                    if i == 1 and not first:
                        dve.wait_ge(x1_stats, b)
                    p_invert(t)
                    if first and i == 0:
                        keys_over(dve)
                    if i == 1 and not first:
                        x1_moments(b - 1)
                    if not (first and i == 0):
                        o_low(t - 1)
                    if last and i == 1:
                        select_rows(0)
                    if last and i == 2:
                        number_rows(0)

            attend(0, True, False)
            dve.wait_ge(wr_loaded, 16)
            with dve.Fori(1, NB - 1) as b:
                attend(b, False, False)
            attend(NB - 1, False, True)

            def weigh(i, src, ln):
                dve.wait_ge(f_rooted, i + 1)
                dve.scalar_tensor_tensor(hn_row[i % NJ][:], src, f_rs[:, i:i + 1], ln,
                                         ALU.mult, ALU.mult).then_inc(hn_made, 1)

            dve.wait_ge(ln1_loaded, 16)
            weigh(0, h_sel[0][:], ln1_row[:])
            p_low(STEPS - 1)

            def split_low(n):
                dve.wait_ge(piece_hi, n + 1)
                low(wp_lo[n % NSLOT][:, 2:4, :], raw[RAW_OF[n]][:, 2:4, :],
                    wp_hi[n % NSLOT][:, 2:4, :]).then_inc(piece_lo_dve, 1)

            def h_low(i):
                dve.wait_ge(hT_hi_done, i + 1)
                low(hT_lo[:, i % NJ].rearrange("p c t -> p (c t)"), (f_T, f_T2)[i % NJ][:],
                    hT_hi[:, i % NJ].rearrange("p c t -> p (c t)")).then_inc(hT_lo_done, 1)

            split_low(0)
            o_low(STEPS - 1)
            split_low(1)
            add_residual(NB - 1)
            dve.wait_ge(x1_stats, NB)
            x1_moments(NB - 1)
            dve.wait_ge(y_added, STEPS)
            h_low(0)
            norm_out(NB - 1)
            split_low(2)
            rank(NB - 1)

            def bias(r, u):
                dve.wait_ge(f_projected, r + 1)
                dve.wait_ge(bias_loaded[u % 2], 16 * (u // 2 + 1))
                dve.tensor_tensor(proj[r % 2][:], f_proj[r % 2][:], bias_row[u % 2][:],
                                  ALU.add).then_inc(f_biased, 1)

            def rotate(r, k, j):
                q = proj[r % 2][:].rearrange("p (h a d) -> p h a d", h=QUAD, a=2)
                s = by_sin[:].rearrange("p (h a d) -> p h a d", h=QUAD, a=2)
                dve.wait_ge(gathered_rope[j], 16)
                dve.wait_ge(f_biased, r + 1)
                wait(dve, f_roped, k)
                for a in range(2):
                    sin = rope[j][:, HD + a * (HD // 2):HD + (a + 1) * (HD // 2)]
                    last = dve.tensor_tensor(s[:, :, a, :], q[:, :, 1 - a, :],
                                             sin.unsqueeze(1).to_broadcast([P, QUAD, HD // 2]), ALU.mult)
                last.then_inc(sin_done, 1)

            def add_rotated(k, j):
                dve.wait_ge(sin_done, k + 1)
                dve.wait_ge(cos_done, k + 1)
                before = [o for o, block_ in ROPED[:k] if block_ == j]
                if before:
                    kind, n = PROJECTIONS[before[-1]]
                    if kind == "k":
                        dve.wait_ge(fk_turned, KEYS.index((n, j)) + 1)
                    else:
                        dve.wait_ge(fq_turned, NJ * n + j + 1)
                dve.tensor_tensor(turned[j][:], by_cos[:], by_sin[:], ALU.add).then_inc(f_roped, 1)

            def fk_low(n, j):
                dve.wait_ge(fk_hi_done, KEYS.index((n, j)) + 1)
                low(fkT_lo[:, n * QUAD:(n + 1) * QUAD, j * P:(j + 1) * P],
                    (f_T, f_T2)[j][:].rearrange("p (h t) -> p h t", h=QUAD),
                    fkT_hi[:, n * QUAD:(n + 1) * QUAD, j * P:(j + 1) * P]).then_inc(fk_lo_done, 1)

            def take_rows(o, j):
                r = TILES.index((o, j))
                if r >= 2 and PROJECTIONS[TILES[r - 2][0]][0] == "v":
                    before, block_ = TILES[r - 2]
                    dve.wait_ge(fv_hi_done, NJ * PROJECTIONS[before][1] + block_ + 1)
                    dve.wait_ge(fv_lo_done, NJ * PROJECTIONS[before][1] + block_ + 1)
                bias(r, bias_use(o, j))
                if PROJECTIONS[o][0] != "v":
                    rotate(r, ROPED.index((o, j)), j)

            def finish_rows(o, j):
                if PROJECTIONS[o][0] != "v":
                    add_rotated(ROPED.index((o, j)), j)

            take_rows(0, 0)
            select_rows(1)
            number_rows(1)
            finish_rows(0, 0)
            take_rows(1, 0)
            split_low(3)
            take_rows(2, 0)
            fk_low(0, 0)
            finish_rows(2, 0)
            layer1_over(dve)
            weigh(1, h_sel[1][:], ln1_row[:])
            take_rows(3, 0)
            h_low(1)
            fk_low(1, 0)
            finish_rows(3, 0)
            for o in range(AHEAD):
                take_rows(o, 1)
                if o > 0 and PROJECTIONS[o - 1][0] == "k":
                    fk_low(PROJECTIONS[o - 1][1], 1)
                finish_rows(o, 1)
                if o > 0:
                    split_low(NSLOT + o - 1)
            def probs_low(n):
                for i, (hi, lo, bank) in enumerate((
                        (fp0_hi[:, 0:2, :], fp0_lo[:, 0:2, :], f_T),
                        (fp0_hi[:, 2:4, :], fp0_lo[:, 2:4, :], f_T2),
                        (fp1_hi[:], fp1_lo[:], f_S))):
                    dve.wait_ge(fp_hi_done, 3 * n + i + 1)
                    low(lo.rearrange("p h t -> p (h t)"), bank[:],
                        hi.rearrange("p h t -> p (h t)")).then_inc(fp_lo_done, 1)

            def mixed_low(n):
                for g in range(2):
                    dve.wait_ge(fo_hi_done, 2 * n + g + 1)
                    low(foT_lo[:, 2 * g:2 * g + 2, :].rearrange("p h t -> p (h t)"), (f_O, f_T)[g][:],
                        foT_hi[:, 2 * g:2 * g + 2, :].rearrange("p h t -> p (h t)")
                        ).then_inc(fo_lo_done, 1)

            for n in range(FQ):
                if n < FQ - 1:
                    o = PROJECTIONS.index(("q", n + 1))
                if n == 0:
                    take_rows(o, 0)
                for j in range(NJ):
                    dve.wait_ge(fq_hi_done, NJ * n + j + 1)
                    low(fqT_lo[:, j].rearrange("p h t -> p (h t)"), (f_T, f_T2)[j][:],
                        fqT_hi[:, j].rearrange("p h t -> p (h t)")).then_inc(fq_lo_done, 1)
                if 0 < n < FQ - 1:
                    take_rows(o, 0)
                if n > 0:
                    probs_low(n - 1)
                if n < FQ - 1:
                    finish_rows(o, 0)
                    take_rows(o, 1)
                    finish_rows(o, 1)
                if n > 0:
                    mixed_low(n - 1)
                if 0 < n < FQ - 1:
                    split_low(split_early(n))
                for i, (heads, col) in enumerate(SCORE_TILES):
                    width = W // heads
                    bank = (f_S, f_T2, f_T)[i]
                    dve.wait_ge(f_scored, 3 * n + i + 1)
                    wait(dve, fp_turned, 3 * n)
                    dve.scalar_tensor_tensor(
                        fs[i][:].rearrange("p (h t) -> p h t", h=heads),
                        bank[:].rearrange("p (h t) -> p h t", h=heads), SCALE,
                        causal[:, 2 * P - width:2 * P].unsqueeze(1).to_broadcast([P, heads, width]),
                        ALU.mult, ALU.add).then_inc(f_masked, 1)
                    dve.wait_ge(f_masked, 3 * n + i + 1)
                    dve.tensor_reduce(f_max[:, col:col + heads],
                                      fs[i][:].rearrange("p (h t) -> p h t", h=heads),
                                      AX.X, ALU.max, negate=True).then_inc(f_maxed, 1)
                if n == 0:
                    take_rows(PROJECTIONS.index(("v", 1)), 0)
                    split_low(split_early(n))
                    take_rows(PROJECTIONS.index(("v", 1)), 1)
                for i, (heads, col) in enumerate(SCORE_TILES):
                    dve.wait_ge(f_exped, 3 * n + i + 1)
                    dve.reciprocal(f_inv[:, col:col + heads],
                                   f_sum[:, col:col + heads]).then_inc(f_inverted, 1)
                for piece in split_late(n):
                    split_low(piece)
            dve.wait_ge(f_rows_loaded, 32)
            for j in range(NJ):
                dve.tensor_tensor_reduce(x2_row[j][:], h_sel[j][:], wr2_row[:], 1.0, 0.0, ALU.mult,
                                         ALU.add, accum_out=g_dot[:, j:j + 1]).then_inc(g_dotted, 1)
            split_low(split_early(FQ - 1))
            probs_low(FQ - 1)
            mixed_low(FQ - 1)
            split_low(P_MLP + 2)

            def add_attention(j):
                dve.wait_ge(attn_done, NJ * (FQ - 1) + j + 1)
                dve.tensor_tensor(x2_row[j][:], f_W[j][:], h_sel[j][:], ALU.add).then_inc(x2_made, 1)

            add_attention(0)
            weigh(NJ, x2_row[0][:], ln2_row[:])
            add_attention(1)
            h_low(NJ)
            weigh(NJ + 1, x2_row[1][:], ln2_row[:])
            h_low(NJ + 1)
            split_low(P_MLP + 3)
            dve.wait_ge(g_exped, 1)
            dve.tensor_scalar(g_one[:], g_exp[:], 1.0, None, ALU.add).then_inc(g_made, 1)
            dve.wait_ge(g_made, 1)
            dve.reciprocal(gate[:], g_one[:]).then_inc(g_made, 1)
            for m in range(FI):
                for j in range(NJ):
                    dve.wait_ge(tanh_done, NJ * m + j + 1)
                    wait(dve, act_turned, NJ * (m - 1) + j + 1)
                    dve.scalar_tensor_tensor(act_row[j][:], tanh_row[j][:], 1.0, f_proj[j][:],
                                             ALU.add, ALU.mult).then_inc(silu_done, 1)
                    dve.wait_ge(silu_done, NJ * m + j + 1)
                    dve.wait_ge(upped, NJ * m + j + 1)
                    dve.scalar_tensor_tensor(act_row[j][:], act_row[j][:], 0.5, (f_S, f_O)[j][:],
                                             ALU.mult, ALU.mult).then_inc(act_done, 1)
                for piece in split_mlp(m):
                    split_low(piece)
                for j in range(NJ):
                    dve.wait_ge(aT_hi_done, NJ * m + j + 1)
                    low(fqT_lo[:, j].rearrange("p h t -> p (h t)"), (f_T, f_T2)[j][:],
                        fqT_hi[:, j].rearrange("p h t -> p (h t)")).then_inc(aT_lo_done, 1)
                if m == 0:
                    dve.wait_ge(attn_copied, NJ)
                    dve.wait_ge(g_made, 2)
                    dve.wait_ge(gathered_base, 16 * NJ)
                    for j in range(NJ):
                        dve.scalar_tensor_tensor(attn_row[j][:], attn_row[j][:], gate[:, j:j + 1], base[j][:],
                                                 ALU.mult, ALU.add).then_inc(attn_gated, 1)
            for j in range(NJ):
                dve.wait_ge(attn_gated, j + 1)
                dve.wait_ge(mlp_done, NJ * (FI - 1) + j + 1)
                dve.scalar_tensor_tensor(final[j][:], f_W[j][:], gate[:, j:j + 1], attn_row[j][:],
                                         ALU.mult, ALU.add).then_inc(final_made, 1)

        @block.tensor
        def _(pe):
            def product(dst, left, right, start, stop):
                pe.matmul(dst, left[0], right[0], start=start, stop=False)
                pe.matmul(dst, left[0], right[1], start=False, stop=False)
                return pe.matmul(dst, left[1], right[0], start=False, stop=stop)

            def turn(dst, src, n=4):
                for i in range(n):
                    last = pe.transpose(dst[:, i * P:(i + 1) * P], src[:, i * P:(i + 1) * P], ident[:])
                return last

            pe.wait_ge(const_made, 13)

            def turn_c(b, par, nth):
                pe.wait_ge(cx_loaded[par], 16 * nth)
                wait(pe, c_lo, b)
                turn(b_c, cx[par]).then_inc(c_turned, 1)

            def turn_k(b):
                pe.wait_ge(k_normed, b + 1)
                wait(pe, k_weighted, b)
                turn(b_kT, k_row[:].rearrange("p h d -> p (h d)")).then_inc(k_turned, 1)

            def turn_x(b):
                pe.wait_ge(x_normed, b + 1)
                wait(pe, xT_lo_done, b)
                turn(b_xT, xn).then_inc(x_turned, 1)

            def kv_project(bank, par, w_hi_, w_lo_, split_at=None):
                for c in range(DC):
                    if split_at is not None:
                        pe.wait_ge(kv_w_lo, split_at + c + 1)
                    last = product(bank[:], (cT_hi[par][:, c, :], cT_lo[par][:, c, :]),
                                   (w_hi_[:, c, :], w_lo_[:, c, :]), c == 0, c == DC - 1)
                return last

            def kv_batch(b, par, next_nth, first=False, last=False):
                if not last:
                    turn_c(b + 1, 1 - par, next_nth)
                pe.wait_ge(c_lo, b + 1)
                wait(pe, k_biased, b)
                kv_project(b_k, par, wk_hi, wk_lo, 0 if first else None).then_inc(k_projected, 1)
                if not first:
                    turn_k(b - 1)
                wait(pe, v_biased, b)
                kv_project(b_v, par, wv_hi, wv_lo, DC if first else None).then_inc(v_projected, 1)
                if last:
                    turn_x(0)

            turn_c(0, 0, 1)
            kv_batch(0, 0, 1, first=True)
            with pe.Fori(0, NB // 2 - 1) as g:
                kv_batch(2 * g + 1, 1, g + 2)
                kv_batch(2 * g + 2, 0, g + 2)
            kv_batch(NB - 1, 1, None, last=True)


            def project_q(t, b, quad, bank=b_q):
                pe.wait_ge(xT_lo_done, b + 1)
                if bank is b_q:
                    wait(pe, q_biased, t)
                for c in range(DC):
                    last = product(bank[:], (xT_hi[:, c, :], xT_lo[:, c, :]),
                                   (wq_hi[:, c, quad * W:(quad + 1) * W], wq_lo[:, c, quad * W:(quad + 1) * W]),
                                   c == 0, c == DC - 1)
                last.then_inc(q_projected, 1)

            def turn_q(t):
                pe.wait_ge(q_normed, t + 1)
                wait(pe, qT_lo_done, t)
                turn(b_qT, q_nrm[:].rearrange("p h d -> p (h d)")).then_inc(q_turned, 1)

            def score_quad(t, b, quad):
                pe.wait_ge(qT_lo_done, t + 1)
                if quad == 0:
                    pe.wait_ge(kT_lo_done, b + 1)
                wait(pe, s_summed, t)
                keys = kT[:, quad, :, :].rearrange("p a s -> p (a s)")
                for h in range(QUAD):
                    hs = slice(h * P, (h + 1) * P)
                    pe.matmul(b_scores[:, h, :], qT_hi[:, hs], keys, start=True, stop=False)
                    last = pe.matmul(b_scores[:, h, :], qT_lo[:, hs], keys, start=False, stop=True)
                last.then_inc(scored, 1)

            def turn_p(t):
                pe.wait_ge(p_normed, t + 1)
                wait(pe, pT_lo_done, t)
                turn(b_pT, p_row[:].rearrange("p h t -> p (h t)")).then_inc(p_turned, 1)

            def mix(t, b, quad):
                pe.wait_ge(pT_lo_done, t + 1)
                if quad == 0:
                    pe.wait_ge(v_lo_done, b + 1)
                wait(pe, oT_lo_done, t)
                vs = slice(quad * HD, (quad + 1) * HD)
                product(b_o[:], (v_hi[:, vs], v_lo[:, vs]), (pT_hi[:], pT_lo[:]), True, True
                        ).then_inc(mixed, 1)

            def add_y(t, b, quad):
                pe.wait_ge(oT_lo_done, t + 1)
                if quad == 0:
                    wait(pe, x1_made, b)
                for h in range(QUAD):
                    hs = slice(h * P, (h + 1) * P)
                    head = quad * QUAD + h
                    last = product(b_y[:], (oT_hi[:, hs], oT_lo[:, hs]),
                                   (wo_hi[:, head, :], wo_lo[:, head, :]),
                                   quad == 0 and h == 0, quad == NQUAD - 1 and h == QUAD - 1)
                last.then_inc(y_added, 1)

            def find_places(j):
                pe.matmul(b_xT[:, 0:BPJ], later[:], picked[:, j * BPJ:(j + 1) * BPJ],
                          start=True, stop=True).then_inc(place_found, 1)

            def find_rows(j):
                pe.wait_ge(onehot_made, 2 * (j + 1))
                pe.matmul(b_xT[:, BPJ:BPJ + 1],
                          onehot[:, j * BPJ:(j + 1) * BPJ, :].rearrange("p b s -> p (b s)"),
                          token[:], start=True, stop=True).then_inc(rows_found, 1)

            def spread_scores(b, rows_turned):
                pe.wait_ge(score_spread, b + 1)
                pe.wait_ge(xT_lo_done, rows_turned)
                pe.transpose(b_rank[:, 0:S], score_wide[:], ident[:]).then_inc(score_turned, 1)

            pe.wait_ge(w_lo, 2 * QUAD)
            pe.wait_ge(k_biased, NB)
            project_q(0, 0, 0)
            turn_k(NB - 1)
            pe.wait_ge(w_hi, 2 * NB)
            pe.wait_ge(w_lo, 2 * NB)
            project_q(1, 0, 1, b_y)
            pe.wait_ge(k_weighted, NB)
            pe.wait_ge(v_biased, NB)

            def attend(b, first, last):
                for i in range(NQUAD):
                    t = NQUAD * b + i
                    if last and i == 1:
                        pe.wait_ge(picks_made, NB - 2)
                        pe.wait_ge(xT_lo_done, NB)
                        find_places(0)
                    turn_q(t)
                    if not (first and i == 0) and not (last and i == NQUAD - 1):
                        project_q(t + 1, b if i < NQUAD - 1 else b + 1, (i + 1) % NQUAD)
                    score_quad(t, b, i)
                    if not (first and i == 0):
                        turn_p(t - 1)
                    if last and i == 2:
                        find_rows(0)
                    if i == 2 and not last:
                        turn_x(b + 1)
                    if i == NQUAD - 1 and not first:
                        if last:
                            pe.wait_ge(idx_made, 2)
                        spread_scores(b - 1, NB if last else b + 2)
                    if not (first and i < 2):
                        add_y(t - 2, b if i >= 2 else b - 1, (i - 2) % NQUAD)
                    if not (first and i == 0):
                        mix(t - 1, b if i >= 1 else b - 1, (i - 1) % NQUAD)

            attend(0, True, False)
            with pe.Fori(1, NB - 1) as b:
                attend(b, False, False)
            attend(NB - 1, False, True)

            def turn_h(i):
                pe.wait_ge(hn_made, i + 1)
                turn((f_T, f_T2)[i % NJ], hn_row[i % NJ]).then_inc(h_turned, 1)

            turn_p(STEPS - 1)
            add_y(STEPS - 2, NB - 1, NQUAD - 2)
            mix(STEPS - 1, NB - 1, NQUAD - 1)
            turn_h(0)
            add_y(STEPS - 1, NB - 1, NQUAD - 1)

            def piece_ready(n):
                pe.wait_ge(piece_lo_dve, n + 1)
                pe.wait_ge(piece_lo_pool, n + 1)

            def piece_rows(n, c):
                return wp_hi[n % NSLOT][:, c, :], wp_lo[n % NSLOT][:, c, :]

            def project(bank, j, n):
                for c in range(DC):
                    last = product(bank[:], (hT_hi[:, j, c, :], hT_lo[:, j, c, :]), piece_rows(n, c),
                                   c == 0, c == DC - 1)
                return last

            def project_tile(o, j):
                r = TILES.index((o, j))
                if j == 0:
                    piece_ready(ATTENTION.index(PROJECTIONS[o]))
                if o == 0:
                    pe.wait_ge(hT_lo_done, j + 1)
                if r == 1:
                    pe.wait_ge(x1_made, NB)
                wait(pe, f_biased, r - 1)
                project(f_proj[r % 2], j, ATTENTION.index(PROJECTIONS[o])).then_inc(f_projected, 1)

            def turn_fk(n, j):
                pe.wait_ge(f_roped, ROPED.index((PROJECTIONS.index(("k", n)), j)) + 1)
                if n == 0:
                    pe.wait_ge(hT_lo_done, j + 1)
                else:
                    pe.wait_ge(fk_lo_done, KEYS.index((n - 1, j)) + 1)
                turn((f_T, f_T2)[j], turned[j]).then_inc(fk_turned, 1)

            project_tile(0, 0)
            spread_scores(NB - 1, NB)
            project_tile(1, 0)
            pe.wait_ge(picks_made, NB)
            find_places(1)
            find_rows(1)
            project_tile(2, 0)
            turn_fk(0, 0)
            project_tile(3, 0)
            turn_fk(1, 0)
            turn_h(1)
            for o in range(AHEAD):
                project_tile(o, 1)
                if o > 0 and PROJECTIONS[o - 1][0] == "k":
                    turn_fk(PROJECTIONS[o - 1][1], 1)

            def next_query_rows(n, j):
                project_tile(PROJECTIONS.index(("q", n + 1)), j)

            def turn_queries(n):
                for j in range(NJ):
                    pe.wait_ge(f_roped, ROPED.index((PROJECTIONS.index(("q", n)), j)) + 1)
                    if n == 0:
                        pe.wait_ge(fk_lo_done, NJ * FK)
                    else:
                        pe.wait_ge(f_masked, 3 * n)
                    turn((f_T, f_T2)[j], turned[j]).then_inc(fq_turned, 1)

            def score_quad(n):
                pe.wait_ge(fq_lo_done, NJ * n + NJ)
                if n == 0:
                    pe.wait_ge(fk_lo_done, NJ * FK)
                wait(pe, fp_lo_done, 3 * n)
                for h in range(QUAD):
                    g = 2 * n + h // 2
                    last = product(f_S[:, h * P:(h + 1) * P], (fqT_hi[:, 0, h, :], fqT_lo[:, 0, h, :]),
                                   (fkT_hi[:, g, 0:P], fkT_lo[:, g, 0:P]), True, True)
                last.then_inc(f_scored, 1)
                for half_quad in range(2):
                    if half_quad == 1:
                        wait(pe, fo_lo_done, 2 * n)
                    for a in range(2):
                        h, g = 2 * half_quad + a, 2 * n + half_quad
                        last = product((f_T2, f_T)[half_quad][:, a * NSEL:(a + 1) * NSEL],
                                       (fqT_hi[:, 1, h, :], fqT_lo[:, 1, h, :]),
                                       (fkT_hi[:, g, :], fkT_lo[:, g, :]), True, True)
                    last.then_inc(f_scored, 1)

            def turn_probs(n):
                pe.wait_ge(f_normed, 3 * n + 3)
                if n < FQ - 1:
                    pe.wait_ge(fq_lo_done, NJ * (n + 2))
                for half_quad in range(2):
                    bank = (f_T, f_T2)[half_quad]
                    for a in range(2):
                        h = 2 * half_quad + a
                        pe.transpose(bank[:, a * NSEL:a * NSEL + P], fs[0][:, h * P:(h + 1) * P], ident[:])
                        last = pe.transpose(bank[:, a * NSEL + P:(a + 1) * NSEL],
                                            fs[1 + half_quad][:, a * NSEL:a * NSEL + P], ident[:])
                    last.then_inc(fp_turned, 1)
                for h in range(QUAD):
                    last = pe.transpose(f_S[:, h * P:(h + 1) * P],
                                        fs[1 + h // 2][:, (h % 2) * NSEL + P:(h % 2 + 1) * NSEL], ident[:])
                last.then_inc(fp_turned, 1)

            def mix_quad(n):
                pe.wait_ge(fp_lo_done, 3 * n + 3)
                if n == 0:
                    pe.wait_ge(fv_lo_done, NJ * FK)
                wait(pe, fo_lo_done, 2 * n)
                for g in range(2):
                    bank = (f_O, f_T)[g]
                    vs = slice((2 * n + g) * HD, (2 * n + g + 1) * HD)
                    product(bank[:], (fv_hi[:, 0, vs], fv_lo[:, 0, vs]),
                            (fp0_hi[:, 2 * g:2 * g + 2, :].rearrange("p h t -> p (h t)"),
                             fp0_lo[:, 2 * g:2 * g + 2, :].rearrange("p h t -> p (h t)")), True, False)
                    product(bank[:].rearrange("p (h t) -> p h t", h=2)[:, :, P:NSEL],
                            (fv_hi[:, 1, vs], fv_lo[:, 1, vs]),
                            (fp1_hi[:, 2 * g:2 * g + 2, :], fp1_lo[:, 2 * g:2 * g + 2, :]), False, True
                            ).then_inc(f_mixed, 1)

            def attend_out(n):
                piece_ready(p_wo(n))
                pe.wait_ge(fo_lo_done, 2 * n + 2)
                for j in range(NJ):
                    for h in range(QUAD):
                        hs = slice(j * P, (j + 1) * P)
                        last = product(f_W[j][:], (foT_hi[:, h, hs], foT_lo[:, h, hs]),
                                       piece_rows(p_wo(n), h),
                                       n == 0 and h == 0, n == FQ - 1 and h == QUAD - 1)
                    last.then_inc(attn_done, 1)

            next_query_rows(0, 0)
            for n in range(FQ):
                turn_queries(n)
                if 0 < n < FQ - 1:
                    next_query_rows(n, 0)
                if n > 0:
                    turn_probs(n - 1)
                if n < FQ - 1:
                    next_query_rows(n, 1)
                if n > 0:
                    mix_quad(n - 1)
                score_quad(n)
                if n == 0:
                    for j in range(NJ):
                        project_tile(PROJECTIONS.index(("v", 1)), j)
                else:
                    attend_out(n - 1)
            turn_probs(FQ - 1)
            mix_quad(FQ - 1)
            attend_out(FQ - 1)

            def gate_rows(m, j):
                piece_ready(p_gate(m))
                if m == 0:
                    pe.wait_ge(hT_lo_done, NJ + j + 1)
                wait(pe, silu_done, NJ * (m - 1) + j + 1)
                project(f_proj[j], j, p_gate(m)).then_inc(gated, 1)

            def up_rows(m, j):
                piece_ready(p_up(m))
                wait(pe, act_done, NJ * (m - 1) + j + 1)
                project((f_S, f_O)[j], j, p_up(m)).then_inc(upped, 1)

            def turn_inner(m):
                for j in range(NJ):
                    pe.wait_ge(act_done, NJ * m + j + 1)
                    wait(pe, aT_lo_done, NJ * (m - 1) + j + 1)
                    turn((f_T, f_T2)[j], act_row[j]).then_inc(act_turned, 1)

            turn_h(NJ)
            gate_rows(0, 0)
            turn_h(NJ + 1)
            up_rows(0, 0)
            gate_rows(0, 1)
            up_rows(0, 1)
            for m in range(FI):
                if m < FI - 1:
                    for j in range(NJ):
                        gate_rows(m + 1, j)
                    turn_inner(m)
                    for j in range(NJ):
                        up_rows(m + 1, j)
                piece_ready(p_down(m))
                if m == 0:
                    pe.wait_ge(attn_copied, NJ)
                for j in range(NJ):
                    pe.wait_ge(aT_lo_done, NJ * m + j + 1)
                    for c in range(4):
                        last = product(f_W[j][:], (fqT_hi[:, j, c, :], fqT_lo[:, j, c, :]),
                                       piece_rows(p_down(m), c),
                                       m == 0 and c == 0, m == FI - 1 and c == 3)
                    last.then_inc(mlp_done, 1)
                    if m == FI - 2 and j == NJ - 2:
                        turn_inner(FI - 1)


_INS = ['x', 'ctx_2048', 'mask_1xSxS2_ff0', 'L0_xattn_Wq', 'L0_xattn_bq', 'L0_xattn_Wk', 'L0_xattn_bk',
        'L0_xattn_Wv', 'L0_xattn_bv', 'L0_xattn_Wo', 'L0_xattn_qn_w', 'L0_xattn_kn_w', 'L0_ffn_w_router',
        'L0_ffn_wq', 'L0_ffn_bq', 'L0_ffn_wk', 'L0_ffn_bk', 'L0_ffn_wv', 'L0_ffn_bv', 'L0_ffn_wo',
        'L0_ffn_w_gate', 'L0_ffn_w_up', 'L0_ffn_w_down', 'L0_ffn_ln1_w', 'L0_ffn_ln2_w']


def _rope_table(positions, head_dim, theta=10000.0):
    import numpy as np
    inv = (1.0 / np.float32(theta) ** (np.arange(0, head_dim, 2, dtype=np.float32) / np.float32(head_dim)))
    ang = np.arange(positions, dtype=np.float32)[:, None] * inv.astype(np.float32)
    c, s = np.cos(ang), np.sin(ang)
    return np.concatenate([c, c, -s, s], axis=1).astype(np.float32)


def kernel(**inputs):
    import numpy as _np
    import concourse.bacc as _bacc
    from concourse import mybir as _mybir
    from concourse.bass_utils import run_bass_kernel_spmd as _run

    nc = _bacc.Bacc("TRN2", target_bir_lowering=False, num_devices=1)
    arrays, args = {}, []
    named = [(n, _np.ascontiguousarray(inputs[n])) for n in _INS]
    batches, seq, _ = named[0][1].shape
    pick = seq // 8
    blocks = batches * pick // 128
    slot = _np.arange(blocks)[None, :] * 128 + _np.arange(128)[:, None]
    named += [("rope_table", _rope_table(seq, 128)),
              ("slot_base", (slot // pick * seq).astype(_np.float32))]
    for name, a in named:
        arrays[f"in_{name}_dram"] = a
        args.append(nc.dram_tensor(f"in_{name}_dram", a.shape, _mybir.dt.from_np(a.dtype), kind="ExternalInput").ap())
    out = nc.dram_tensor("out_0_dram", (batches, seq, 512), _mybir.dt.float32, kind="ExternalOutput").ap()
    xattn_then_routed_ffn(nc, *args, out)
    r = _run(nc, [arrays], core_ids=[0])
    return r.results[0]["out_0_dram"]
```
